# Optimizing a Trainium2 kernel written in Bass

```python
import numpy as np
import jax
import jax.numpy as jnp

def _softmax(x, axis=-1):
    return jax.nn.softmax(x, axis=axis)

def _gelu(x):
    return jax.nn.gelu(x, approximate=True)

def _silu(x):
    return jax.nn.silu(x)

def _sigmoid(x):
    return jax.nn.sigmoid(x)

def _layernorm(x, axis=-1, eps=1e-05):
    m = jnp.mean(x, axis=axis, keepdims=True)
    v = jnp.var(x, axis=axis, keepdims=True)
    return (x - m) / jnp.sqrt(v + eps)

def _scatter_add(tgt, idx, src, axis=0):
    return tgt.at[idx].add(src)

def _segment_sum(src, seg, n):
    return jax.ops.segment_sum(src, seg, n)
kernel_name = 'mk_flamingo_gated_d4_seqx_r8_30cc56'

def setup_inputs(seed: int=0):
    np.random.seed(seed)
    _w = jnp.asarray

    def _rec_inputs():
        import jax
        import jax.numpy as jnp
        _rk = jax.random.key(seed)
        x = -0.0002928 + 1 * jax.random.normal(jax.random.fold_in(_rk, 1), (16, 64, 128), jnp.float32)
        _lenS = 64 - jax.random.randint(jax.random.fold_in(_rk, 7), (16,), 0, max(1, 64 // 4) + 1, jnp.int32)
        _lenS2 = 64 - jax.random.randint(jax.random.fold_in(_rk, 8), (16,), 0, max(1, 64 // 4) + 1, jnp.int32)
        _ctx_1024P = jax.random.normal(jax.random.fold_in(_rk, 11), (16, 16, 128), jnp.float32)
        _ctx_1024c = jax.random.dirichlet(jax.random.fold_in(_rk, 511), 0.3 * jnp.ones((16,), jnp.float32), (16, 64))
        _ctx_1024t = jnp.einsum('bsk,bkd->bsd', _ctx_1024c, _ctx_1024P)
        _ctx_1024t = _ctx_1024t * jax.lax.rsqrt(jnp.mean(jnp.square(_ctx_1024t)) + 1e-12) * 0.953939
        ctx_1024 = -1.39393e-06 + 0.999914 * (_ctx_1024t + 0.3 * jax.random.normal(jax.random.fold_in(_rk, 611), (16, 64, 128), jnp.float32))
        fside_Bx16xSxS2_0 = 9.80324e-06 + 0.100009 * jax.random.normal(jax.random.fold_in(_rk, 12), (16, 16, 64, 64), jnp.float32)
        fside_SxS2_0 = -2.64403e-05 + 0.100002 * jax.random.normal(jax.random.fold_in(_rk, 14), (64, 64), jnp.float32)
        _validS = jnp.arange(64)[None, :] < _lenS[:, None]
        _validS2 = jnp.arange(64)[None, :] < _lenS2[:, None]
        _causal = jnp.tril(jnp.ones((64, 64), dtype=bool))
        mask_BxS2_bf0 = jnp.logical_not(jnp.ones((16, 64), dtype=bool))
        mask_BxS_bf1 = jnp.ones((16, 64), dtype=bool)
        _g = jax.random.normal(jax.random.fold_in(_rk, 9001), (2, 4), jnp.float32)
        _g = jnp.sign(_g) * jnp.maximum(jnp.abs(_g), 1.0) + (_g == 0) * 1.0
        g_xattn = _g[0]
        g_ffn = _g[1]
        return (x, ctx_1024, fside_Bx16xSxS2_0, fside_SxS2_0, mask_BxS2_bf0, mask_BxS_bf1, g_xattn, g_ffn)
    x, ctx_1024, fside_Bx16xSxS2_0, fside_SxS2_0, mask_BxS2_bf0, mask_BxS_bf1, g_xattn, g_ffn = _rec_inputs()

    def _L0_xattn_setup():
        import jax, jax.numpy as jnp
        import numpy as np
        import math
        EMBED_DIM = 128
        NUM_HEADS = 16
        HEAD_DIM = EMBED_DIM // NUM_HEADS
        ROPE_BASE = 10000.0

        def _rope_cache(S, D, dtype):
            inv_freq = 1.0 / ROPE_BASE ** (jnp.arange(0, D, 2, dtype=jnp.float32) / D)
            t = jnp.arange(S, dtype=jnp.float32)
            freqs = t[:, None] * inv_freq[None, :]
            return (jnp.cos(freqs).astype(dtype), jnp.sin(freqs).astype(dtype))

        def _apply_rope(x, cos, sin):
            x_even = x[..., 0::2]
            x_odd = x[..., 1::2]
            rot_even = x_even * cos - x_odd * sin
            rot_odd = x_odd * cos + x_even * sin
            return jnp.stack([rot_even, rot_odd], axis=-1).reshape(x.shape)
        key = jax.random.key(seed)
        ks = jax.random.split(key, 11)
        B, S, E = (2, 256, EMBED_DIM)
        s = 1.0 / math.sqrt(E)
        return {'query': jax.random.normal(ks[0], (B, S, E), jnp.float32), 'key': jax.random.normal(ks[1], (B, S, E), jnp.float32), 'value': jax.random.normal(ks[2], (B, S, E), jnp.float32), 'Wq': jax.random.normal(ks[3], (E, E), jnp.float32) * s, 'bq': jnp.zeros((E,), jnp.float32), 'Wk': jax.random.normal(ks[4], (E, E), jnp.float32) * s, 'bk': jnp.zeros((E,), jnp.float32), 'Wv': jax.random.normal(ks[5], (E, E), jnp.float32) * s, 'bv': jnp.zeros((E,), jnp.float32), 'Wo': jax.random.normal(ks[6], (E, E), jnp.float32) * s, 'bo': jnp.zeros((E,), jnp.float32)}
    _L0_xattn_all = _L0_xattn_setup()
    _L0_xattn_in = {k: v for k, v in _L0_xattn_all.items() if k in ('Wq', 'bq', 'Wk', 'bk', 'Wv', 'bv', 'Wo', 'bo')}
    del _L0_xattn_all

    def _L0_ffn_setup():
        import jax, jax.numpy as jnp
        import numpy as np
        H = 128
        DFF = 512
        E_ROUTED = 7
        TOP_K = 2

        def _swiglu(flat, gate_w, up_w, down_w):
            g = flat @ gate_w.T
            up = flat @ up_w.T
            return jax.nn.silu(g) * up @ down_w.T
        key = jax.random.key(seed)
        ks = jax.random.split(key, 8)
        s = 0.02
        return {'x': jax.random.normal(ks[0], (4, 256, H), jnp.float32), 'shared_up': jax.random.normal(ks[1], (DFF, H), jnp.float32) * s, 'shared_gate': jax.random.normal(ks[2], (DFF, H), jnp.float32) * s, 'shared_down': jax.random.normal(ks[3], (H, DFF), jnp.float32) * s, 'routed_up': jax.random.normal(ks[4], (E_ROUTED, DFF, H), jnp.float32) * s, 'routed_gate': jax.random.normal(ks[5], (E_ROUTED, DFF, H), jnp.float32) * s, 'routed_down': jax.random.normal(ks[6], (E_ROUTED, H, DFF), jnp.float32) * s, 'router_w': jax.random.normal(ks[7], (E_ROUTED, H), jnp.float32) * 0.02}
    _L0_ffn_all = _L0_ffn_setup()
    _L0_ffn_in = {k: v for k, v in _L0_ffn_all.items() if k in ('shared_up', 'shared_gate', 'shared_down', 'routed_up', 'routed_gate', 'routed_down', 'router_w')}
    del _L0_ffn_all

    def _L1_xattn_setup():
        import jax, jax.numpy as jnp
        import numpy as np
        E = 128
        H = 16
        D = E // H
        key = jax.random.key(seed)
        ks = jax.random.split(key, 12)
        B, T, S = (2, 256, 256)
        inp = {'query': jax.random.normal(ks[0], (B, T, E), jnp.float32), 'key': jax.random.normal(ks[1], (B, S, E), jnp.float32), 'value': jax.random.normal(ks[2], (B, S, E), jnp.float32), 'spatial_bias': jax.random.normal(ks[3], (B, H, T, S), jnp.float32) * 0.1, 'directional_bias': jax.random.normal(ks[4], (B, H, T, S), jnp.float32) * 0.1, 'key_padding_mask': jnp.zeros((B, S), dtype=bool), 'attn_mask': jax.random.normal(ks[5], (T, S), jnp.float32) * 0.1, 'Wq': jax.random.normal(ks[6], (E, E), jnp.float32) / np.sqrt(E), 'bq': jnp.zeros((E,), jnp.float32), 'Wk': jax.random.normal(ks[7], (E, E), jnp.float32) / np.sqrt(E), 'bk': jnp.zeros((E,), jnp.float32), 'Wv': jax.random.normal(ks[8], (E, E), jnp.float32) / np.sqrt(E), 'bv': jnp.zeros((E,), jnp.float32), 'Wo': jax.random.normal(ks[9], (E, E), jnp.float32) / np.sqrt(E), 'bo': jnp.zeros((E,), jnp.float32)}
        return inp
    _L1_xattn_all = _L1_xattn_setup()
    _L1_xattn_in = {k: v for k, v in _L1_xattn_all.items() if k in ('Wq', 'bq', 'Wk', 'bk', 'Wv', 'bv', 'Wo', 'bo')}
    del _L1_xattn_all

    def _L1_ffn_setup():
        import jax, jax.numpy as jnp
        import numpy as np
        B, S, D = (4, 256, 128)
        DFF = 64
        E = 16
        TOP_K = 2
        N_SHARED = 2
        FUSED_DFF = DFF * N_SHARED
        key = jax.random.key(seed)
        ks = jax.random.split(key, 16)
        sc_d = 1.0 / np.sqrt(D)
        sc_f = 1.0 / np.sqrt(DFF)
        sc_sf = 1.0 / np.sqrt(FUSED_DFF)
        inp = {'x': jax.random.normal(ks[0], (B, S, D), dtype=jnp.float32), 'gate_w': jax.random.uniform(ks[1], (E, D), dtype=jnp.float32, minval=-sc_d, maxval=sc_d), 'expert_bias': jnp.zeros((E,), dtype=jnp.float32), 'w1': jax.random.uniform(ks[2], (E, DFF, D), dtype=jnp.float32, minval=-sc_d, maxval=sc_d), 'b1': jax.random.uniform(ks[3], (E, DFF), dtype=jnp.float32, minval=-sc_d, maxval=sc_d), 'w3': jax.random.uniform(ks[4], (E, DFF, D), dtype=jnp.float32, minval=-sc_d, maxval=sc_d), 'b3': jax.random.uniform(ks[5], (E, DFF), dtype=jnp.float32, minval=-sc_d, maxval=sc_d), 'w2': jax.random.uniform(ks[6], (E, D, DFF), dtype=jnp.float32, minval=-sc_f, maxval=sc_f), 'b2': jax.random.uniform(ks[7], (E, D), dtype=jnp.float32, minval=-sc_f, maxval=sc_f), 'sw1': jax.random.uniform(ks[8], (FUSED_DFF, D), dtype=jnp.float32, minval=-sc_d, maxval=sc_d), 'sb1': jax.random.uniform(ks[9], (FUSED_DFF,), dtype=jnp.float32, minval=-sc_d, maxval=sc_d), 'sw3': jax.random.uniform(ks[10], (FUSED_DFF, D), dtype=jnp.float32, minval=-sc_d, maxval=sc_d), 'sb3': jax.random.uniform(ks[11], (FUSED_DFF,), dtype=jnp.float32, minval=-sc_d, maxval=sc_d), 'sw2': jax.random.uniform(ks[12], (D, FUSED_DFF), dtype=jnp.float32, minval=-sc_sf, maxval=sc_sf), 'sb2': jax.random.uniform(ks[13], (D,), dtype=jnp.float32, minval=-sc_sf, maxval=sc_sf)}
        return inp
    _L1_ffn_all = _L1_ffn_setup()
    _L1_ffn_in = {k: v for k, v in _L1_ffn_all.items() if k in ('gate_w', 'expert_bias', 'w1', 'b1', 'w2', 'b2', 'w3', 'b3', 'sw1', 'sb1', 'sw2', 'sb2', 'sw3', 'sb3')}
    del _L1_ffn_all

    def _L2_xattn_setup():
        import jax, jax.numpy as jnp
        import numpy as np
        D_MODEL = 128
        NUM_HEADS = 16
        D_K = D_MODEL // NUM_HEADS
        key = jax.random.key(seed)
        ks = jax.random.split(key, 11)
        B, S = (2, 256)
        scale = 1.0 / np.sqrt(D_MODEL)
        inp = {'Q': jax.random.normal(ks[0], (B, S, D_MODEL), jnp.float32), 'K': jax.random.normal(ks[1], (B, S, D_MODEL), jnp.float32), 'V': jax.random.normal(ks[2], (B, S, D_MODEL), jnp.float32), 'W_q': jax.random.normal(ks[3], (D_MODEL, D_MODEL), jnp.float32) * scale, 'b_q': jnp.zeros((D_MODEL,), jnp.float32), 'W_k': jax.random.normal(ks[4], (D_MODEL, D_MODEL), jnp.float32) * scale, 'b_k': jnp.zeros((D_MODEL,), jnp.float32), 'W_v': jax.random.normal(ks[5], (D_MODEL, D_MODEL), jnp.float32) * scale, 'b_v': jnp.zeros((D_MODEL,), jnp.float32), 'W_o': jax.random.normal(ks[6], (D_MODEL, D_MODEL), jnp.float32) * scale, 'b_o': jnp.zeros((D_MODEL,), jnp.float32)}
        return inp
    _L2_xattn_all = _L2_xattn_setup()
    _L2_xattn_in = {k: v for k, v in _L2_xattn_all.items() if k in ('W_q', 'b_q', 'W_k', 'b_k', 'W_v', 'b_v', 'W_o', 'b_o')}
    del _L2_xattn_all

    def _L2_ffn_setup():
        import jax, jax.numpy as jnp
        import numpy as np
        DIM = 128
        E = 16
        TOPK = 2
        G = 4
        TOPK_G = 2
        INTER = 64
        N_SHARED = 2
        ROUTE_SCALE = 1.0

        def _gate(xf, gate_w, gate_b):
            scores = xf @ gate_w.T
            scores = jax.nn.softmax(scores.astype(jnp.float32), axis=-1)
            orig = scores
            scores = scores + gate_b
            T = xf.shape[0]
            sg = scores.reshape(T, G, E // G)
            group_scores = jax.lax.top_k(sg, 2)[0].sum(-1)
            _, gidx = jax.lax.top_k(group_scores, TOPK_G)
            keep = jax.nn.one_hot(gidx, G).sum(axis=1) > 0
            sg = jnp.where(keep[:, :, None], sg, -jnp.inf)
            scores = sg.reshape(T, E)
            _, idx = jax.lax.top_k(scores, TOPK)
            weights = jnp.take_along_axis(orig, idx, axis=1)
            weights = (weights * ROUTE_SCALE).astype(xf.dtype)
            return (weights, idx)
        key = jax.random.key(seed)
        ks = jax.random.split(key, 16)
        s = lambda fan_in: 1.0 / np.sqrt(fan_in)
        inp = {'x': jax.random.normal(ks[0], (4, 128, DIM), dtype=jnp.float32), 'gate_w': jax.random.normal(ks[1], (E, DIM), dtype=jnp.float32) * s(DIM), 'gate_b': jnp.zeros((E,), dtype=jnp.float32), 'We1': jax.random.normal(ks[2], (E, DIM, INTER), dtype=jnp.float32) * s(DIM), 'be1': jnp.zeros((E, INTER), dtype=jnp.float32), 'We2': jax.random.normal(ks[3], (E, INTER, DIM), dtype=jnp.float32) * s(INTER), 'be2': jnp.zeros((E, DIM), dtype=jnp.float32), 'We3': jax.random.normal(ks[4], (E, DIM, INTER), dtype=jnp.float32) * s(DIM), 'be3': jnp.zeros((E, INTER), dtype=jnp.float32), 'ws1': jax.random.normal(ks[5], (DIM, N_SHARED * INTER), dtype=jnp.float32) * s(DIM), 'bs1': jnp.zeros((N_SHARED * INTER,), dtype=jnp.float32), 'ws2': jax.random.normal(ks[6], (N_SHARED * INTER, DIM), dtype=jnp.float32) * s(N_SHARED * INTER), 'bs2': jnp.zeros((DIM,), dtype=jnp.float32), 'ws3': jax.random.normal(ks[7], (DIM, N_SHARED * INTER), dtype=jnp.float32) * s(DIM), 'bs3': jnp.zeros((N_SHARED * INTER,), dtype=jnp.float32)}
        return inp
    _L2_ffn_all = _L2_ffn_setup()
    _L2_ffn_in = {k: v for k, v in _L2_ffn_all.items() if k in ('gate_w', 'gate_b', 'We1', 'be1', 'We2', 'be2', 'We3', 'be3', 'ws1', 'bs1', 'ws2', 'bs2', 'ws3', 'bs3')}
    del _L2_ffn_all

    def _L3_xattn_setup():
        import jax, jax.numpy as jnp
        import numpy as np
        NUM_HEADS = 16
        TOKEN_DIM = 128
        D_HEAD = TOKEN_DIM // NUM_HEADS

        def masked_softmax(scores, mask):
            scores = jnp.clip(scores, -50.0, 50.0)
            exp_scores = jnp.exp(scores)
            if mask is not None:
                exp_scores = jnp.where(mask, exp_scores, 0.0)
            denom = jnp.sum(exp_scores, axis=-1, keepdims=True)
            denom = jnp.where(denom <= 0.0, 1.0, denom)
            return exp_scores / denom
        key = jax.random.key(seed)
        ks = jax.random.split(key, 8)
        B, Sq, Sk = (2, 256, 256)
        scale = 1.0 / np.sqrt(TOKEN_DIM)
        return {'Q': jax.random.normal(ks[0], (B, Sq, TOKEN_DIM), dtype=jnp.float32), 'K': jax.random.normal(ks[1], (B, Sk, TOKEN_DIM), dtype=jnp.float32), 'V': jax.random.normal(ks[2], (B, Sk, TOKEN_DIM), dtype=jnp.float32), 'mask': jnp.ones((B, Sq), dtype=bool), 'W_q': jax.random.normal(ks[3], (TOKEN_DIM, TOKEN_DIM), dtype=jnp.float32) * scale, 'W_k': jax.random.normal(ks[4], (TOKEN_DIM, TOKEN_DIM), dtype=jnp.float32) * scale, 'W_v': jax.random.normal(ks[5], (TOKEN_DIM, TOKEN_DIM), dtype=jnp.float32) * scale, 'W_o': jax.random.normal(ks[6], (TOKEN_DIM, TOKEN_DIM), dtype=jnp.float32) * scale}
    _L3_xattn_all = _L3_xattn_setup()
    _L3_xattn_in = {k: v for k, v in _L3_xattn_all.items() if k in ('W_q', 'W_k', 'W_v', 'W_o')}
    del _L3_xattn_all

    def _L3_ffn_setup():
        import jax, jax.numpy as jnp
        import numpy as np
        import math
        B, S, H, I, E = (4, 256, 128, 512, 8)
        TOP_K = 2
        CAPACITY_FACTOR = 1.25
        key = jax.random.key(seed)
        k1, k2, k3, k4, k5 = jax.random.split(key, 5)
        x = jax.random.normal(k1, (B, S, H), dtype=jnp.float32)
        W_router = jax.random.normal(k2, (E, H), dtype=jnp.float32) * (1.0 / math.sqrt(H))
        b_router = jnp.zeros((E,), dtype=jnp.float32)
        experts_inter = jax.random.normal(k3, (E, H, I), dtype=jnp.float32) * 0.02
        experts_out = jax.random.normal(k4, (E, I, H), dtype=jnp.float32) * 0.02
        return {'x': x, 'W_router': W_router, 'b_router': b_router, 'experts_inter': experts_inter, 'experts_out': experts_out}
    _L3_ffn_all = _L3_ffn_setup()
    _L3_ffn_in = {k: v for k, v in _L3_ffn_all.items() if k in ('W_router', 'b_router', 'experts_inter', 'experts_out')}
    del _L3_ffn_all
    return {'x': x, 'ctx_1024': ctx_1024, 'fside_Bx16xSxS2_0': fside_Bx16xSxS2_0, 'fside_SxS2_0': fside_SxS2_0, 'mask_BxS2_bf0': mask_BxS2_bf0, 'mask_BxS_bf1': mask_BxS_bf1, 'g_xattn': g_xattn, 'g_ffn': g_ffn, 'L0_xattn_Wq': _L0_xattn_in['Wq'], 'L0_xattn_bq': _L0_xattn_in['bq'], 'L0_xattn_Wk': _L0_xattn_in['Wk'], 'L0_xattn_bk': _L0_xattn_in['bk'], 'L0_xattn_Wv': _L0_xattn_in['Wv'], 'L0_xattn_bv': _L0_xattn_in['bv'], 'L0_xattn_Wo': _L0_xattn_in['Wo'], 'L0_xattn_bo': _L0_xattn_in['bo'], 'L0_ffn_shared_up': _L0_ffn_in['shared_up'], 'L0_ffn_shared_gate': _L0_ffn_in['shared_gate'], 'L0_ffn_shared_down': _L0_ffn_in['shared_down'], 'L0_ffn_routed_up': _L0_ffn_in['routed_up'], 'L0_ffn_routed_gate': _L0_ffn_in['routed_gate'], 'L0_ffn_routed_down': _L0_ffn_in['routed_down'], 'L0_ffn_router_w': _L0_ffn_in['router_w'], 'L1_xattn_Wq': _L1_xattn_in['Wq'], 'L1_xattn_bq': _L1_xattn_in['bq'], 'L1_xattn_Wk': _L1_xattn_in['Wk'], 'L1_xattn_bk': _L1_xattn_in['bk'], 'L1_xattn_Wv': _L1_xattn_in['Wv'], 'L1_xattn_bv': _L1_xattn_in['bv'], 'L1_xattn_Wo': _L1_xattn_in['Wo'], 'L1_xattn_bo': _L1_xattn_in['bo'], 'L1_ffn_gate_w': _L1_ffn_in['gate_w'], 'L1_ffn_expert_bias': _L1_ffn_in['expert_bias'], 'L1_ffn_w1': _L1_ffn_in['w1'], 'L1_ffn_b1': _L1_ffn_in['b1'], 'L1_ffn_w2': _L1_ffn_in['w2'], 'L1_ffn_b2': _L1_ffn_in['b2'], 'L1_ffn_w3': _L1_ffn_in['w3'], 'L1_ffn_b3': _L1_ffn_in['b3'], 'L1_ffn_sw1': _L1_ffn_in['sw1'], 'L1_ffn_sb1': _L1_ffn_in['sb1'], 'L1_ffn_sw2': _L1_ffn_in['sw2'], 'L1_ffn_sb2': _L1_ffn_in['sb2'], 'L1_ffn_sw3': _L1_ffn_in['sw3'], 'L1_ffn_sb3': _L1_ffn_in['sb3'], 'L2_xattn_W_q': _L2_xattn_in['W_q'], 'L2_xattn_b_q': _L2_xattn_in['b_q'], 'L2_xattn_W_k': _L2_xattn_in['W_k'], 'L2_xattn_b_k': _L2_xattn_in['b_k'], 'L2_xattn_W_v': _L2_xattn_in['W_v'], 'L2_xattn_b_v': _L2_xattn_in['b_v'], 'L2_xattn_W_o': _L2_xattn_in['W_o'], 'L2_xattn_b_o': _L2_xattn_in['b_o'], 'L2_ffn_gate_w': _L2_ffn_in['gate_w'], 'L2_ffn_gate_b': _L2_ffn_in['gate_b'], 'L2_ffn_We1': _L2_ffn_in['We1'], 'L2_ffn_be1': _L2_ffn_in['be1'], 'L2_ffn_We2': _L2_ffn_in['We2'], 'L2_ffn_be2': _L2_ffn_in['be2'], 'L2_ffn_We3': _L2_ffn_in['We3'], 'L2_ffn_be3': _L2_ffn_in['be3'], 'L2_ffn_ws1': _L2_ffn_in['ws1'], 'L2_ffn_bs1': _L2_ffn_in['bs1'], 'L2_ffn_ws2': _L2_ffn_in['ws2'], 'L2_ffn_bs2': _L2_ffn_in['bs2'], 'L2_ffn_ws3': _L2_ffn_in['ws3'], 'L2_ffn_bs3': _L2_ffn_in['bs3'], 'L3_xattn_W_q': _L3_xattn_in['W_q'], 'L3_xattn_W_k': _L3_xattn_in['W_k'], 'L3_xattn_W_v': _L3_xattn_in['W_v'], 'L3_xattn_W_o': _L3_xattn_in['W_o'], 'L3_ffn_W_router': _L3_ffn_in['W_router'], 'L3_ffn_b_router': _L3_ffn_in['b_router'], 'L3_ffn_experts_inter': _L3_ffn_in['experts_inter'], 'L3_ffn_experts_out': _L3_ffn_in['experts_out']}

def reference(x, ctx_1024, fside_Bx16xSxS2_0, fside_SxS2_0, mask_BxS2_bf0, mask_BxS_bf1, g_xattn, g_ffn, L0_xattn_Wq, L0_xattn_bq, L0_xattn_Wk, L0_xattn_bk, L0_xattn_Wv, L0_xattn_bv, L0_xattn_Wo, L0_xattn_bo, L0_ffn_shared_up, L0_ffn_shared_gate, L0_ffn_shared_down, L0_ffn_routed_up, L0_ffn_routed_gate, L0_ffn_routed_down, L0_ffn_router_w, L1_xattn_Wq, L1_xattn_bq, L1_xattn_Wk, L1_xattn_bk, L1_xattn_Wv, L1_xattn_bv, L1_xattn_Wo, L1_xattn_bo, L1_ffn_gate_w, L1_ffn_expert_bias, L1_ffn_w1, L1_ffn_b1, L1_ffn_w2, L1_ffn_b2, L1_ffn_w3, L1_ffn_b3, L1_ffn_sw1, L1_ffn_sb1, L1_ffn_sw2, L1_ffn_sb2, L1_ffn_sw3, L1_ffn_sb3, L2_xattn_W_q, L2_xattn_b_q, L2_xattn_W_k, L2_xattn_b_k, L2_xattn_W_v, L2_xattn_b_v, L2_xattn_W_o, L2_xattn_b_o, L2_ffn_gate_w, L2_ffn_gate_b, L2_ffn_We1, L2_ffn_be1, L2_ffn_We2, L2_ffn_be2, L2_ffn_We3, L2_ffn_be3, L2_ffn_ws1, L2_ffn_bs1, L2_ffn_ws2, L2_ffn_bs2, L2_ffn_ws3, L2_ffn_bs3, L3_xattn_W_q, L3_xattn_W_k, L3_xattn_W_v, L3_xattn_W_o, L3_ffn_W_router, L3_ffn_b_router, L3_ffn_experts_inter, L3_ffn_experts_out):
    import jax
    import jax.numpy as jnp

    def _L0_xattn_ref(query, key, value, Wq, bq, Wk, bk, Wv, bv, Wo, bo):
        import jax, jax.numpy as jnp
        import numpy as np
        import math
        EMBED_DIM = 128
        NUM_HEADS = 16
        HEAD_DIM = EMBED_DIM // NUM_HEADS
        ROPE_BASE = 10000.0

        def _rope_cache(S, D, dtype):
            inv_freq = 1.0 / ROPE_BASE ** (jnp.arange(0, D, 2, dtype=jnp.float32) / D)
            t = jnp.arange(S, dtype=jnp.float32)
            freqs = t[:, None] * inv_freq[None, :]
            return (jnp.cos(freqs).astype(dtype), jnp.sin(freqs).astype(dtype))

        def _apply_rope(x, cos, sin):
            x_even = x[..., 0::2]
            x_odd = x[..., 1::2]
            rot_even = x_even * cos - x_odd * sin
            rot_odd = x_odd * cos + x_even * sin
            return jnp.stack([rot_even, rot_odd], axis=-1).reshape(x.shape)
        B, S, E = query.shape
        H, D = (NUM_HEADS, HEAD_DIM)
        q = (query @ Wq.T + bq).reshape(B, S, H, D).transpose(0, 2, 1, 3)
        k = (key @ Wk.T + bk).reshape(B, S, H, D).transpose(0, 2, 1, 3)
        v = (value @ Wv.T + bv).reshape(B, S, H, D).transpose(0, 2, 1, 3)
        cos, sin = _rope_cache(S, D, q.dtype)
        q = _apply_rope(q, cos, sin)
        k = _apply_rope(k, cos, sin)
        scores = jnp.einsum('bhsd,bhtd->bhst', q, k) / math.sqrt(D)
        attn = jax.nn.softmax(scores, axis=-1)
        out = jnp.einsum('bhst,bhtd->bhsd', attn, v)
        out = out.transpose(0, 2, 1, 3).reshape(B, S, E)
        return out @ Wo.T + bo

    def _L0_ffn_ref(x, shared_up, shared_gate, shared_down, routed_up, routed_gate, routed_down, router_w):
        import jax, jax.numpy as jnp
        import numpy as np
        H = 128
        DFF = 512
        E_ROUTED = 7
        TOP_K = 2

        def _swiglu(flat, gate_w, up_w, down_w):
            g = flat @ gate_w.T
            up = flat @ up_w.T
            return jax.nn.silu(g) * up @ down_w.T
        orig_shape = x.shape
        flat = x.reshape(-1, H)
        out = _swiglu(flat, shared_gate, shared_up, shared_down)
        logits = flat @ router_w.T
        probs = jax.nn.softmax(logits, axis=-1)
        top_vals, top_idx = jax.lax.top_k(probs, TOP_K)
        top_vals = top_vals / (top_vals.sum(-1, keepdims=True) + 1e-09)
        combine = jnp.sum(jax.nn.one_hot(top_idx, E_ROUTED, dtype=flat.dtype) * top_vals[..., None], axis=1)
        routed = jnp.zeros_like(flat)
        for e in range(E_ROUTED):
            eo = _swiglu(flat, routed_gate[e], routed_up[e], routed_down[e])
            routed = routed + combine[:, e:e + 1] * eo
        return (out + routed).reshape(orig_shape)

    def _L1_xattn_ref(query, key, value, spatial_bias, directional_bias, key_padding_mask, attn_mask, Wq, bq, Wk, bk, Wv, bv, Wo, bo):
        import jax, jax.numpy as jnp
        import numpy as np
        E = 128
        H = 16
        D = E // H
        B, T, _ = query.shape
        S = key.shape[1]
        scale = D ** (-0.5)
        q = (query @ Wq.T + bq).reshape(B, T, H, D).transpose(0, 2, 1, 3)
        k = (key @ Wk.T + bk).reshape(B, S, H, D).transpose(0, 2, 1, 3)
        v = (value @ Wv.T + bv).reshape(B, S, H, D).transpose(0, 2, 1, 3)
        scores = jnp.einsum('bhtd,bhsd->bhts', q, k) * scale
        scores = scores + attn_mask[None, None, :, :]
        pad = key_padding_mask[:, None, None, :]
        scores = jnp.where(pad, -jnp.inf, scores)
        if T == S:
            scores = scores + spatial_bias + directional_bias
        probs = jax.nn.softmax(scores, axis=-1)
        out = jnp.einsum('bhts,bhsd->bhtd', probs, v)
        out = out.transpose(0, 2, 1, 3).reshape(B, T, E)
        return out @ Wo.T + bo

    def _L1_ffn_ref(x, gate_w, expert_bias, w1, b1, w2, b2, w3, b3, sw1, sb1, sw2, sb2, sw3, sb3):
        import jax, jax.numpy as jnp
        import numpy as np
        B, S, D = (4, 256, 128)
        DFF = 64
        E = 16
        TOP_K = 2
        N_SHARED = 2
        FUSED_DFF = DFF * N_SHARED
        Bv, Sv, Dv = x.shape
        xf = x.reshape(-1, Dv)
        logits = xf @ gate_w.T
        scores = jax.nn.sigmoid(logits)
        biased = logits + expert_bias.astype(logits.dtype)[None, :]
        _, topk_idx = jax.lax.top_k(biased, TOP_K)
        topk_w = jnp.take_along_axis(scores, topk_idx, axis=-1)
        topk_w = topk_w / (topk_w.sum(-1, keepdims=True) + 1e-10)
        gatew = (jax.nn.one_hot(topk_idx, E, dtype=xf.dtype) * topk_w[..., None]).sum(1)
        y = jnp.zeros_like(xf)
        for e in range(E):
            h = jax.nn.silu(xf @ w1[e].T + b1[e]) * (xf @ w3[e].T + b3[e])
            y = y + gatew[:, e:e + 1] * (h @ w2[e].T + b2[e])
        hs = jax.nn.silu(xf @ sw1.T + sb1) * (xf @ sw3.T + sb3)
        y = y + hs @ sw2.T + sb2
        return y.reshape(Bv, Sv, Dv)

    def _L2_xattn_ref(Q, K, V, W_q, b_q, W_k, b_k, W_v, b_v, W_o, b_o):
        import jax, jax.numpy as jnp
        import numpy as np
        D_MODEL = 128
        NUM_HEADS = 16
        D_K = D_MODEL // NUM_HEADS
        B, S, _ = Q.shape
        H, d_k = (NUM_HEADS, D_K)
        q = Q @ W_q.T + b_q
        k = K @ W_k.T + b_k
        v = V @ W_v.T + b_v
        q = q.reshape(B, S, H, d_k).transpose(0, 2, 1, 3)
        k = k.reshape(B, S, H, d_k).transpose(0, 2, 1, 3)
        v = v.reshape(B, S, H, d_k).transpose(0, 2, 1, 3)
        scores = jnp.einsum('bhqd,bhkd->bhqk', q, k) / jnp.sqrt(jnp.float32(d_k)).astype(q.dtype)
        attn = jax.nn.softmax(scores, axis=-1)
        out = jnp.einsum('bhqk,bhkd->bhqd', attn, v)
        out = out.transpose(0, 2, 1, 3).reshape(B, S, H * d_k)
        return out @ W_o.T + b_o

    def _L2_ffn_ref(x, gate_w, gate_b, We1, be1, We2, be2, We3, be3, ws1, bs1, ws2, bs2, ws3, bs3):
        import jax, jax.numpy as jnp
        import numpy as np
        DIM = 128
        E = 16
        TOPK = 2
        G = 4
        TOPK_G = 2
        INTER = 64
        N_SHARED = 2
        ROUTE_SCALE = 1.0

        def _gate(xf, gate_w, gate_b):
            scores = xf @ gate_w.T
            scores = jax.nn.softmax(scores.astype(jnp.float32), axis=-1)
            orig = scores
            scores = scores + gate_b
            T = xf.shape[0]
            sg = scores.reshape(T, G, E // G)
            group_scores = jax.lax.top_k(sg, 2)[0].sum(-1)
            _, gidx = jax.lax.top_k(group_scores, TOPK_G)
            keep = jax.nn.one_hot(gidx, G).sum(axis=1) > 0
            sg = jnp.where(keep[:, :, None], sg, -jnp.inf)
            scores = sg.reshape(T, E)
            _, idx = jax.lax.top_k(scores, TOPK)
            weights = jnp.take_along_axis(orig, idx, axis=1)
            weights = (weights * ROUTE_SCALE).astype(xf.dtype)
            return (weights, idx)
        shape = x.shape
        xf = x.reshape(-1, DIM)
        weights, idx = _gate(xf, gate_w, gate_b)
        combine = (jax.nn.one_hot(idx, E, dtype=xf.dtype) * weights[..., None]).sum(1)
        h1 = jnp.einsum('td,edi->tei', xf, We1) + be1
        h3 = jnp.einsum('td,edi->tei', xf, We3) + be3
        h = jax.nn.silu(h1) * h3
        yo = jnp.einsum('tei,eid->ted', h, We2) + be2
        y = jnp.einsum('te,ted->td', combine, yo)
        z = jax.nn.silu(xf @ ws1 + bs1) * (xf @ ws3 + bs3) @ ws2 + bs2
        return (y + z).reshape(shape)

    def _L3_xattn_ref(Q, K, V, mask, W_q, W_k, W_v, W_o):
        import jax, jax.numpy as jnp
        import numpy as np
        NUM_HEADS = 16
        TOKEN_DIM = 128
        D_HEAD = TOKEN_DIM // NUM_HEADS

        def masked_softmax(scores, mask):
            scores = jnp.clip(scores, -50.0, 50.0)
            exp_scores = jnp.exp(scores)
            if mask is not None:
                exp_scores = jnp.where(mask, exp_scores, 0.0)
            denom = jnp.sum(exp_scores, axis=-1, keepdims=True)
            denom = jnp.where(denom <= 0.0, 1.0, denom)
            return exp_scores / denom
        B = Q.shape[0]
        q = (Q @ W_q.T).reshape(B, -1, NUM_HEADS, D_HEAD).transpose(0, 2, 1, 3)
        k = (K @ W_k.T).reshape(B, -1, NUM_HEADS, D_HEAD).transpose(0, 2, 1, 3)
        v = (V @ W_v.T).reshape(B, -1, NUM_HEADS, D_HEAD).transpose(0, 2, 1, 3)
        scores = jnp.einsum('bhqd,bhkd->bhqk', q, k) / np.sqrt(D_HEAD)
        m = mask[:, None, :, None] if mask is not None else None
        attn = masked_softmax(scores, m)
        out = jnp.einsum('bhqk,bhkd->bhqd', attn, v)
        out = out.transpose(0, 2, 1, 3).reshape(B, -1, NUM_HEADS * D_HEAD)
        return out @ W_o.T

    def _L3_ffn_ref(x, W_router, b_router, experts_inter, experts_out):
        import jax, jax.numpy as jnp
        import numpy as np
        import math
        B, S, H, I, E = (4, 256, 128, 512, 8)
        TOP_K = 2
        CAPACITY_FACTOR = 1.25
        b, s, h = x.shape
        e = experts_inter.shape[0]
        T = b * s
        capacity = math.ceil(T / e * CAPACITY_FACTOR)
        x_flat = x.reshape(T, h)
        logits = x_flat @ W_router.T + b_router
        weights_flat = jax.nn.softmax(logits, axis=-1)
        top_vals, top_idx = jax.lax.top_k(weights_flat, TOP_K)
        topk_flat = jnp.zeros_like(weights_flat).at[jnp.arange(T)[:, None], top_idx].set(top_vals)
        routing_mask = (topk_flat > 0).astype(jnp.int32)
        order = jnp.argsort(-routing_mask, axis=0, stable=True)
        sorted_mask = jnp.take_along_axis(routing_mask, order, axis=0)
        sorted_mask = sorted_mask[:capacity]
        sorted_idx = order[:capacity]
        used_tokens = (sorted_idx * sorted_mask).reshape(-1)
        mask_flat = sorted_mask.reshape(-1).astype(x.dtype)
        inputs_tokens = x_flat[used_tokens] * mask_flat[:, None]
        inputs_tokens = inputs_tokens.reshape(capacity, e, h)
        inputs_weights = jnp.take_along_axis(topk_flat, sorted_idx, axis=0)
        hmid = jnp.einsum('ceh,ehi->cei', inputs_tokens, experts_inter)
        hmid = jax.nn.relu(hmid)
        out = jnp.einsum('cei,eih->ceh', hmid, experts_out)
        out = out * inputs_weights[:, :, None]
        combined = jnp.zeros((T, h), dtype=x.dtype).at[used_tokens].add(out.reshape(-1, h))
        return combined.reshape(b, s, h)
    x = x + jnp.tanh(g_xattn[0]) * _L0_xattn_ref(_layernorm(x, axis=-1), ctx_1024, ctx_1024, L0_xattn_Wq, L0_xattn_bq, L0_xattn_Wk, L0_xattn_bk, L0_xattn_Wv, L0_xattn_bv, L0_xattn_Wo, L0_xattn_bo)
    x = x + jnp.tanh(g_ffn[0]) * _L0_ffn_ref(_layernorm(x, axis=-1), L0_ffn_shared_up, L0_ffn_shared_gate, L0_ffn_shared_down, L0_ffn_routed_up, L0_ffn_routed_gate, L0_ffn_routed_down, L0_ffn_router_w)
    x = x + jnp.tanh(g_xattn[1]) * _L1_xattn_ref(_layernorm(x, axis=-1), ctx_1024, ctx_1024, fside_Bx16xSxS2_0, fside_Bx16xSxS2_0, mask_BxS2_bf0, fside_SxS2_0, L1_xattn_Wq, L1_xattn_bq, L1_xattn_Wk, L1_xattn_bk, L1_xattn_Wv, L1_xattn_bv, L1_xattn_Wo, L1_xattn_bo)
    x = x + jnp.tanh(g_ffn[1]) * _L1_ffn_ref(_layernorm(x, axis=-1), L1_ffn_gate_w, L1_ffn_expert_bias, L1_ffn_w1, L1_ffn_b1, L1_ffn_w2, L1_ffn_b2, L1_ffn_w3, L1_ffn_b3, L1_ffn_sw1, L1_ffn_sb1, L1_ffn_sw2, L1_ffn_sb2, L1_ffn_sw3, L1_ffn_sb3)
    x = x + jnp.tanh(g_xattn[2]) * _L2_xattn_ref(_layernorm(x, axis=-1), ctx_1024, ctx_1024, L2_xattn_W_q, L2_xattn_b_q, L2_xattn_W_k, L2_xattn_b_k, L2_xattn_W_v, L2_xattn_b_v, L2_xattn_W_o, L2_xattn_b_o)
    x = x + jnp.tanh(g_ffn[2]) * _L2_ffn_ref(_layernorm(x, axis=-1), L2_ffn_gate_w, L2_ffn_gate_b, L2_ffn_We1, L2_ffn_be1, L2_ffn_We2, L2_ffn_be2, L2_ffn_We3, L2_ffn_be3, L2_ffn_ws1, L2_ffn_bs1, L2_ffn_ws2, L2_ffn_bs2, L2_ffn_ws3, L2_ffn_bs3)
    x = x + jnp.tanh(g_xattn[3]) * _L3_xattn_ref(_layernorm(x, axis=-1), ctx_1024, ctx_1024, mask_BxS_bf1, L3_xattn_W_q, L3_xattn_W_k, L3_xattn_W_v, L3_xattn_W_o)
    x = x + jnp.tanh(g_ffn[3]) * _L3_ffn_ref(_layernorm(x, axis=-1), L3_ffn_W_router, L3_ffn_b_router, L3_ffn_experts_inter, L3_ffn_experts_out)
    return x

_drawn_inputs = setup_inputs


def setup_inputs(seed=0):
    import zlib

    import numpy as np

    out = dict(_drawn_inputs(seed))
    spreads = {'L0_xattn_bq': (0.0, 0.329),
     'L0_xattn_bk': (0.0, 0.519),
     'L0_xattn_bv': (0.0, 0.1),
     'L0_xattn_bo': (0.0, 0.1),
     'L1_xattn_bq': (0.0, 0.319),
     'L1_xattn_bk': (0.0, 2.0),
     'L1_xattn_bv': (0.0, 0.1),
     'L1_xattn_bo': (0.0, 0.1),
     'L1_ffn_expert_bias': (0.0, 0.1),
     'L2_xattn_b_q': (0.0, 0.433),
     'L2_xattn_b_k': (0.0, 2.0),
     'L2_xattn_b_v': (0.0, 0.1),
     'L2_xattn_b_o': (0.0, 0.1),
     'L2_ffn_gate_b': (0.0, 0.1),
     'L2_ffn_be1': (0.0, 0.789),
     'L2_ffn_be2': (0.0, 0.485),
     'L2_ffn_be3': (0.0, 0.8),
     'L2_ffn_bs1': (0.0, 0.1),
     'L2_ffn_bs2': (0.0, 0.1),
     'L2_ffn_bs3': (0.0, 0.269),
     'L3_ffn_b_router': (0.0, 0.8)}
    factors = {'fside_SxS2_0': 3.162,
     'g_ffn': 8.0,
     'L0_ffn_shared_up': 4.824,
     'L0_ffn_shared_gate': 4.292,
     'L0_ffn_shared_down': 4.277,
     'L0_ffn_routed_up': 5.679,
     'L0_ffn_routed_gate': 5.596,
     'L0_ffn_routed_down': 5.653,
     'L0_ffn_router_w': 5.675,
     'L1_ffn_b1': 8.0,
     'L1_ffn_b3': 7.767,
     'L1_ffn_sb1': 5.733,
     'L1_ffn_sb3': 5.399,
     'L3_ffn_W_router': 3.824,
     'L3_ffn_experts_inter': 4.09,
     'L3_ffn_experts_out': 3.449}
    for name, (base, spread) in spreads.items():
        noise = np.random.default_rng([zlib.crc32(name.encode()), seed]).standard_normal(out[name].shape)
        drawn = base * np.exp(spread * noise) if base else spread * noise
        out[name] = jnp.asarray(drawn.astype(out[name].dtype))
    for name, factor in factors.items():
        out[name] = (out[name] * factor).astype(out[name].dtype)
    return out
```

```python
from contextlib import ExitStack

import concourse.bass as bass
from concourse import mybir

ALU = mybir.AluOpType
ACT = mybir.ActivationFunctionType
AX_X = mybir.AxisListType.X
F32 = mybir.dt.float32
F16 = mybir.dt.float16
U8 = mybir.dt.uint8

P = 128
B, S, D = 16, 64, 128
HEADS, HD = 16, 8
LAYERS = 4
TILES = B * S // P
HALF = 512
HP = HEADS // 2
SCALE = HD ** -0.5
EPS = 1e-5
NEG = -1e30
CAPACITY = 160

EXPERTS = [7, 16, 16, 8]
ROUTER_AT = [0, 7, 23, 39]
CHUNKS = [32, 9, 9, 32]
PER_EXPERT = [4, 9, 9, 4]
MATS = [3, 3, 3, 2]
UNITS = [2 * c for c in CHUNKS]
UNIT_AT = [sum(UNITS[:l]) for l in range(LAYERS + 1)]
FFN_COLS = [CHUNKS[l] * MATS[l] * P for l in range(LAYERS)]
GRAIN = 768
AW_COLS = 18 * P
COMB = 17
SUMS = [16, 2, 2, 16]
SUM_AT = [sum(SUMS[:l]) for l in range(LAYERS + 1)]

GRAINS = []
for _l in range(LAYERS):
    for _c in range(0, FFN_COLS[_l], GRAIN):
        GRAINS.append((_l, _c, min(GRAIN, FFN_COLS[_l] - _c)))
GRAIN_AT = [next(n for n, g in enumerate(GRAINS) if g[0] == l) for l in range(LAYERS)]


def bc_last(ap, n):
    return ap.unsqueeze(len(ap.shape)).broadcast_to(list(ap.shape) + [n])


def bc_mid(ap, n):
    return ap.unsqueeze(1).broadcast_to([ap.shape[0], n, ap.shape[1]])


def build(nc, a):
    ctx = ExitStack()
    with ctx:
        def sb(name, shape, dt=F32):
            return ctx.enter_context(nc.sbuf_tensor(name, shape, dt))

        def sem(name):
            return ctx.enter_context(nc.semaphore(name))

        bank = [ctx.enter_context(nc.psum_tensor(f"bank{i}", [P, 512], F32)) for i in range(8)]

        X = sb("X", [P, TILES, D])
        XN = sb("XN", [P, TILES, D])
        xT = sb("xT", [P, 2, B * S], F16)
        QT = sb("QT", [P, 2, B * S], F16)
        KT = sb("KT", [P, 2, B * S], F16)
        KM = sb("KM", [P, 2, HD, B * S], F16)
        VH = sb("VH", [P, B, HP, 2, HD + 1], F16)
        VL = sb("VL", [P, B, HP, 2, HD + 1], F16)
        CT = sb("CT", [P, 2, B, 2, S], F16)
        AW = sb("AW", [P, 2, 18, P], F16)
        WA = sb("WA", [P, 2, FFN_COLS[0]], F16)
        WB = sb("WB", [P, 2, FFN_COLS[1]], F16)
        stage = sb("stage", [P, 2, GRAIN])
        CB = sb("CB", [P, 4, B * S])
        work = sb("work", [P, 4096])
        BIAS = sb("BIAS", [P, 2, HEADS, S])
        ident = sb("ident", [P, P])
        before = sb("before", [P, P], F16)
        ones16 = sb("ones16", [P, P], F16)
        ones8 = sb("ones8", [P, TILES])
        expo = sb("expo", [P, TILES])
        cols = sb("cols", [P, 50])
        rope = sb("rope", [P, 2, S])
        BO = sb("BO", [P, LAYERS, D])
        TG = sb("TG", [P, 8])
        RW = sb("RW", [P, 2, 47], F16)
        rw32 = sb("rw32", [P, 47])
        RB = sb("RB", [P, 40])
        SXS = sb("SXS", [P, S])
        base = sb("base", [P, TILES, S])
        pad8 = sb("pad8", [P, TILES, S], U8)
        qm8 = sb("qm8", [P, TILES], U8)
        QM = sb("QM", [P, TILES])
        B2 = sb("B2", [COMB, 2, D])
        REV = sb("REV", [P, HEADS])
        bn = sb("bn", [P, TILES, 6])
        mv = sb("mv", [P, TILES, 2])
        veps = sb("veps", [P, TILES])
        rstd = sb("rstd", [P, TILES])
        top = sb("top", [P, 2, HEADS])
        rden = sb("rden", [P, 2, HEADS])
        ON = [sb(f"ON{i}", [P, D]) for i in range(2)]
        OT = sb("OT", [P, 2, P], F16)
        rt = [sb(f"rt{i}", [P, TILES * 16]) for i in range(8)]
        rs = [sb(f"rs{i}", [P, 32]) for i in range(8)]
        mask16 = sb("mask16", [P, TILES * 8], F16)
        comb = sb("comb", [P, TILES * COMB])
        combT = sb("combT", [COMB, B * S])

        prob = [work[:, 0:1024], work[:, 1024:2048]]
        PT = [[work[:, at:at + 512].bitcast(F16) for at in (lo, lo + 512)] for lo in (2048, 3072)]
        gated = [work[:, 0:512], work[:, 512:1024]]
        h32 = [work[:, 1024:1536], work[:, 1536:2048]]
        hh = work[:, 2048:3072].bitcast(F16).rearrange("p (s n) -> p s n", s=4)
        hl = work[:, 3072:4096].bitcast(F16).rearrange("p (s n) -> p s n", s=4)
        raw = WB[:, :, :].rearrange("p a n -> p (a n)").bitcast(F32)

        comb_dram = nc.dram_tensor("comb_scratch", [2, COMB, B * S], F32, kind="Internal").ap()

        names = """consts_in rw_in aw_in ctx_in x_in fside_in0 fside_in1 stage_in0 stage_in1 km_in km_zero
        comb_out comb_in0 comb_in1 comb_in2 comb_in3 out_done
        ident_made consts_made tanh_made aw_hi aw_lo ctx_hi ctx_lo rw_hi
        dve_step pool_step split_hi split_lo bias_ready
        var_ready rstd_ready xn_ready xn_turned xh_ready xl_ready
        k_proj k_rot k_hi k_lo v_proj v_hi v_lo q_proj q_rot q_hi q_lo
        scores shifted probs pt_turned pt_hi pt_lo pv o_norm o_turned ot_hi ot_lo y_done x_attn
        logits copied exp_in exp_out counts_in counts comb_ready comb_turned combT_ready
        gate_done up_done silu_done h32_done hh_done hl_done down_done sum_done sum_read x_out""".split()
        s = {n: sem(n) for n in names}

        def aw(i, hl):
            return AW[:, hl, i, :]

        def weight(l, chunk, m, hl):
            at = (chunk * MATS[l] + m) * P
            return (WA if l in (0, 3) else WB)[:, hl, at:at + P]

        def grain_of(l, chunk):
            return GRAIN_AT[l] + ((chunk + 1) * MATS[l] * P - 1) // GRAIN + 1

        block = ctx.enter_context(nc.Block())

        @block.sync
        def _(sp):
            sp.dma_start(raw[:, 0:AW_COLS], a["attn_w"]).then_inc(s["aw_in"], 16)
            sp.dma_start(raw[:, AW_COLS:AW_COLS + B * S], a["ctxT"]).then_inc(s["ctx_in"], 16)
            sp.dma_start(X[:, :, :], a["x"].rearrange("(t p) d -> p t d", p=P)).then_inc(s["x_in"], 16)
            sp.dma_start(rw32[:, :], a["router_w"]).then_inc(s["rw_in"], 16)
            for dst, src in (
                (cols[:, :], a["cols"]), (rope[:, :, :], a["rope"]),
                (BO[:, :, :], a["bo"].partition_broadcast(P)), (TG[:, :], a["gates"].partition_broadcast(P)),
                (RB[:, :], a["router_b"].partition_broadcast(P)), (SXS[:, :], a["sxs"]),
                (pad8[0:S, :, :], a["pad"][0].partition_broadcast(S)),
                (pad8[S:P, :, :], a["pad"][1].partition_broadcast(S)),
                (qm8[:, :], a["qmask"]), (B2[:, :, :], a["b2"]),
            ):
                sp.dma_start(dst, src).then_inc(s["consts_in"], 16)

            def load_grain(n):
                l, c, w = GRAINS[n]
                if n >= 2:
                    sp.wait_ge(s["split_lo"], n - 1)
                sp.dma_start(stage[:, n % 2, 0:w], a[f"ffn_w{l}"][:, c:c + w]).then_inc(s[f"stage_in{n % 2}"], 16)

            def place_keys(l):
                sp.wait_ge(s["k_lo"], 2 * l + 2)
                if l == 0:
                    sp.wait_ge(s["km_zero"], 2)
                else:
                    sp.wait_ge(s["scores"], TILES * l)
                for j in range(HD):
                    for r in (0, S):
                        lo = r + HD * j
                        sp.dma_start(KM[lo:lo + HD, :, j, :], KT[lo:lo + HD, :, :]).then_inc(s["km_in"], 16)

            def load_fside(p):
                if p >= 2:
                    sp.wait_ge(s["shifted"], TILES + p - 1)
                sp.dma_start(BIAS[:, p % 2, :, :].rearrange("p h k -> p (h k)"),
                             a["fside"][p]).then_inc(s[f"fside_in{p % 2}"], 16)

            def spread_comb(l):
                sp.wait_ge(s["combT_ready"], l)
                sp.dma_start(comb_dram[l - 1], combT[:, :]).then_inc(s["comb_out"], 16)
                sp.wait_ge(s["comb_out"], 16 * l)
                for j in range(8):
                    if j >= 4:
                        sp.wait_ge(s["h32_done"], UNIT_AT[l] + 2 * (j - 4 + 1) + 2)
                    for e in range(2):
                        sp.dma_start(CB[S * e:S * e + S, j % 4, :],
                                     comb_dram[l - 1, 1 + 2 * j + e].partition_broadcast(S)
                                     ).then_inc(s[f"comb_in{j % 4}"], 16)

            for n in range(4):
                load_grain(n)
            place_keys(0)
            for n in range(4, GRAIN_AT[1]):
                load_grain(n)
            for n in range(GRAIN_AT[1], GRAIN_AT[1] + 2):
                load_grain(n)
            place_keys(1)
            for n in range(GRAIN_AT[1] + 2, GRAIN_AT[2] + 2):
                load_grain(n)
            for p in range(TILES):
                load_fside(p)
            place_keys(2)
            spread_comb(1)
            for n in range(GRAIN_AT[2] + 2, GRAIN_AT[3] + 2):
                load_grain(n)
            place_keys(3)
            spread_comb(2)
            for n in range(GRAIN_AT[3] + 2, len(GRAINS)):
                load_grain(n)
            for t in range(2):
                sp.wait_ge(s["sum_read"], SUM_AT[4] - 1 + t)
                sp.dma_start(a["out"].rearrange("(t p) d -> p t d", p=P)[:, 4 * t:4 * t + 4, :],
                             X[:, 4 * t:4 * t + 4, :]).then_inc(s["out_done"], 16)
            sp.wait_ge(s["out_done"], 32)

        @block.gpsimd
        def _(pool):
            steps = [0]

            def step(ins):
                steps[0] += 1
                ins.then_inc(s["pool_step"], 1)

            def settle():
                pool.wait_ge(s["pool_step"], steps[0])

            def link(ins):
                step(ins)
                settle()

            link(pool.memset(ident[:, :], 0.0))
            link(pool.memset(before[:, :], 1.0))
            link(pool.memset(expo[:, :], -0.5))
            pool.affine_select(out=ident[:, :], in_=ident[:, :], compare_op=ALU.not_equal, fill=1.0, base=0,
                               pattern=[[-1, P]], channel_multiplier=1).then_inc(s["ident_made"], 1)
            pool.wait_ge(s["ident_made"], 1)
            for hl_ in range(2):
                pool.memset(KM[:, hl_, :, :].rearrange("p j n -> p (j n)").bitcast(F32), 0.0
                            ).then_inc(s["km_zero"], 1)
                pool.wait_ge(s["km_zero"], hl_ + 1)
            for v in (VH, VL):
                link(pool.memset(v[:, :, :, :, :].rearrange("p b h e d -> p (b h e d)"), 0.0))
            for e in range(2):
                link(pool.memset(VH[S * e:S * e + S, :, :, e, HD], 1.0))
            link(pool.affine_select(out=before[:, :], in_=before[:, :], compare_op=ALU.is_gt, fill=0.0, base=0,
                                    pattern=[[1, P]], channel_multiplier=-1))
            link(pool.memset(ones16[:, :], 1.0))
            link(pool.memset(ones8[:, :], 1.0))
            for j in range(HEADS):
                link(pool.memset(REV[:, j:j + 1], float(HEADS - j)))
            pool.memset(REV[:, 0:1], float(HEADS)).then_inc(s["consts_made"], 1)
            pool.wait_ge(s["consts_made"], 1)

            def split_grain(n):
                l, c, w = GRAINS[n]
                dst = WA if l in (0, 3) else WB
                pool.wait_ge(s[f"stage_in{n % 2}"], 16 * (n // 2 + 1))
                if n == GRAIN_AT[1]:
                    pool.wait_ge(s["aw_lo"], 1)
                    pool.wait_ge(s["ctx_lo"], 1)
                if n == GRAIN_AT[2]:
                    pool.wait_ge(s["down_done"], UNIT_AT[2])
                if n == GRAIN_AT[3]:
                    pool.wait_ge(s["down_done"], UNIT_AT[1])
                pool.tensor_copy(dst[:, 0, c:c + w], stage[:, n % 2, 0:w]).then_inc(s["split_hi"], 1)
                pool.wait_ge(s["split_hi"], n + 1)
                pool.tensor_tensor(dst[:, 1, c:c + w], stage[:, n % 2, 0:w], dst[:, 0, c:c + w],
                                   ALU.subtract).then_inc(s["split_lo"], 1)
                pool.wait_ge(s["split_lo"], n + 1)

            def powers(n):
                for t in range(2):
                    pool.wait_ge(s["var_ready"], 2 * n + t + 1)
                    pool.tensor_tensor(rstd[:, 4 * t:4 * t + 4], veps[:, 4 * t:4 * t + 4],
                                       expo[:, 4 * t:4 * t + 4], ALU.pow).then_inc(s["rstd_ready"], 1)
                    pool.wait_ge(s["rstd_ready"], 2 * n + t + 1)

            def add_bias(p):
                pool.wait_ge(s[f"fside_in{p % 2}"], 16 * (p // 2 + 1))
                if p == 0:
                    pool.wait_ge(s["copied"], 1)
                pool.tensor_tensor(BIAS[:, p % 2, :, :], BIAS[:, p % 2, :, :], bc_mid(base[:, p, :], HEADS),
                                   ALU.add).then_inc(s["bias_ready"], 1)
                pool.wait_ge(s["bias_ready"], p + 1)

            powers(0)
            for n in range(GRAIN_AT[0], GRAIN_AT[1]):
                split_grain(n)
            powers(1)
            for n in range(GRAIN_AT[1], GRAIN_AT[2]):
                split_grain(n)
            add_bias(0)
            powers(2)
            for p in range(1, TILES):
                add_bias(p)
            powers(3)
            powers(4)
            for n in range(GRAIN_AT[2], GRAIN_AT[3]):
                split_grain(n)
            powers(5)
            powers(6)
            for n in range(GRAIN_AT[3], len(GRAINS)):
                split_grain(n)
            powers(7)

        @block.scalar
        def _(act):
            act.wait_ge(s["aw_in"], 16)
            act.activation(AW[:, 0, :, :].rearrange("p i n -> p (i n)"), raw[:, 0:AW_COLS], ACT.Copy
                           ).then_inc(s["aw_hi"], 1)
            act.wait_ge(s["ctx_in"], 16)
            ctx32 = raw[:, AW_COLS:AW_COLS + B * S].rearrange("p (b k) -> p b k", b=B)
            for e in range(2):
                act.activation(CT[:, 0, :, e, :], ctx32, ACT.Copy).then_inc(s["ctx_hi"], 1)
            act.wait_ge(s["rw_in"], 16)
            act.activation(RW[:, 0, :], rw32[:, :], ACT.Copy).then_inc(s["rw_hi"], 1)
            act.wait_ge(s["consts_in"], 160)
            act.activation(TG[:, :], TG[:, :], ACT.Tanh).then_inc(s["tanh_made"], 1)

            def keys_values(l):
                for t in range(2):
                    dst = KT[:, 0, HALF * t:HALF * t + HALF]
                    if t == 0 and l:
                        act.wait_ge(s["km_in"], 256 * l)
                    if l == 0:
                        act.wait_ge(s["k_rot"], t + 1)
                        act.activation(dst, work[:, HALF * t:HALF * t + HALF], ACT.Copy).then_inc(s["k_hi"], 1)
                    else:
                        act.wait_ge(s["k_proj"], 2 * l + t + 1)
                        act.activation(dst, bank[t][:, :], ACT.Identity, bias=cols[:, 3 * l + 1:3 * l + 2]
                                       ).then_inc(s["k_hi"], 1)
                if l == 0:
                    act.wait_ge(s["consts_made"], 1)
                for j in range(4):
                    act.wait_ge(s["v_proj"], 4 * l + j + 1)
                    for e in range(2):
                        rows = slice(S * e, S * e + S)
                        src = bank[2 + j][rows, :].rearrange("p (b h e d) -> p (b h) e d", b=4, h=HP, e=2)[:, :, e, :]
                        dst = VH[rows, 4 * j:4 * j + 4, :, e, 0:HD].rearrange("p b h d -> p (b h) d")
                        ins = act.activation(dst, src, ACT.Copy)
                    ins.then_inc(s["v_hi"], 1)

            def normed(n):
                for t in range(2):
                    act.wait_ge(s["xn_turned"], 2 * n + t + 1)
                    act.activation(xT[:, 0, HALF * t:HALF * t + HALF], bank[6 + t][:, :], ACT.Copy
                                   ).then_inc(s["xh_ready"], 1)

            def queries(l):
                for t in range(2):
                    dst = QT[:, 0, HALF * t:HALF * t + HALF]
                    if l == 0:
                        act.wait_ge(s["q_rot"], t + 1)
                        act.activation(dst, work[:, HALF * t:HALF * t + HALF], ACT.Copy).then_inc(s["q_hi"], 1)
                    else:
                        act.wait_ge(s["q_proj"], 2 * l + t + 1)
                        act.activation(dst, bank[t][:, :], ACT.Identity, bias=cols[:, 3 * l:3 * l + 1]
                                       ).then_inc(s["q_hi"], 1)

            def attention(l):
                exp_scale = 2.0 if l == 1 else SCALE
                for k in range(TILES + 4):
                    if 1 <= k <= TILES:
                        i = TILES * l + k - 1
                        for g in range(2):
                            act.wait_ge(s["pt_turned"], 2 * i + g + 1)
                            if i >= 2:
                                act.wait_ge(s["pv"], i - 1)
                            act.activation(PT[i % 2][0][:, HALF * g:HALF * g + HALF], bank[4 + g][:, :], ACT.Copy
                                           ).then_inc(s["pt_hi"], 1)
                    if k < TILES:
                        i = TILES * l + k
                        act.wait_ge(s["shifted"], i + 1)
                        act.activation(prob[k % 2], prob[k % 2], ACT.Exp, scale=exp_scale).then_inc(s["probs"], 1)
                    if 3 <= k < TILES + 3:
                        i = TILES * l + k - 3
                        act.wait_ge(s["o_turned"], i + 1)
                        act.wait_ge(s["y_done"], i)
                        act.activation(OT[:, 0, :], bank[7][:, 0:P], ACT.Identity, bias=cols[:, 3 * l + 2:3 * l + 3]
                                       ).then_inc(s["ot_hi"], 1)

            def ffn(l):
                at = UNIT_AT[l]
                act.wait_ge(s["exp_in"], l + 1)
                act.activation(rt[1][:, 0:TILES * EXPERTS[l]], rt[1][:, 0:TILES * EXPERTS[l]], ACT.Exp,
                               scale=-1.0 if l == 1 else 1.0).then_inc(s["exp_out"], 1)
                if l == 3:
                    for u in range(UNITS[l]):
                        act.wait_ge(s["gate_done"], at + u + 1)
                        if u >= 4:
                            act.wait_ge(s["down_done"], at + u - 3)
                        act.activation(hh[:, u % 4, :], bank[u % 4][:, :], ACT.Relu).then_inc(s["hh_done"], 1)
                    return
                for u in range(UNITS[l] + 1):
                    if u < UNITS[l]:
                        act.wait_ge(s["gate_done"], at + u + 1)
                        if u >= 2:
                            act.wait_ge(s["h32_done"], at + u - 1)
                        kind = {"bias": cols[:, 12 + 18 * (l - 1) + u // 2:13 + 18 * (l - 1) + u // 2]} if l else {}
                        act.activation(gated[u % 2], bank[u % 2][:, :], ACT.Silu, **kind).then_inc(s["silu_done"], 1)
                    if u >= 1:
                        v = u - 1
                        act.wait_ge(s["h32_done"], at + v + 1)
                        if v >= 4:
                            act.wait_ge(s["down_done"], at + v - 3)
                        act.activation(hh[:, v % 4, :], h32[v % 2], ACT.Copy).then_inc(s["hh_done"], 1)

            keys_values(0)
            for l in range(LAYERS):
                normed(2 * l)
                queries(l)
                attention(l)
                normed(2 * l + 1)
                if l < 3:
                    keys_values(l + 1)
                ffn(l)

        @block.tensor
        def _(pe):
            def three(out, lhsT, rhs, start=True, stop=True):
                pe.matmul(out, lhsT(0), rhs(0), start=start, stop=False, skip_group_check=True)
                pe.matmul(out, lhsT(1), rhs(0), start=False, stop=False, skip_group_check=True)
                return pe.matmul(out, lhsT(0), rhs(1), start=False, stop=stop, skip_group_check=True)

            def project(out, w, src, t):
                return three(out, lambda h: aw(w, h), lambda h: src(h)[:, HALF * t:HALF * t + HALF] if src else
                             CT[:, h, 8 * t:8 * t + 8, 0, :])

            def keys_values(l):
                if l == 0:
                    pe.wait_ge(s["aw_lo"], 1)
                    pe.wait_ge(s["ctx_lo"], 2)
                for t in range(2):
                    mm = project(bank[t][:, :].rearrange("p (b k) -> p b k", b=8), 4 * l + 1, None, t)
                    if l == 0:
                        mm = project(bank[6 + t][:, :].rearrange("p (b k) -> p b k", b=8), 17, None, t)
                    mm.then_inc(s["k_proj"], 1)
                for j in range(4):
                    for b in range(4):
                        mm = three(bank[2 + j][:, P * b:P * b + P],
                                   lambda h: CT[:, h, 4 * j + b, :, :].rearrange("p e k -> p (e k)"),
                                   lambda h: aw(4 * l + 2, h), start=(b == 0))
                    mm.then_inc(s["v_proj"], 1)

            def normed(n):
                if n == 0:
                    pe.wait_ge(s["ident_made"], 1)
                for t in range(2):
                    pe.wait_ge(s["xn_ready"], 2 * n + t + 1)
                    for q in range(4):
                        mm = pe.transpose(bank[6 + t][:, P * q:P * q + P], XN[:, 4 * t + q, :], ident[:, :])
                    mm.then_inc(s["xn_turned"], 1)

            def xn_split(n, t):
                pe.wait_ge(s["xh_ready"], 2 * n + t + 1)
                pe.wait_ge(s["xl_ready"], 2 * n + t + 1)

            def queries(l):
                for t in range(2):
                    xn_split(2 * l, t)
                    mm = project(bank[t][:, :], 4 * l, lambda h: xT[:, h, :], t)
                    if l == 0:
                        mm = project(bank[2 + t][:, :], 16, lambda h: xT[:, h, :], t)
                    mm.then_inc(s["q_proj"], 1)

            def take_scores(l, p):
                i = TILES * l + p
                if p == 0:
                    pe.wait_ge(s["km_in"], 256 * (l + 1))
                    pe.wait_ge(s["q_lo"], 2 * l + 2)
                    pe.wait_ge(s["q_hi"], 2 * l + 2)
                if p >= 2:
                    pe.wait_ge(s["shifted"], i - 1)
                for ha, hb in ((0, 0), (1, 0), (0, 1)):
                    for r in range(2):
                        for b in range(2):
                            rows = slice(S * r, S * r + S)
                            tok = slice(P * p + S * b, P * p + S * b + S)
                            mm = pe.matmul(bank[2 * (p % 2) + r][S * b:S * b + S, :].rearrange("p (j k) -> p j k", j=HD),
                                           QT[rows, ha, tok], KM[rows, hb, :, tok],
                                           start=(ha == 0 and hb == 0), stop=(hb == 1))
                mm.then_inc(s["scores"], 1)

            def turn_probs(l, p):
                i = TILES * l + p
                pe.wait_ge(s["probs"], i + 1)
                for g in range(2):
                    if i >= 1:
                        pe.wait_ge(s["pt_lo"], 2 * i - 1 + g)
                    for q in range(4):
                        at = (4 * g + q) * P
                        mm = pe.transpose(bank[4 + g][:, P * q:P * q + P], prob[p % 2][:, at:at + P], ident[:, :])
                    mm.then_inc(s["pt_turned"], 1)

            def weigh_values(l, p):
                i = TILES * l + p
                if i == 0:
                    pe.wait_ge(s["v_lo"], 4)
                    pe.wait_ge(s["consts_made"], 1)
                if i >= 1:
                    pe.wait_ge(s["o_norm"], i)
                for g in range(2):
                    pe.wait_ge(s["pt_hi"], 2 * i + g + 1)
                    pe.wait_ge(s["pt_lo"], 2 * i + g + 1)
                    for q in range(4 * g, 4 * g + 4):
                        for ha, v in ((0, VH), (1, VH), (0, VL)):
                            for b in range(2):
                                mm = pe.matmul(bank[6][S * b:S * b + S, 18 * q:18 * q + 18],
                                               PT[i % 2][ha][:, P * q + S * b:P * q + S * b + S],
                                               v[:, 2 * p + b, q, :, :].rearrange("p e d -> p (e d)"),
                                               start=(q == 0 and ha == 0 and v is VH), stop=(v is VL),
                                               skip_group_check=True)
                mm.then_inc(s["pv"], 1)

            def turn_out(l, p):
                i = TILES * l + p
                pe.wait_ge(s["o_norm"], i + 1)
                if i >= 1:
                    pe.wait_ge(s["x_attn"], i)
                pe.transpose(bank[7][:, 0:P], ON[p % 2][:, :], ident[:, :]).then_inc(s["o_turned"], 1)

            def project_out(l, p):
                i = TILES * l + p
                pe.wait_ge(s["ot_hi"], i + 1)
                pe.wait_ge(s["ot_lo"], i + 1)
                three(bank[7][:, P:2 * P], lambda h: OT[:, h, :], lambda h: aw(4 * l + 3, h)
                      ).then_inc(s["y_done"], 1)

            def attention(l):
                take_scores(l, 0)
                for k in range(TILES + 4):
                    if k >= 4:
                        project_out(l, k - 4)
                    if 1 <= k <= TILES:
                        turn_probs(l, k - 1)
                    if k + 1 < TILES:
                        take_scores(l, k + 1)
                    if 2 <= k < TILES + 2:
                        weigh_values(l, k - 2)
                    if 3 <= k < TILES + 3:
                        turn_out(l, k - 3)

            def ffn(l):
                at, experts = UNIT_AT[l], EXPERTS[l]
                for t in range(2):
                    xn_split(2 * l + 1, t)
                for q in range(TILES):
                    mm = three(bank[7][:, experts * q:experts * q + experts],
                               lambda h: xT[:, h, P * q:P * q + P],
                               lambda h: RW[:, h, ROUTER_AT[l]:ROUTER_AT[l] + experts], start=(q == 0))
                mm.then_inc(s["logits"], 1)
                if l < 3:
                    pe.wait_ge(s["k_lo"], 2 * l + 4)
                    pe.wait_ge(s["v_lo"], 4 * l + 8)

                def slice_in(u):
                    c, t = u // 2, u % 2
                    pe.wait_ge(s["split_lo"], grain_of(l, c))
                    rhs = lambda h: xT[:, h, HALF * t:HALF * t + HALF]
                    if l == 3:
                        if u >= 4:
                            pe.wait_ge(s["hl_done"], at + u - 3)
                        three(bank[u % 4][:, :], lambda h: weight(l, c, 0, h), rhs).then_inc(s["gate_done"], 1)
                        return
                    if u >= 2:
                        pe.wait_ge(s["silu_done"], at + u - 1)
                    three(bank[u % 2][:, :], lambda h: weight(l, c, 0, h), rhs).then_inc(s["gate_done"], 1)
                    if u >= 2:
                        pe.wait_ge(s["h32_done"], at + u - 1)
                    three(bank[2 + u % 2][:, :], lambda h: weight(l, c, 1, h), rhs).then_inc(s["up_done"], 1)

                def slice_out(u):
                    c, t = u // 2, u % 2
                    e, k = c // PER_EXPERT[l], c % PER_EXPERT[l]
                    acc = bank[4 + 2 * (e % 2) + t]
                    if k == 0 and e >= 2:
                        pe.wait_ge(s["sum_read"], SUM_AT[l] + 2 * (e - 2) + t + 1)
                    if k == 0 and e == 1:
                        pe.wait_ge(s["comb_ready"], l + 1)
                    pe.wait_ge(s["hl_done"], at + u + 1)
                    last = k == PER_EXPERT[l] - 1
                    for q in range(4):
                        mm = three(acc[:, P * q:P * q + P], lambda h: (hh, hl)[h][:, u % 4, P * q:P * q + P],
                                   lambda h: weight(l, c, MATS[l] - 1, h), start=(k == 0 and q == 0), stop=last)
                    mm.then_inc(s["down_done"], 1)
                    if last:
                        if l in (1, 2):
                            for q in range(4):
                                tile = (4 * t + q) * P
                                mm = pe.matmul(acc[:, P * q:P * q + P], combT[:, tile:tile + P], B2[:, l - 1, :],
                                               start=False, stop=True, skip_group_check=True)
                            mm.then_inc(s["sum_done"], 1)

                for u in range(UNITS[l] + 2):
                    if u < UNITS[l]:
                        slice_in(u)
                    if l in (1, 2) and u == 1:
                        pe.wait_ge(s["comb_ready"], l + 1)
                        for q in range(TILES):
                            mm = pe.transpose(bank[6 + q // 4][0:COMB, P * (q % 4):P * (q % 4) + P],
                                              comb[:, COMB * q:COMB * q + COMB], ident[:, :])
                        mm.then_inc(s["comb_turned"], 1)
                        pe.wait_ge(s["combT_ready"], l)
                    if l == 3 and u == 1:
                        pe.wait_ge(s["counts_in"], 1)
                        pe.wait_ge(s["consts_made"], 1)
                        pe.matmul(bank[7][:, 0:64], before[:, :], mask16[:, :], start=True, stop=False,
                                  skip_group_check=True)
                        for q in range(TILES - 1):
                            mm = pe.matmul(bank[7][:, 8 * q + 8:64].rearrange("p (t e) -> p t e", e=8), ones16[:, :],
                                           bc_mid(mask16[:, 8 * q:8 * q + 8], TILES - 1 - q),
                                           start=False, stop=(q == TILES - 2), skip_group_check=True)
                        mm.then_inc(s["counts"], 1)
                    if u >= 2:
                        slice_out(u - 2)

            keys_values(0)
            for l in range(LAYERS):
                normed(2 * l)
                queries(l)
                attention(l)
                normed(2 * l + 1)
                if l < 3:
                    keys_values(l + 1)
                ffn(l)

        @block.vector
        def _(dve):
            steps = [0]

            def step(ins):
                steps[0] += 1
                ins.then_inc(s["dve_step"], 1)

            def settle():
                dve.wait_ge(s["dve_step"], steps[0])

            def link(ins):
                step(ins)
                settle()

            tt, ts, stt = dve.tensor_tensor, dve.tensor_scalar, dve.scalar_tensor_tensor

            dve.wait_ge(s["aw_hi"], 1)
            tt(AW[:, 1, :, :].rearrange("p i n -> p (i n)"), raw[:, 0:AW_COLS],
               AW[:, 0, :, :].rearrange("p i n -> p (i n)"), ALU.subtract).then_inc(s["aw_lo"], 1)
            dve.wait_ge(s["ctx_hi"], 2)
            ctx32 = raw[:, AW_COLS:AW_COLS + B * S].rearrange("p (b k) -> p b k", b=B)
            for e in range(2):
                tt(CT[:, 1, :, e, :], ctx32, CT[:, 0, :, e, :], ALU.subtract).then_inc(s["ctx_lo"], 1)
            dve.wait_ge(s["rw_hi"], 1)
            step(tt(RW[:, 1, :], rw32[:, :], RW[:, 0, :], ALU.subtract))
            dve.wait_ge(s["consts_in"], 160)
            step(dve.tensor_copy(QM[:, :], qm8[:, :]))
            link(ts(base[:, :, :], pad8[:, :, :], NEG, None, ALU.mult))
            stt(base[:, :, :], bc_mid(SXS[:, :], TILES), 0.5, base[:, :, :], ALU.mult, ALU.add
                ).then_inc(s["copied"], 1)

            def rotate(l, sem_in, count, even, swap, b0, b1, done, t):
                dve.wait_ge(s[sem_in], count)
                ra = work[:, HALF * t:HALF * t + HALF].rearrange("p (b k) -> p b k", b=8)
                rb = work[:, 1024 + HALF * t:1024 + HALF * t + HALF].rearrange("p (b k) -> p b k", b=8)
                step(stt(ra, even[:, :].rearrange("p (b k) -> p b k", b=8), cols[:, b0:b0 + 1],
                         bc_mid(rope[:, 0, :], 8), ALU.add, ALU.mult))
                link(stt(rb, swap[:, :].rearrange("p (b k) -> p b k", b=8), cols[:, b1:b1 + 1],
                         bc_mid(rope[:, 1, :], 8), ALU.add, ALU.mult))
                tt(ra, ra, rb, ALU.add).then_inc(s[done], 1)

            def keys_values(l):
                if l == 0:
                    for t in range(2):
                        rotate(l, "k_proj", t + 1, bank[t], bank[6 + t], 1, 49, "k_rot", t)
                for t in range(2):
                    dve.wait_ge(s["k_hi"], 2 * l + t + 1)
                    half = slice(HALF * t, HALF * t + HALF)
                    if l == 0:
                        tt(KT[:, 1, half], work[:, half], KT[:, 0, half], ALU.subtract).then_inc(s["k_lo"], 1)
                    else:
                        stt(KT[:, 1, half], bank[t][:, :], cols[:, 3 * l + 1:3 * l + 2], KT[:, 0, half],
                            ALU.add, ALU.subtract).then_inc(s["k_lo"], 1)
                for j in range(4):
                    dve.wait_ge(s["v_hi"], 4 * l + j + 1)
                    for e in range(2):
                        rows = slice(S * e, S * e + S)
                        src = bank[2 + j][rows, :].rearrange("p (b h e d) -> p (b h) e d", b=4, h=HP, e=2)[:, :, e, :]
                        hi, lo = (v[rows, 4 * j:4 * j + 4, :, e, 0:HD].rearrange("p b h d -> p (b h) d")
                                  for v in (VH, VL))
                        ins = tt(lo, src, hi, ALU.subtract)
                    ins.then_inc(s["v_lo"], 1)

            def stats(q):
                link(dve.bn_stats(bn[:, q, :], X[:, q, :]))
                step(dve.bn_aggr(mv[:, q, :], bn[:, q, :]))

            def normed(n, with_stats):
                for t in range(2):
                    if with_stats:
                        for q in range(4 * t, 4 * t + 4):
                            stats(q)
                    settle()
                    ts(veps[:, 4 * t:4 * t + 4], mv[:, 4 * t:4 * t + 4, 1], EPS, None, ALU.add
                       ).then_inc(s["var_ready"], 1)
                for t in range(2):
                    dve.wait_ge(s["rstd_ready"], 2 * n + t + 1)
                    if n:
                        dve.wait_ge(s["xn_turned"], 2 * n)
                    for q in range(4 * t, 4 * t + 4):
                        ins = ts(XN[:, q, :], X[:, q, :], mv[:, q, 0:1], rstd[:, q:q + 1], ALU.subtract, ALU.mult)
                    ins.then_inc(s["xn_ready"], 1)
                for t in range(2):
                    dve.wait_ge(s["xh_ready"], 2 * n + t + 1)
                    half = slice(HALF * t, HALF * t + HALF)
                    tt(xT[:, 1, half], bank[6 + t][:, :], xT[:, 0, half], ALU.subtract).then_inc(s["xl_ready"], 1)

            def queries(l):
                if l == 0:
                    dve.wait_ge(s["tanh_made"], 1)
                    for t in range(2):
                        rotate(l, "q_proj", t + 1, bank[t], bank[2 + t], 0, 48, "q_rot", t)
                for t in range(2):
                    dve.wait_ge(s["q_hi"], 2 * l + t + 1)
                    half = slice(HALF * t, HALF * t + HALF)
                    if l == 0:
                        tt(QT[:, 1, half], work[:, half], QT[:, 0, half], ALU.subtract).then_inc(s["q_lo"], 1)
                    else:
                        stt(QT[:, 1, half], bank[t][:, :], cols[:, 3 * l:3 * l + 1], QT[:, 0, half],
                            ALU.add, ALU.subtract).then_inc(s["q_lo"], 1)
                if l < 3:
                    link(stt(X[:, :, :], bc_mid(BO[:, l, :], TILES), TG[:, l:l + 1], X[:, :, :], ALU.mult, ALU.add))

            def attention(l):
                def shift(p):
                    i = TILES * l + p
                    dve.wait_ge(s["scores"], i + 1)
                    if i >= 2:
                        dve.wait_ge(s["pt_turned"], 2 * i - 2)
                    three_d = prob[p % 2].rearrange("p (h k) -> p h k", h=HEADS)
                    pairs = [(bank[2 * (p % 2) + r][:, :].rearrange("p (h k) -> p h k", h=HD),
                              three_d[:, HD * r:HD * r + HD, :], slice(HD * r, HD * r + HD)) for r in range(2)]
                    if l == 1:
                        dve.wait_ge(s["bias_ready"], p + 1)
                    for ps, dst, heads in pairs:
                        if l == 3:
                            ins = ts(dst, ps, 50.0 / SCALE, -50.0 / SCALE, ALU.min, ALU.max)
                        elif l == 1:
                            step(stt(dst, ps, SCALE / 2, BIAS[:, p % 2, heads, :], ALU.mult, ALU.add))
                        else:
                            step(dve.tensor_reduce(top[:, p % 2, heads], ps, AX_X, ALU.max))
                    if l == 1:
                        settle()
                        link(dve.tensor_reduce(top[:, p % 2, :], three_d, AX_X, ALU.max))
                        ins = tt(three_d, three_d, bc_last(top[:, p % 2, :], S), ALU.subtract)
                    elif l != 3:
                        settle()
                        for ps, dst, heads in pairs:
                            ins = tt(dst, ps, bc_last(top[:, p % 2, heads], S), ALU.subtract)
                    ins.then_inc(s["shifted"], 1)

                def normalise(p):
                    i = TILES * l + p
                    dve.wait_ge(s["pv"], i + 1)
                    o = bank[6][:, 0:HEADS * (HD + 1)].rearrange("p (h d) -> p h d", h=HEADS)
                    link(dve.reciprocal(rden[:, p % 2, :], o[:, :, HD]))
                    if l == 3:
                        link(ts(rden[:, p % 2, :], rden[:, p % 2, :], QM[:, p:p + 1], None, ALU.mult))
                    if i >= 2:
                        dve.wait_ge(s["o_turned"], i - 1)
                    tt(ON[p % 2][:, :].rearrange("p (h d) -> p h d", h=HEADS), o[:, :, 0:HD],
                       bc_last(rden[:, p % 2, :], HD), ALU.mult).then_inc(s["o_norm"], 1)

                def add_out(p):
                    i = TILES * l + p
                    dve.wait_ge(s["y_done"], i + 1)
                    stt(X[:, p, :], bank[7][:, P:2 * P], TG[:, l:l + 1], X[:, p, :], ALU.mult, ALU.add
                        ).then_inc(s["x_attn"], 1)
                    dve.wait_ge(s["x_attn"], i + 1)
                    stats(p)

                for k in range(TILES + 4):
                    if k < TILES:
                        shift(k)
                    if k >= 4:
                        add_out(k - 4)
                    if 1 <= k <= TILES:
                        i = TILES * l + k - 1
                        for g in range(2):
                            dve.wait_ge(s["pt_hi"], 2 * i + g + 1)
                            half = slice(HALF * g, HALF * g + HALF)
                            tt(PT[i % 2][1][:, half], bank[4 + g][:, :], PT[i % 2][0][:, half], ALU.subtract
                               ).then_inc(s["pt_lo"], 1)
                    if 2 <= k < TILES + 2:
                        normalise(k - 2)
                    if 3 <= k < TILES + 3:
                        i = TILES * l + k - 3
                        dve.wait_ge(s["ot_hi"], i + 1)
                        stt(OT[:, 1, :], bank[7][:, 0:P], cols[:, 3 * l + 2:3 * l + 3], OT[:, 0, :],
                            ALU.add, ALU.subtract).then_inc(s["ot_lo"], 1)

            def router(l):
                e = EXPERTS[l]
                n = TILES * e
                v3 = lambda ap, g=TILES: ap.rearrange("p (t e) -> p t e", t=g)
                T = [r[:, 0:n] for r in rt]

                def first_max(src, sel, small, small2, tmp, groups, width):
                    sm, sm2 = small[:, 0:groups], small2[:, 0:groups]
                    link(dve.tensor_reduce(sm, v3(src, groups), AX_X, ALU.max))
                    link(tt(v3(sel, groups), v3(src, groups), bc_last(sm, width), ALU.is_equal))
                    link(tt(v3(tmp, groups), v3(sel, groups), bc_mid(REV[:, HEADS - width:HEADS], groups), ALU.mult))
                    link(dve.tensor_reduce(sm2, v3(tmp, groups), AX_X, ALU.max))
                    link(tt(v3(sel, groups), v3(tmp, groups), bc_last(sm2, width), ALU.is_equal))

                def top_two(src, groups, width):
                    w = groups * width
                    first_max(src, T[3][:, 0:w], rs[0], rs[1], T[4][:, 0:w], groups, width)
                    link(stt(T[5][:, 0:w], T[3][:, 0:w], NEG, src, ALU.mult, ALU.add))
                    first_max(T[5][:, 0:w], T[6][:, 0:w], rs[2], rs[1], T[4][:, 0:w], groups, width)
                    link(tt(T[3][:, 0:w], T[3][:, 0:w], T[6][:, 0:w], ALU.add))

                dve.wait_ge(s["logits"], l + 1)
                dve.wait_ge(s["consts_made"], 1)
                if l == 3:
                    link(tt(v3(T[0]), v3(bank[7][:, 0:n]), bc_mid(RB[:, 32:40], TILES), ALU.add))
                else:
                    link(dve.tensor_copy(T[0], bank[7][:, 0:n]))
                tg = TG[:, 4 + l:5 + l]
                if l == 1:
                    dve.tensor_copy(T[1], T[0]).then_inc(s["exp_in"], 1)
                    link(tt(v3(T[2]), v3(T[0]), bc_mid(RB[:, 0:16], TILES), ALU.add))
                    top_two(T[2], TILES, e)
                    dve.wait_ge(s["exp_out"], l + 1)
                    link(ts(T[1], T[1], 1.0, None, ALU.add))
                    link(dve.reciprocal(T[0], T[1]))
                    link(tt(T[0], T[0], T[3], ALU.mult))
                    link(dve.tensor_reduce(rs[3][:, 0:TILES], v3(T[0]), AX_X, ALU.add))
                    link(ts(rs[3][:, 0:TILES], rs[3][:, 0:TILES], 1e-10, None, ALU.add))
                    link(dve.reciprocal(rs[4][:, 0:TILES], rs[3][:, 0:TILES]))
                else:
                    link(dve.tensor_reduce(rs[5][:, 0:TILES], v3(T[0]), AX_X, ALU.max))
                    tt(v3(T[1]), v3(T[0]), bc_last(rs[5][:, 0:TILES], e), ALU.subtract).then_inc(s["exp_in"], 1)
                    dve.wait_ge(s["exp_out"], l + 1)
                    link(dve.tensor_reduce(rs[3][:, 0:TILES], v3(T[1]), AX_X, ALU.add))
                    link(dve.reciprocal(rs[4][:, 0:TILES], rs[3][:, 0:TILES]))
                    link(tt(v3(T[0]), v3(T[1]), bc_last(rs[4][:, 0:TILES], e), ALU.mult))
                c3 = comb[:, 0:TILES * COMB].rearrange("p (t e) -> p t e", t=TILES)
                if l == 0:
                    top_two(T[0], TILES, e)
                    link(stt(rs[3][:, 0:TILES], rs[0][:, 0:TILES], 1e-9, rs[2][:, 0:TILES], ALU.add, ALU.add))
                    link(dve.reciprocal(rs[4][:, 0:TILES], rs[3][:, 0:TILES]))
                    link(tt(T[0], T[0], T[3], ALU.mult))
                    link(tt(v3(T[0]), v3(T[0]), bc_last(rs[4][:, 0:TILES], e), ALU.mult))
                    ts(comb[:, 0:n], T[0], tg, None, ALU.mult).then_inc(s["comb_ready"], 1)
                if l in (1, 2):
                    if l == 2:
                        link(tt(v3(T[1]), v3(T[0]), bc_mid(RB[:, 16:32], TILES), ALU.add))
                        top_two(T[1], 4 * TILES, 4)
                        link(tt(rs[6][:, :], rs[0][:, :], rs[2][:, :], ALU.add))
                        top_two(rs[6][:, :], TILES, 4)
                        link(ts(rs[7][:, :], T[3][:, 0:32], -NEG, NEG, ALU.mult, ALU.add))
                        link(tt(v3(T[1], 32), v3(T[1], 32), bc_last(rs[7][:, :], 4), ALU.add))
                        top_two(T[1], TILES, e)
                    if l == 2:
                        link(tt(c3[:, :, 1:COMB], v3(T[0]), v3(T[3]), ALU.mult))
                    else:
                        link(tt(c3[:, :, 1:COMB], v3(T[0]), bc_last(rs[4][:, 0:TILES], e), ALU.mult))
                    dve.tensor_copy(c3[:, :, 0], ones8[:, :]).then_inc(s["comb_ready"], 1)
                if l == 3:
                    top_two(T[0], TILES, e)
                    link(tt(T[0], T[0], T[3], ALU.mult))
                    ts(mask16[:, :], T[0], 0.0, None, ALU.is_gt).then_inc(s["counts_in"], 1)
                    dve.wait_ge(s["counts"], 1)
                    link(ts(T[1], bank[7][:, 0:n], float(CAPACITY), None, ALU.is_lt))
                    link(tt(T[0], T[0], T[1], ALU.mult))
                    ts(comb[:, 0:n], T[0], tg, None, ALU.mult).then_inc(s["comb_ready"], 1)

            def spread(l):
                dve.wait_ge(s["comb_turned"], l)
                step(dve.tensor_copy(combT[:, 0:HALF], bank[6][0:COMB, :]))
                dve.tensor_copy(combT[:, HALF:2 * HALF], bank[7][0:COMB, :]).then_inc(s["combT_ready"], 1)

            def ffn(l):
                at = UNIT_AT[l]
                tg = TG[:, 4 + l:5 + l]
                last_down = UNITS[l] - 1

                def product(u):
                    c, t = u // 2, u % 2
                    dve.wait_ge(s["silu_done"], at + u + 1)
                    dve.wait_ge(s["up_done"], at + u + 1)
                    if u >= 2:
                        dve.wait_ge(s["hh_done"], at + u - 1)
                        dve.wait_ge(s["hl_done"], at + u - 1)
                    if l == 0:
                        tt(h32[u % 2], bank[2 + u % 2][:, :], gated[u % 2], ALU.mult).then_inc(s["h32_done"], 1)
                        return
                    b3 = cols[:, 21 + 18 * (l - 1) + c:22 + 18 * (l - 1) + c]
                    ins = stt(h32[u % 2], bank[2 + u % 2][:, :], b3, gated[u % 2], ALU.add, ALU.mult)
                    if c:
                        link(ins)
                        j = c - 1
                        dve.wait_ge(s[f"comb_in{j % 4}"], 32 * (2 * (l - 1) + j // 4 + 1))
                        ins = tt(h32[u % 2], h32[u % 2], CB[:, j % 4, HALF * t:HALF * t + HALF], ALU.mult)
                    ins.then_inc(s["h32_done"], 1)

                def rest(u):
                    dve.wait_ge(s["hh_done"], at + u + 1)
                    if u >= 4:
                        dve.wait_ge(s["down_done"], at + u - 3)
                    if l == 3:
                        stt(hl[:, u % 4, :], bank[u % 4][:, :], 0.0, hh[:, u % 4, :], ALU.max, ALU.subtract
                            ).then_inc(s["hl_done"], 1)
                    else:
                        tt(hl[:, u % 4, :], h32[u % 2], hh[:, u % 4, :], ALU.subtract).then_inc(s["hl_done"], 1)

                def sums(u):
                    c, t = u // 2, u % 2
                    e, k = c // PER_EXPERT[l], c % PER_EXPERT[l]
                    if k < PER_EXPERT[l] - 1:
                        return
                    if l in (1, 2):
                        dve.wait_ge(s["sum_done"], 2 * (l - 1) + t + 1)
                    dve.wait_ge(s["down_done"], at + u + 1)
                    acc = bank[4 + 2 * (e % 2) + t][:, :].rearrange("p (t d) -> p t d", t=4)
                    four = X[:, 4 * t:4 * t + 4, :]
                    if l in (1, 2) or (l == 0 and e == 0):
                        settle()
                        step_ = stt(four, acc, tg, four, ALU.mult, ALU.add)
                    else:
                        col = e - 1 if l == 0 else e
                        dve.wait_ge(s["comb_ready"], l + 1)
                        dve.wait_ge(s["sum_read"], SUM_AT[l] + 2 * e + t)
                        for q in range(4):
                            cc = EXPERTS[l] * (4 * t + q) + col
                            step_ = stt(X[:, 4 * t + q, :], acc[:, q, :], comb[:, cc:cc + 1],
                                        X[:, 4 * t + q, :], ALU.mult, ALU.add)
                    step_.then_inc(s["sum_read"], 1)

                router(l)
                if l in (1, 2):
                    spread(l)
                for u in range(UNITS[l] + 4):
                    if u < UNITS[l] and l != 3:
                        product(u)
                    if 1 <= u <= UNITS[l]:
                        rest(u - 1)
                    if u >= 4:
                        sums(u - 4)
                dve.wait_ge(s["sum_read"], SUM_AT[l + 1])

            keys_values(0)
            dve.wait_ge(s["x_in"], 16)
            for l in range(LAYERS):
                normed(2 * l, True)
                queries(l)
                attention(l)
                normed(2 * l + 1, False)
                if l < 3:
                    keys_values(l + 1)
                ffn(l)


def kernel(**inputs):
    import numpy as np
    import concourse.bacc as bacc
    from concourse.bass_utils import run_bass_kernel_spmd

    v = {k: np.asarray(x) for k, x in inputs.items()}
    zero = np.zeros(P, np.float32)
    swap = np.arange(P) ^ 1

    names = [("L0_xattn_Wq", "L0_xattn_Wk", "L0_xattn_Wv", "L0_xattn_Wo"),
             ("L1_xattn_Wq", "L1_xattn_Wk", "L1_xattn_Wv", "L1_xattn_Wo"),
             ("L2_xattn_W_q", "L2_xattn_W_k", "L2_xattn_W_v", "L2_xattn_W_o"),
             ("L3_xattn_W_q", "L3_xattn_W_k", "L3_xattn_W_v", "L3_xattn_W_o")]
    mats = [v[n].T for layer in names for n in layer]
    mats += [v["L0_xattn_Wq"][swap].T, v["L0_xattn_Wk"][swap].T]
    attn_w = np.stack(mats, 1).reshape(P, AW_COLS)

    columns = [v["L0_xattn_bq"], v["L0_xattn_bk"], v["L0_xattn_bv"],
               v["L1_xattn_bq"], v["L1_xattn_bk"], v["L1_xattn_bv"],
               v["L2_xattn_b_q"], v["L2_xattn_b_k"], v["L2_xattn_b_v"],
               zero, zero, zero]
    layer1 = [v["L1_ffn_sb1"]] + list(v["L1_ffn_b1"].reshape(8, P)) + [v["L1_ffn_sb3"]] + list(v["L1_ffn_b3"].reshape(8, P))
    layer2 = [v["L2_ffn_bs1"]] + list(v["L2_ffn_be1"].reshape(8, P)) + [v["L2_ffn_bs3"]] + list(v["L2_ffn_be3"].reshape(8, P))
    columns = columns + layer1 + layer2 + [v["L0_xattn_bq"][swap], v["L0_xattn_bk"][swap]]

    freq = 1.0 / 10000.0 ** (np.arange(0, HD, 2, dtype=np.float32) / HD)
    angle = np.repeat(freq, 2)[:, None].astype(np.float32) * np.arange(S, dtype=np.float32)[None, :]
    sign = np.where(np.arange(HD) % 2 == 0, -1.0, 1.0)[:, None]
    rope = np.stack([np.tile(np.cos(angle), (HEADS, 1)), np.tile(np.sin(angle) * sign, (HEADS, 1))], 1)

    def slices(*ms):
        return np.stack(ms, 2).reshape(P, -1)

    def wide(m):
        return m.reshape(P, -1, P)

    def tall(m):
        return m.reshape(-1, P, P).transpose(1, 0, 2)

    def hidden(first, rest, flip):
        parts = ([first] if first is not None else []) + list(rest)
        return [p.T for p in parts] if flip else parts

    f = v
    ffn0 = slices(
        wide(np.concatenate(hidden(f["L0_ffn_shared_gate"], f["L0_ffn_routed_gate"], True), 1)),
        wide(np.concatenate(hidden(f["L0_ffn_shared_up"], f["L0_ffn_routed_up"], True), 1)),
        tall(np.concatenate(hidden(f["L0_ffn_shared_down"], f["L0_ffn_routed_down"], True), 0)))
    ffn1 = slices(
        wide(np.concatenate(hidden(f["L1_ffn_sw1"], f["L1_ffn_w1"], True), 1)),
        wide(np.concatenate(hidden(f["L1_ffn_sw3"], f["L1_ffn_w3"], True), 1)),
        tall(np.concatenate(hidden(f["L1_ffn_sw2"], f["L1_ffn_w2"], True), 0)))
    ffn2 = slices(
        wide(np.concatenate(hidden(f["L2_ffn_ws1"], f["L2_ffn_We1"], False), 1)),
        wide(np.concatenate(hidden(f["L2_ffn_ws3"], f["L2_ffn_We3"], False), 1)),
        tall(np.concatenate(hidden(f["L2_ffn_ws2"], f["L2_ffn_We2"], False), 0)))
    ffn3 = slices(
        wide(np.concatenate(hidden(None, f["L3_ffn_experts_inter"], False), 1)),
        tall(np.concatenate(hidden(None, f["L3_ffn_experts_out"], False), 0)))

    b2 = np.stack([np.concatenate([v["L1_ffn_sb2"][None], v["L1_ffn_b2"]]),
                   np.concatenate([v["L2_ffn_bs2"][None], v["L2_ffn_be2"]])], 1)
    fside = v["fside_Bx16xSxS2_0"].transpose(0, 2, 1, 3).reshape(TILES, P, HEADS * S)
    arrays = {
        "x": v["x"].reshape(B * S, D), "ctxT": v["ctx_1024"].reshape(B * S, D).T, "attn_w": attn_w,
        "ffn_w0": ffn0, "ffn_w1": ffn1, "ffn_w2": ffn2, "ffn_w3": ffn3,
        "router_w": np.concatenate([v["L0_ffn_router_w"].T, v["L1_ffn_gate_w"].T, v["L2_ffn_gate_w"].T,
                                    v["L3_ffn_W_router"].T], 1),
        "router_b": np.concatenate([v["L1_ffn_expert_bias"], v["L2_ffn_gate_b"], v["L3_ffn_b_router"]]),
        "cols": np.stack(columns, 1), "rope": rope.astype(np.float32),
        "bo": np.stack([v["L0_xattn_bo"], v["L1_xattn_bo"], v["L2_xattn_b_o"], zero]),
        "gates": np.concatenate([v["g_xattn"], v["g_ffn"]]),
        "sxs": np.concatenate([v["fside_SxS2_0"]] * 2),
        "pad": v["mask_BxS2_bf0"].reshape(TILES, 2, S).transpose(1, 0, 2),
        "qmask": v["mask_BxS_bf1"].reshape(TILES, P).T, "b2": b2, "fside": fside,
    }
    arrays = {k: np.ascontiguousarray(x) for k, x in arrays.items()}
    nc = bacc.Bacc("TRN2", target_bir_lowering=False, num_devices=1)
    aps = {k: nc.dram_tensor(f"in_{k}", x.shape, mybir.dt.from_np(x.dtype), kind="ExternalInput").ap()
           for k, x in arrays.items()}
    aps["out"] = nc.dram_tensor("out_x", (B * S, D), F32, kind="ExternalOutput").ap()
    build(nc, aps)
    r = run_bass_kernel_spmd(nc, [{f"in_{k}": x for k, x in arrays.items()}], core_ids=[0])
    return r.results[0]["out_x"].reshape(B, S, D)
```

```python
from contextlib import ExitStack

import concourse.bass as bass
from concourse import mybir

ALU = mybir.AluOpType
ACT = mybir.ActivationFunctionType
AX_X = mybir.AxisListType.X
F32 = mybir.dt.float32
F16 = mybir.dt.float16
U8 = mybir.dt.uint8

P = 128
B, S, D = 16, 64, 128
HEADS, HD = 16, 8
LAYERS = 4
TILES = B * S // P
HALF = 512
HP = HEADS // 2
SCALE = HD ** -0.5
EPS = 1e-5
NEG = -1e30
CAPACITY = 160

EXPERTS = [7, 16, 16, 8]
ROUTER_AT = [0, 7, 23, 39]
CHUNKS = [32, 9, 9, 32]
PER_EXPERT = [4, 9, 9, 4]
MATS = [3, 3, 3, 2]
UNITS = [2 * c for c in CHUNKS]
UNIT_AT = [sum(UNITS[:l]) for l in range(LAYERS + 1)]
FFN_COLS = [CHUNKS[l] * MATS[l] * P for l in range(LAYERS)]
GRAIN = 768
AW_COLS = 18 * P
AW_FIRST = 6 * P
COMB = 17
SUMS = [16, 2, 2, 16]
LAST_FIRST = [59, 16, 16, 59]
TURN_AT = [2, 1, 1, 3]
KV_AT = [24, 4, 4]
COUNT_AT = 12
ROUTER_FIRST = 6
SUM_AT = [sum(SUMS[:l]) for l in range(LAYERS + 1)]

GRAINS = []
for _l in range(LAYERS):
    for _c in range(0, FFN_COLS[_l], GRAIN):
        GRAINS.append((_l, _c, min(GRAIN, FFN_COLS[_l] - _c)))
GRAIN_AT = [next(n for n, g in enumerate(GRAINS) if g[0] == l) for l in range(LAYERS)]
SPLIT_AT = [[range(2 * p, 2 * p + 2) for p in range(TILES)],
            [range(GRAIN_AT[1] + p, min(GRAIN_AT[1] + p + 1, GRAIN_AT[2])) for p in range(TILES)],
            [range(GRAIN_AT[2] + 2 * p, min(GRAIN_AT[2] + 2 * p + 2, len(GRAINS))) for p in range(TILES)],
            [range(0)] * TILES]
assert [n for layer in SPLIT_AT for r in layer for n in r] == list(range(len(GRAINS)))


def unit(l, u):
    if l in (0, 3):
        k = PER_EXPERT[l]
        e, t, place = u // (2 * k), u // k % 2, u % k
        return k * e + place, t, e, place
    return u // 2, u % 2, 0, u // 2


def mat(l, m):
    return m if l == 0 else 2 + 4 * l + m


def bc_last(ap, n):
    return ap.unsqueeze(len(ap.shape)).broadcast_to(list(ap.shape) + [n])


def bc_mid(ap, n):
    return ap.unsqueeze(1).broadcast_to([ap.shape[0], n, ap.shape[1]])


def build(nc, a):
    ctx = ExitStack()
    with ctx:
        def sb(name, shape, dt=F32):
            return ctx.enter_context(nc.sbuf_tensor(name, shape, dt))

        def sem(name):
            return ctx.enter_context(nc.semaphore(name))

        bank = [ctx.enter_context(nc.psum_tensor(f"bank{i}", [P, 512], F32)) for i in range(8)]

        X = sb("X", [P, TILES, D])
        XN = sb("XN", [P, TILES // 2, D])
        xT = sb("xT", [P, 2, B * S], F16)
        QZ = sb("QZ", [P, 2, 2, B * S], F16)
        KT = sb("KT", [P, 2, B * S], F16)
        KM = sb("KM", [P, 2, HD, B * S], F16)
        VH = sb("VH", [P, B, HP, 2, HD + 1], F16)
        VL = sb("VL", [P, B, HP, 2, HD + 1], F16)
        CT = sb("CT", [P, 2, B, 2, S], F16)
        AW = sb("AW", [P, 2, 18, P], F16)
        WA = sb("WA", [P, 2, FFN_COLS[0]], F16)
        WB = sb("WB", [P, 2, FFN_COLS[1]], F16)
        stage = sb("stage", [P, 2, GRAIN])
        CB = sb("CB", [P, 4, B * S])
        work = sb("work", [P, 4096])
        ident = sb("ident", [P, P])
        before = sb("before", [P, P], F16)
        ones16 = sb("ones16", [P, P], F16)
        ones8 = sb("ones8", [P, TILES])
        expo = sb("expo", [P, TILES])
        cols = sb("cols", [P, 50])
        rope = sb("rope", [P, 2, S])
        BO = sb("BO", [P, LAYERS, D])
        TG = sb("TG", [P, 8])
        RW = sb("RW", [P, 2, 47], F16)
        rw32 = sb("rw32", [P, 47])
        RB = sb("RB", [P, 40])
        SXS = sb("SXS", [P, S])
        base = sb("base", [P, TILES, S])
        pad8 = sb("pad8", [P, TILES, S], U8)
        qm8 = sb("qm8", [P, TILES], U8)
        QM = sb("QM", [P, TILES])
        B2 = sb("B2", [COMB, 2, D])
        REV = sb("REV", [P, HEADS])
        bn = sb("bn", [P, TILES, 6])
        mv = sb("mv", [P, TILES, 2])
        veps = sb("veps", [P, TILES])
        rstd = sb("rstd", [P, TILES])
        top = sb("top", [P, 2, HEADS])
        rden = sb("rden", [P, 2, HEADS])
        ON = [sb(f"ON{i}", [P, D]) for i in range(2)]
        OT = sb("OT", [P, 2, P], F16)
        rt = [sb(f"rt{i}", [P, TILES * 16]) for i in range(8)]
        rs = [sb(f"rs{i}", [P, 32]) for i in range(8)]
        mask16 = sb("mask16", [P, TILES * 8], F16)
        spare = sb("spare", [P, 1])
        comb = sb("comb", [P, TILES * COMB])
        combT = sb("combT", [COMB, B * S])

        BIAS = CB[:, 0:2, :].rearrange("p i (h k) -> p i h k", h=HEADS)
        prob = [work[:, 0:1024], work[:, 1024:2048]]
        PT = [[work[:, at:at + 512].bitcast(F16) for at in (lo, lo + 512)] for lo in (2048, 3072)]
        gated = [work[:, 0:512], work[:, 512:1024]]
        h32 = [work[:, 1024:1536], work[:, 1536:2048]]
        hh = work[:, 2048:3072].bitcast(F16).rearrange("p (s n) -> p s n", s=4)
        hl = work[:, 3072:4096].bitcast(F16).rearrange("p (s n) -> p s n", s=4)
        raw = WB[:, :, :].rearrange("p a n -> p (a n)").bitcast(F32)

        comb_dram = nc.dram_tensor("comb_scratch", [2, COMB, B * S], F32, kind="Internal").ap()

        names = """first_in consts_in rw_in aw0_in aw_in ctx_in x_in fside_in0 fside_in1 stage_in0 stage_in1 km_in km_zero
        comb_out comb_in0 comb_in1 comb_in2 comb_in3 out_done
        ident_made consts_made tanh_made table_used q_zero aw_hi aw_lo ctx_hi ctx_lo rw_hi rw_lo
        dve_step pool_step split_hi split_lo bias_ready
        var_ready rstd_ready xn_ready xn_turned xh_ready xl_ready
        k_proj k_rot k_hi k_lo v_proj v_hi v_lo q_proj q_rot q_hi q_lo
        scores maxima shifted shifted_last probs pt_turned pt_hi pt_lo pv o_norm o_turned ot_hi ot_lo y_done x_attn
        logits copied exp_in exp_out counts_in counts comb_ready comb_turned combT_ready
        gate_done up_done silu_done h32_done hh_done hl_done down_done sum_done sum_read x_out""".split()
        s = {n: sem(n) for n in names}

        def aw(i, hl):
            return AW[:, hl, i, :]

        def weight(l, chunk, m, hl):
            at = (chunk * MATS[l] + m) * P
            return (WA if l in (0, 3) else WB)[:, hl, at:at + P]

        def grain_of(l, chunk):
            return GRAIN_AT[l] + ((chunk + 1) * MATS[l] * P - 1) // GRAIN + 1

        def turn_bank(n, t):
            return bank[0 if n % 2 and t == 0 else 6 + t]

        def acc_bank(l, e, t):
            return bank[4 + t + (2 * (e % 2) if l == 3 else 0)]

        CONTEXT = [("k", 0), ("k", 1), ("v", 0), ("v", 1), ("v", 2), ("v", 3)]

        def context_bank(l, i):
            if l:
                return bank[6 + i % 2]
            return bank[i]

        def query_bank(l, t):
            return bank[t] if l == 0 else bank[4 + 2 * t]

        block = ctx.enter_context(nc.Block())

        @block.sync
        def _(sp):
            sp.dma_start(X[:, :, :], a["x"].rearrange("(t p) d -> p t d", p=P)).then_inc(s["x_in"], 16)
            sp.dma_start(raw[:, 0:AW_FIRST], a["attn_w"][:, 0:AW_FIRST]).then_inc(s["aw0_in"], 16)
            sp.dma_start(raw[:, AW_COLS:AW_COLS + B * S], a["ctxT"]).then_inc(s["ctx_in"], 16)
            for dst, src in ((cols[:, :], a["cols"]), (rope[:, :, :], a["rope"]),
                             (TG[:, :], a["gates"].partition_broadcast(P))):
                sp.dma_start(dst, src).then_inc(s["first_in"], 16)
            sp.dma_start(raw[:, AW_FIRST:AW_COLS], a["attn_w"][:, AW_FIRST:AW_COLS]).then_inc(s["aw_in"], 16)
            sp.dma_start(rw32[:, :], a["router_w"]).then_inc(s["rw_in"], 16)
            for dst, src in (
                (BO[:, :, :], a["bo"].partition_broadcast(P)),
                (RB[:, :], a["router_b"].partition_broadcast(P)), (SXS[:, :], a["sxs"]),
                (pad8[0:S, :, :], a["pad"][0].partition_broadcast(S)),
                (pad8[S:P, :, :], a["pad"][1].partition_broadcast(S)),
                (qm8[:, :], a["qmask"]), (B2[:, :, :], a["b2"]),
            ):
                sp.dma_start(dst, src).then_inc(s["consts_in"], 16)

            def load_grain(n):
                l, c, w = GRAINS[n]
                if n >= 2:
                    sp.wait_ge(s["split_lo"], n - 1)
                sp.dma_start(stage[:, n % 2, 0:w], a[f"ffn_w{l}"][:, c:c + w]).then_inc(s[f"stage_in{n % 2}"], 16)

            def place_keys(l):
                sp.wait_ge(s["k_lo"], 2 * l + 2)
                if l == 0:
                    sp.wait_ge(s["km_zero"], 2)
                else:
                    sp.wait_ge(s["scores"], TILES * l)
                for j in range(HD):
                    for r in (0, S):
                        lo = r + HD * j
                        sp.dma_start(KM[lo:lo + HD, :, j, :], KT[lo:lo + HD, :, :]).then_inc(s["km_in"], 16)

            def load_fside(p):
                if p >= 2:
                    sp.wait_ge(s["shifted"], TILES + p - 1)
                sp.dma_start(BIAS[:, p % 2, :, :].rearrange("p h k -> p (h k)"),
                             a["fside"][p]).then_inc(s[f"fside_in{p % 2}"], 16)

            def spread_comb(l):
                sp.wait_ge(s["combT_ready"], l)
                sp.dma_start(comb_dram[l - 1], combT[:, :]).then_inc(s["comb_out"], 16)
                sp.wait_ge(s["comb_out"], 16 * l)
                for j in range(8):
                    if j >= 4:
                        sp.wait_ge(s["h32_done"], UNIT_AT[l] + 2 * (j - 4 + 1) + 2)
                    for e in range(2):
                        sp.dma_start(CB[S * e:S * e + S, j % 4, :],
                                     comb_dram[l - 1, 1 + 2 * j + e].partition_broadcast(S)
                                     ).then_inc(s[f"comb_in{j % 4}"], 16)

            for n in range(2):
                load_grain(n)
            place_keys(0)
            for n in range(2, GRAIN_AT[1]):
                load_grain(n)
            load_fside(0)
            load_fside(1)
            place_keys(1)
            for n in range(GRAIN_AT[1], GRAIN_AT[1] + 2):
                load_grain(n)
            for p in range(2, TILES):
                load_fside(p)
                if GRAIN_AT[1] + p < GRAIN_AT[2] + 2:
                    load_grain(GRAIN_AT[1] + p)
            spread_comb(1)
            place_keys(2)
            for n in range(GRAIN_AT[2] + 2, len(GRAINS)):
                load_grain(n)
            spread_comb(2)
            place_keys(3)
            for t in range(2):
                sp.wait_ge(s["sum_read"], SUM_AT[4] - 1 + t)
                sp.dma_start(a["out"].rearrange("(t p) d -> p t d", p=P)[:, 4 * t:4 * t + 4, :],
                             X[:, 4 * t:4 * t + 4, :]).then_inc(s["out_done"], 16)
            sp.wait_ge(s["out_done"], 32)

        @block.gpsimd
        def _(pool):
            steps = [0]

            def step(ins):
                steps[0] += 1
                ins.then_inc(s["pool_step"], 1)

            def settle():
                pool.wait_ge(s["pool_step"], steps[0])

            def link(ins):
                step(ins)
                settle()

            link(pool.memset(ident[:, :], 0.0))
            link(pool.memset(before[:, :], 1.0))
            link(pool.memset(expo[:, :], -0.5))
            pool.affine_select(out=ident[:, :], in_=ident[:, :], compare_op=ALU.not_equal, fill=1.0, base=0,
                               pattern=[[-1, P]], channel_multiplier=1).then_inc(s["ident_made"], 1)
            pool.wait_ge(s["ident_made"], 1)

            def powers(n, t):
                pool.wait_ge(s["var_ready"], 2 * n + t + 1)
                pool.tensor_tensor(rstd[:, 4 * t:4 * t + 4], veps[:, 4 * t:4 * t + 4],
                                   expo[:, 4 * t:4 * t + 4], ALU.pow).then_inc(s["rstd_ready"], 1)
                pool.wait_ge(s["rstd_ready"], 2 * n + t + 1)

            powers(0, 0)
            powers(0, 1)
            pool.memset(QZ[:, :, :, :].rearrange("p r h n -> p (r h n)").bitcast(F32), 0.0).then_inc(s["q_zero"], 1)
            pool.wait_ge(s["q_zero"], 1)
            for hl_ in range(2):
                pool.memset(KM[:, hl_, :, :].rearrange("p j n -> p (j n)").bitcast(F32), 0.0
                            ).then_inc(s["km_zero"], 1)
                pool.wait_ge(s["km_zero"], hl_ + 1)
            for v in (VH, VL):
                link(pool.memset(v[:, :, :, :, :].rearrange("p b h e d -> p (b h e d)"), 0.0))
            for e in range(2):
                link(pool.memset(VH[S * e:S * e + S, :, :, e, HD], 1.0))
            link(pool.affine_select(out=before[:, :], in_=before[:, :], compare_op=ALU.is_gt, fill=0.0, base=0,
                                    pattern=[[1, P]], channel_multiplier=-1))
            link(pool.memset(ones16[:, :], 1.0))
            link(pool.memset(ones8[:, :], 1.0))
            for j in range(HEADS):
                link(pool.memset(REV[:, j:j + 1], float(HEADS - j)))
            pool.memset(REV[:, 0:1], float(HEADS)).then_inc(s["consts_made"], 1)
            pool.wait_ge(s["consts_made"], 1)

            def low_grain(n):
                l, c, w = GRAINS[n]
                dst = WA if l in (0, 3) else WB
                pool.wait_ge(s["split_hi"], n + 1)
                pool.tensor_tensor(dst[:, 1, c:c + w], stage[:, n % 2, 0:w], dst[:, 0, c:c + w],
                                   ALU.subtract).then_inc(s["split_lo"], 1)
                pool.wait_ge(s["split_lo"], n + 1)

            def low_halves(l):
                at = UNIT_AT[l]
                for u in range(UNITS[l]):
                    pool.wait_ge(s["hh_done"], at + u + 1)
                    if u >= 4:
                        pool.wait_ge(s["down_done"], at + u - 3)
                    pool.tensor_tensor(hl[:, u % 4, :], h32[u % 2], hh[:, u % 4, :], ALU.subtract
                                       ).then_inc(s["hl_done"], 1)
                    pool.wait_ge(s["hl_done"], at + u + 1)

            def shift(p):
                pool.wait_ge(s["maxima"], p + 1)
                dst = prob[p % 2][:, HALF:2 * HALF].rearrange("p (h k) -> p h k", h=HD)
                pool.tensor_tensor(dst, dst, bc_last(top[:, p % 2, HD:2 * HD], S), ALU.subtract
                                   ).then_inc(s["shifted_last"], 1)
                pool.wait_ge(s["shifted_last"], p + 1)

            def add_bias(p):
                pool.wait_ge(s[f"fside_in{p % 2}"], 16 * (p // 2 + 1))
                if p == 0:
                    pool.wait_ge(s["copied"], 1)
                if p >= 2:
                    pool.wait_ge(s["shifted"], TILES + p - 1)
                pool.tensor_tensor(BIAS[:, p % 2, :, :], BIAS[:, p % 2, :, :], bc_mid(base[:, p, :], HEADS),
                                   ALU.add).then_inc(s["bias_ready"], 1)
                pool.wait_ge(s["bias_ready"], p + 1)

            for l in range(LAYERS):
                if l:
                    powers(2 * l, 0)
                    powers(2 * l, 1)
                for p in range(TILES):
                    if l == 1 and p == 0:
                        add_bias(0)
                    if l == 1:
                        shift(p)
                    if l == 1 and p + 1 < TILES:
                        add_bias(p + 1)
                    if p == TILES - 1:
                        powers(2 * l + 1, 0)
                    for n in SPLIT_AT[l][p]:
                        low_grain(n)
                powers(2 * l + 1, 1)
                if l in (1, 2):
                    low_halves(l)

        @block.scalar
        def _(act):
            def split_weights(lo, hi, arrived):
                act.wait_ge(s[arrived], 16)
                act.activation(AW[:, 0, lo:hi, :].rearrange("p i n -> p (i n)"), raw[:, P * lo:P * hi], ACT.Copy
                               ).then_inc(s["aw_hi"], 1)

            def keys(l, t):
                dst = KT[:, 0, HALF * t:HALF * t + HALF]
                if t == 0 and l:
                    act.wait_ge(s["km_in"], 256 * l)
                if l == 0:
                    act.wait_ge(s["k_rot"], t + 1)
                    act.activation(dst, work[:, HALF * t:HALF * t + HALF], ACT.Copy).then_inc(s["k_hi"], 1)
                else:
                    act.wait_ge(s["k_proj"], 2 * l + t + 1)
                    act.activation(dst, context_bank(l, t)[:, :], ACT.Identity, bias=cols[:, 3 * l + 1:3 * l + 2]
                                   ).then_inc(s["k_hi"], 1)

            def values(l, j):
                if l == 0:
                    act.wait_ge(s["consts_made"], 1)
                else:
                    act.wait_ge(s["pv"], TILES * l)
                act.wait_ge(s["v_proj"], 4 * l + j + 1)
                for e in range(2):
                    rows = slice(S * e, S * e + S)
                    src = context_bank(l, 2 + j)[rows, :].rearrange("p (b h e d) -> p (b h) e d", b=4, h=HP, e=2)
                    dst = VH[rows, 4 * j:4 * j + 4, :, e, 0:HD].rearrange("p b h d -> p (b h) d")
                    ins = act.activation(dst, src[:, :, e, :], ACT.Copy)
                ins.then_inc(s["v_hi"], 1)

            def context(l, i):
                kind, part = CONTEXT[i]
                (keys if kind == "k" else values)(l, part)

            tables = [0]

            def load_table(kind):
                if tables[0]:
                    act.wait_ge(s["table_used"], tables[0])
                else:
                    act.wait_ge(s["consts_made"], 1)
                act.activation(spare[:, :], ones8[:, 0:1], kind).then_inc(s["table_used"], 1)
                tables[0] += 1

            def turned(n, t):
                act.wait_ge(s["xn_turned"], 2 * n + t + 1)
                act.activation(xT[:, 0, HALF * t:HALF * t + HALF], turn_bank(n, t)[:, :], ACT.Copy
                               ).then_inc(s["xh_ready"], 1)

            def queries(l, t):
                if l == 0:
                    act.wait_ge(s["q_zero"], 1)
                    act.wait_ge(s["q_rot"], t + 1)
                else:
                    act.wait_ge(s["q_proj"], 2 * l + t + 1)
                    if t == 0:
                        act.wait_ge(s["scores"], TILES * l)
                for r in range(2):
                    rows = slice(S * r, S * r + S)
                    dst = QZ[rows, r, 0, HALF * t:HALF * t + HALF]
                    if l == 0:
                        ins = act.activation(dst, work[rows, HALF * t:HALF * t + HALF], ACT.Copy)
                    else:
                        ins = act.activation(dst, query_bank(l, t)[rows, :], ACT.Identity, bias=cols[rows, 3 * l:3 * l + 1])
                ins.then_inc(s["q_hi"], 1)

            def high_grain(n):
                l, c, w = GRAINS[n]
                act.wait_ge(s[f"stage_in{n % 2}"], 16 * (n // 2 + 1))
                if n == GRAIN_AT[1]:
                    act.wait_ge(s["aw_lo"], 2)
                    act.wait_ge(s["ctx_lo"], 2)
                if n == GRAIN_AT[2]:
                    act.wait_ge(s["down_done"], UNIT_AT[2])
                if n == GRAIN_AT[3]:
                    act.wait_ge(s["down_done"], UNIT_AT[1])
                act.activation((WA if l in (0, 3) else WB)[:, 0, c:c + w], stage[:, n % 2, 0:w], ACT.Copy
                               ).then_inc(s["split_hi"], 1)

            def attention(l):
                exp_scale = 2.0 if l == 1 else SCALE
                for k in range(TILES + 4):
                    if l and k == 0:
                        turned(2 * l, 1)
                    if 1 <= k <= TILES:
                        i = TILES * l + k - 1
                        for g in range(2):
                            act.wait_ge(s["pt_turned"], 2 * i + g + 1)
                            if i >= 2:
                                act.wait_ge(s["pv"], i - 1)
                            act.activation(PT[i % 2][0][:, HALF * g:HALF * g + HALF], bank[4 + g][:, :], ACT.Copy
                                           ).then_inc(s["pt_hi"], 1)
                    if l and k == 1:
                        queries(l, 1)
                    if 3 <= k < TILES + 3:
                        i = TILES * l + k - 3
                        act.wait_ge(s["o_turned"], i + 1)
                        act.wait_ge(s["y_done"], i)
                        act.activation(OT[:, 0, :], bank[7][:, 0:P], ACT.Identity, bias=cols[:, 3 * l + 2:3 * l + 3]
                                       ).then_inc(s["ot_hi"], 1)
                    if k < TILES:
                        i = TILES * l + k
                        act.wait_ge(s["shifted"], i + 1)
                        if l == 1:
                            act.wait_ge(s["shifted_last"], k + 1)
                        act.activation(prob[k % 2], prob[k % 2], ACT.Exp, scale=exp_scale).then_inc(s["probs"], 1)
                    if k < TILES:
                        for n in SPLIT_AT[l][k]:
                            high_grain(n)
                    if k == TILES:
                        turned(2 * l + 1, 0)
                    if l == 0 and k == TILES + 1:
                        load_table(ACT.Silu)

            def ffn(l):
                at = UNIT_AT[l]

                def exponent():
                    act.wait_ge(s["exp_in"], l + 1)
                    act.activation(rt[1][:, 0:TILES * EXPERTS[l]], rt[1][:, 0:TILES * EXPERTS[l]], ACT.Exp,
                                   scale=-1.0 if l == 1 else 1.0).then_inc(s["exp_out"], 1)

                if l in (1, 2):
                    turned(2 * l + 1, 1)
                    exponent()
                for u in range(UNITS[l] + 1):
                    if l == 3 and u < UNITS[l]:
                        act.wait_ge(s["gate_done"], at + u + 1)
                        if u >= 4:
                            act.wait_ge(s["down_done"], at + u - 3)
                        act.activation(hh[:, u % 4, :], bank[u % 4][:, :], ACT.Relu).then_inc(s["hh_done"], 1)
                    if l < 3 and u < UNITS[l]:
                        c = unit(l, u)[0]
                        act.wait_ge(s["gate_done"], at + u + 1)
                        if u >= 2:
                            act.wait_ge(s["h32_done"], at + u - 1)
                        kind = {"bias": cols[:, 12 + 18 * (l - 1) + c:13 + 18 * (l - 1) + c]} if l else {}
                        act.activation(gated[u % 2], bank[u % 2][:, :], ACT.Silu, **kind).then_inc(s["silu_done"], 1)
                    if l < 3 and u >= 1:
                        v = u - 1
                        act.wait_ge(s["h32_done"], at + v + 1)
                        if v >= 4:
                            act.wait_ge(s["down_done"], at + v - 3)
                        act.activation(hh[:, v % 4, :], h32[v % 2], ACT.Copy).then_inc(s["hh_done"], 1)
                    if l in (0, 3) and u == TURN_AT[l]:
                        turned(2 * l + 1, 1)
                    if l in (0, 3) and u == ROUTER_FIRST:
                        exponent()
                    if l < 3 and KV_AT[l] <= u < KV_AT[l] + len(CONTEXT):
                        context(l + 1, u - KV_AT[l])

            split_weights(0, 6, "aw0_in")
            act.wait_ge(s["ctx_in"], 16)
            ctx32 = raw[:, AW_COLS:AW_COLS + B * S].rearrange("p (b k) -> p b k", b=B)
            for e in range(2):
                act.activation(CT[:, 0, :, e, :], ctx32, ACT.Copy).then_inc(s["ctx_hi"], 1)
            turned(0, 0)
            turned(0, 1)
            act.wait_ge(s["first_in"], 48)
            act.activation(TG[:, :], TG[:, :], ACT.Tanh).then_inc(s["tanh_made"], 1)
            for i in range(len(CONTEXT)):
                context(0, i)
            queries(0, 0)
            queries(0, 1)
            split_weights(6, 18, "aw_in")
            act.wait_ge(s["rw_in"], 16)
            act.activation(RW[:, 0, :], rw32[:, :], ACT.Copy).then_inc(s["rw_hi"], 1)
            for l in range(LAYERS):
                if l:
                    turned(2 * l, 0)
                    queries(l, 0)
                load_table(ACT.Exp)
                attention(l)
                ffn(l)

        @block.tensor
        def _(pe):
            def three(out, lhsT, rhs, start=True, stop=True):
                pe.matmul(out, lhsT(0), rhs(0), start=start, stop=False, skip_group_check=True)
                pe.matmul(out, lhsT(1), rhs(0), start=False, stop=False, skip_group_check=True)
                return pe.matmul(out, lhsT(0), rhs(1), start=False, stop=stop, skip_group_check=True)

            def project(out, w, src, t):
                return three(out, lambda h: aw(w, h), lambda h: src(h)[:, HALF * t:HALF * t + HALF] if src else
                             CT[:, h, 8 * t:8 * t + 8, 0, :])

            def keys(l, t):
                mm = project(context_bank(l, t)[:, :].rearrange("p (b k) -> p b k", b=8), mat(l, 1), None, t)
                if l == 0:
                    mm = project(bank[6 + t][:, :].rearrange("p (b k) -> p b k", b=8), mat(0, 5), None, t)
                mm.then_inc(s["k_proj"], 1)

            def values(l, j):
                for b in range(4):
                    mm = three(context_bank(l, 2 + j)[:, P * b:P * b + P],
                               lambda h: CT[:, h, 4 * j + b, :, :].rearrange("p e k -> p (e k)"),
                               lambda h: aw(mat(l, 2), h), start=(b == 0))
                mm.then_inc(s["v_proj"], 1)

            def context(l, i):
                kind, part = CONTEXT[i]
                if l == 0 and i == 0:
                    pe.wait_ge(s["aw_lo"], 1)
                    pe.wait_ge(s["ctx_lo"], 2)
                    pe.wait_ge(s["xl_ready"], 2)
                if l and i == 0:
                    pe.wait_ge(s["aw_lo"], 2)
                    pe.wait_ge(s["exp_in"], l)
                    if l > 1:
                        pe.wait_ge(s["combT_ready"], l - 1)
                if l and i >= 2:
                    last, at = CONTEXT[i - 2]
                    pe.wait_ge(s[f"{last}_lo"], (2 if last == "k" else 4) * l + at + 1)
                (keys if kind == "k" else values)(l, part)

            def turn_normed(n, t):
                if n == 0 and t == 0:
                    pe.wait_ge(s["ident_made"], 1)
                if n and n % 2 == 0 and t == 0:
                    pe.wait_ge(s["v_lo"], 2 * n + 4)
                pe.wait_ge(s["xn_ready"], 2 * n + t + 1)
                for q in range(4):
                    mm = pe.transpose(turn_bank(n, t)[:, P * q:P * q + P], XN[:, q, :], ident[:, :])
                mm.then_inc(s["xn_turned"], 1)

            def xn_split(n, t):
                pe.wait_ge(s["xh_ready"], 2 * n + t + 1)
                pe.wait_ge(s["xl_ready"], 2 * n + t + 1)

            def queries(l, t):
                xn_split(2 * l, t)
                if l == 0:
                    pe.wait_ge(s["k_rot"], t + 1)
                    pe.wait_ge(s["v_lo"], t + 1)
                mm = project(query_bank(l, t)[:, :], mat(l, 0), lambda h: xT[:, h, :], t)
                if l == 0:
                    mm = project(bank[2 + t][:, :], mat(0, 4), lambda h: xT[:, h, :], t)
                mm.then_inc(s["q_proj"], 1)

            def take_scores(l, p):
                i = TILES * l + p
                if p == 0:
                    pe.wait_ge(s["km_in"], 256 * (l + 1))
                if p % 4 == 0:
                    pe.wait_ge(s["q_hi"], 2 * l + p // 4 + 1)
                    pe.wait_ge(s["q_lo"], 2 * l + p // 4 + 1)
                if p >= 2:
                    pe.wait_ge(s["shifted"], i - 1)
                for ha, hb in ((0, 0), (1, 0), (0, 1)):
                    for r in range(2):
                        for b in range(2):
                            tok = slice(P * p + S * b, P * p + S * b + S)
                            mm = pe.matmul(bank[2 * (p % 2) + r][S * b:S * b + S, :].rearrange("p (j k) -> p j k", j=HD),
                                           QZ[:, r, ha, tok], KM[:, hb, :, tok],
                                           start=(ha == 0 and hb == 0), stop=(hb == 1))
                mm.then_inc(s["scores"], 1)

            def turn_probs(l, p):
                i = TILES * l + p
                pe.wait_ge(s["probs"], i + 1)
                for g in range(2):
                    if i >= 1:
                        pe.wait_ge(s["pt_lo"], 2 * i - 1 + g)
                    for q in range(4):
                        at = (4 * g + q) * P
                        mm = pe.transpose(bank[4 + g][:, P * q:P * q + P], prob[p % 2][:, at:at + P], ident[:, :])
                    mm.then_inc(s["pt_turned"], 1)

            def weigh_values(l, p):
                i = TILES * l + p
                if p == 0:
                    pe.wait_ge(s["v_lo"], 4 * (l + 1))
                if i == 0:
                    pe.wait_ge(s["consts_made"], 1)
                if i >= 1:
                    pe.wait_ge(s["o_norm"], i)
                if p == 0:
                    pe.wait_ge(s["q_lo"], 2 * l + 2)
                for g in range(2):
                    pe.wait_ge(s["pt_hi"], 2 * i + g + 1)
                    pe.wait_ge(s["pt_lo"], 2 * i + g + 1)
                    for q in range(4 * g, 4 * g + 4):
                        for ha, v in ((0, VH), (1, VH), (0, VL)):
                            for b in range(2):
                                mm = pe.matmul(bank[6][S * b:S * b + S, 18 * q:18 * q + 18],
                                               PT[i % 2][ha][:, P * q + S * b:P * q + S * b + S],
                                               v[:, 2 * p + b, q, :, :].rearrange("p e d -> p (e d)"),
                                               start=(q == 0 and ha == 0 and v is VH), stop=(v is VL),
                                               skip_group_check=True)
                mm.then_inc(s["pv"], 1)

            def turn_out(l, p):
                i = TILES * l + p
                pe.wait_ge(s["o_norm"], i + 1)
                if i >= 1:
                    pe.wait_ge(s["x_attn"], i)
                pe.transpose(bank[7][:, 0:P], ON[p % 2][:, :], ident[:, :]).then_inc(s["o_turned"], 1)

            def project_out(l, p):
                i = TILES * l + p
                pe.wait_ge(s["ot_hi"], i + 1)
                pe.wait_ge(s["ot_lo"], i + 1)
                three(bank[7][:, P:2 * P], lambda h: OT[:, h, :], lambda h: aw(mat(l, 3), h)
                      ).then_inc(s["y_done"], 1)

            def attention(l):
                take_scores(l, 0)
                for k in range(TILES + 3):
                    if 1 <= k <= TILES:
                        turn_probs(l, k - 1)
                    if 3 <= k < TILES + 3:
                        turn_out(l, k - 3)
                    if l and k == 0:
                        turn_normed(2 * l, 1)
                    if l and k == 1:
                        queries(l, 1)
                    if k + 1 < TILES:
                        take_scores(l, k + 1)
                    if 2 <= k < TILES + 2:
                        weigh_values(l, k - 2)
                    if k == TILES:
                        pe.wait_ge(s["shifted"], TILES * (l + 1))
                        turn_normed(2 * l + 1, 0)
                    if 3 <= k < TILES + 3:
                        project_out(l, k - 3)
                    if k == TILES + (1 if l in (0, 3) else 2):
                        slice_in(l, 0)

            def slice_in(l, u):
                at = UNIT_AT[l]
                c, t = unit(l, u)[0:2]
                xn_split(2 * l + 1, t)
                pe.wait_ge(s["split_lo"], grain_of(l, c))
                rhs = lambda h: xT[:, h, HALF * t:HALF * t + HALF]
                if l == 3:
                    if u >= 4:
                        pe.wait_ge(s["hl_done"], at + u - 3)
                    three(bank[u % 4][:, :], lambda h: weight(l, c, 0, h), rhs).then_inc(s["gate_done"], 1)
                    return
                if u >= 2:
                    pe.wait_ge(s["silu_done"], at + u - 1)
                three(bank[u % 2][:, :], lambda h: weight(l, c, 0, h), rhs).then_inc(s["gate_done"], 1)
                if u >= 2:
                    pe.wait_ge(s["h32_done"], at + u - 1)
                three(bank[2 + u % 2][:, :], lambda h: weight(l, c, 1, h), rhs).then_inc(s["up_done"], 1)

            def ffn(l):
                at, experts = UNIT_AT[l], EXPERTS[l]
                def second_half():
                    pe.wait_ge(s["x_attn"], TILES * (l + 1))
                    turn_normed(2 * l + 1, 1)

                def logits():
                    xn_split(2 * l + 1, 1)
                    if l == 0:
                        pe.wait_ge(s["rw_lo"], 1)
                    for q in range(TILES):
                        mm = three(bank[7][:, experts * q:experts * q + experts],
                                   lambda h: xT[:, h, P * q:P * q + P],
                                   lambda h: RW[:, h, ROUTER_AT[l]:ROUTER_AT[l] + experts], start=(q == 0))
                    mm.then_inc(s["logits"], 1)

                def slice_out(u):
                    c, t, e, k = unit(l, u)
                    acc = acc_bank(l, e, t)
                    sets = 2 if l == 3 else 1
                    if k == 0 and e == 0:
                        pe.wait_ge(s["pt_lo"], 2 * TILES * (l + 1))
                    if k == 0 and e >= sets:
                        pe.wait_ge(s["sum_read"], SUM_AT[l] + 2 * (e - sets) + t + 1)
                    if k == 0 and e == 1 and t == 1 and l == 3:
                        pe.wait_ge(s["comb_ready"], l + 1)
                    pe.wait_ge(s["hl_done"], at + u + 1)
                    last = k == PER_EXPERT[l] - 1
                    for q in range(4):
                        mm = three(acc[:, P * q:P * q + P], lambda h: (hh, hl)[h][:, u % 4, P * q:P * q + P],
                                   lambda h: weight(l, c, MATS[l] - 1, h), start=(k == 0 and q == 0), stop=last)
                    mm.then_inc(s["down_done"], 1)
                    if last:
                        if l in (1, 2):
                            pe.wait_ge(s["combT_ready"], l)
                            for q in range(4):
                                tile = (4 * t + q) * P
                                mm = pe.matmul(acc[:, P * q:P * q + P], combT[:, tile:tile + P], B2[:, l - 1, :],
                                               start=False, stop=True, skip_group_check=True)
                            mm.then_inc(s["sum_done"], 1)

                def turn_comb():
                    pe.wait_ge(s["comb_ready"], l + 1)
                    for q in range(TILES):
                        mm = pe.transpose(bank[6 + q // 4][0:COMB, P * (q % 4):P * (q % 4) + P],
                                          comb[:, COMB * q:COMB * q + COMB], ident[:, :])
                    mm.then_inc(s["comb_turned"], 1)

                def count():
                    pe.wait_ge(s["counts_in"], 1)
                    pe.wait_ge(s["consts_made"], 1)
                    pe.matmul(bank[7][:, 0:64], before[:, :], mask16[:, :], start=True, stop=False,
                              skip_group_check=True)
                    for q in range(TILES - 1):
                        mm = pe.matmul(bank[7][:, 8 * q + 8:64].rearrange("p (t e) -> p t e", e=8), ones16[:, :],
                                       bc_mid(mask16[:, 8 * q:8 * q + 8], TILES - 1 - q),
                                       start=False, stop=(q == TILES - 2), skip_group_check=True)
                    mm.then_inc(s["counts"], 1)

                last_first = LAST_FIRST[l]
                for u in range(UNITS[l] + 2):
                    if l in (1, 2) and u == 1:
                        second_half()
                        logits()
                    if 1 <= u < UNITS[l]:
                        slice_in(l, u)
                    if l in (1, 2) and u == 1:
                        turn_comb()
                    if l in (0, 3) and u == TURN_AT[l]:
                        second_half()
                    if l in (0, 3) and u == 4:
                        logits()
                    if l == 3 and u == COUNT_AT:
                        count()
                    if u >= 2:
                        slice_out(u - 2)
                    if l < 3 and KV_AT[l] <= u < KV_AT[l] + len(CONTEXT):
                        context(l + 1, u - KV_AT[l])
                    if l == 0 and u == last_first + 5:
                        turn_normed(2, 0)
                if l in (1, 2):
                    turn_normed(2 * l + 2, 0)

            turn_normed(0, 0)
            turn_normed(0, 1)
            for i in range(len(CONTEXT)):
                context(0, i)
            for l in range(LAYERS):
                queries(l, 0)
                if l == 0:
                    queries(l, 1)
                attention(l)
                ffn(l)

        @block.vector
        def _(dve):
            steps = [0]

            def step(ins):
                steps[0] += 1
                ins.then_inc(s["dve_step"], 1)

            def settle():
                dve.wait_ge(s["dve_step"], steps[0])

            def link(ins):
                step(ins)
                settle()

            tt, ts, stt = dve.tensor_tensor, dve.tensor_scalar, dve.scalar_tensor_tensor

            def split_weights(lo, hi, n):
                dve.wait_ge(s["aw_hi"], n)
                tt(AW[:, 1, lo:hi, :].rearrange("p i n -> p (i n)"), raw[:, P * lo:P * hi],
                   AW[:, 0, lo:hi, :].rearrange("p i n -> p (i n)"), ALU.subtract).then_inc(s["aw_lo"], 1)

            def split_context():
                dve.wait_ge(s["ctx_hi"], 2)
                ctx32 = raw[:, AW_COLS:AW_COLS + B * S].rearrange("p (b k) -> p b k", b=B)
                for e in range(2):
                    tt(CT[:, 1, :, e, :], ctx32, CT[:, 0, :, e, :], ALU.subtract).then_inc(s["ctx_lo"], 1)

            def prepare():
                dve.wait_ge(s["rw_hi"], 1)
                tt(RW[:, 1, :], rw32[:, :], RW[:, 0, :], ALU.subtract).then_inc(s["rw_lo"], 1)
                dve.wait_ge(s["consts_in"], 16 * 7)
                step(dve.tensor_copy(QM[:, :], qm8[:, :]))
                link(ts(base[:, :, :], pad8[:, :, :], NEG, None, ALU.mult))
                stt(base[:, :, :], bc_mid(SXS[:, :], TILES), 0.5, base[:, :, :], ALU.mult, ALU.add
                    ).then_inc(s["copied"], 1)

            def rotate(l, sem_in, count, even, swap, b0, b1, done, t):
                dve.wait_ge(s[sem_in], count)
                ra = work[:, HALF * t:HALF * t + HALF].rearrange("p (b k) -> p b k", b=8)
                rb = work[:, 1024 + HALF * t:1024 + HALF * t + HALF].rearrange("p (b k) -> p b k", b=8)
                step(stt(ra, even[:, :].rearrange("p (b k) -> p b k", b=8), cols[:, b0:b0 + 1],
                         bc_mid(rope[:, 0, :], 8), ALU.add, ALU.mult))
                link(stt(rb, swap[:, :].rearrange("p (b k) -> p b k", b=8), cols[:, b1:b1 + 1],
                         bc_mid(rope[:, 1, :], 8), ALU.add, ALU.mult))
                tt(ra, ra, rb, ALU.add).then_inc(s[done], 1)

            def keys(l, t):
                dve.wait_ge(s["k_hi"], 2 * l + t + 1)
                half = slice(HALF * t, HALF * t + HALF)
                if l == 0:
                    tt(KT[:, 1, half], work[:, half], KT[:, 0, half], ALU.subtract).then_inc(s["k_lo"], 1)
                else:
                    stt(KT[:, 1, half], context_bank(l, t)[:, :], cols[:, 3 * l + 1:3 * l + 2], KT[:, 0, half],
                        ALU.add, ALU.subtract).then_inc(s["k_lo"], 1)

            def values(l, j):
                dve.wait_ge(s["v_hi"], 4 * l + j + 1)
                for e in range(2):
                    rows = slice(S * e, S * e + S)
                    src = context_bank(l, 2 + j)[rows, :].rearrange("p (b h e d) -> p (b h) e d", b=4, h=HP, e=2)
                    hi, lo = (v[rows, 4 * j:4 * j + 4, :, e, 0:HD].rearrange("p b h d -> p (b h) d")
                              for v in (VH, VL))
                    ins = tt(lo, src[:, :, e, :], hi, ALU.subtract)
                ins.then_inc(s["v_lo"], 1)

            def context(l, i):
                kind, part = CONTEXT[i]
                (keys if kind == "k" else values)(l, part)

            def variance(n, t, with_stats):
                if with_stats:
                    if n:
                        dve.wait_ge(s["sum_read"], SUM_AT[n // 2] - 1 + t)
                    for q in range(4 * t, 4 * t + 4):
                        step(dve.bn_stats(bn[:, q, :], X[:, q, :]))
                    settle()
                    for q in range(4 * t, 4 * t + 4):
                        step(dve.bn_aggr(mv[:, q, :], bn[:, q, :]))
                settle()
                if n:
                    dve.wait_ge(s["rstd_ready"], 2 * (n - 1) + t + 1)
                ts(veps[:, 4 * t:4 * t + 4], mv[:, 4 * t:4 * t + 4, 1], EPS, None, ALU.add
                   ).then_inc(s["var_ready"], 1)

            def normalise_tokens(n, t):
                dve.wait_ge(s["rstd_ready"], 2 * n + t + 1)
                if n or t:
                    dve.wait_ge(s["xn_turned"], 2 * n + t)
                for q in range(4):
                    tile = 4 * t + q
                    ins = ts(XN[:, q, :], X[:, tile, :], mv[:, tile, 0:1], rstd[:, tile:tile + 1],
                             ALU.subtract, ALU.mult)
                ins.then_inc(s["xn_ready"], 1)

            def turned(n, t):
                dve.wait_ge(s["xh_ready"], 2 * n + t + 1)
                half = slice(HALF * t, HALF * t + HALF)
                tt(xT[:, 1, half], turn_bank(n, t)[:, :], xT[:, 0, half], ALU.subtract).then_inc(s["xl_ready"], 1)

            def queries(l, t):
                dve.wait_ge(s["q_hi"], 2 * l + t + 1)
                for r in range(2):
                    rows = slice(S * r, S * r + S)
                    half = slice(HALF * t, HALF * t + HALF)
                    if l == 0:
                        ins = tt(QZ[rows, r, 1, half], work[rows, half], QZ[rows, r, 0, half], ALU.subtract)
                    else:
                        ins = stt(QZ[rows, r, 1, half], query_bank(l, t)[rows, :], cols[rows, 3 * l:3 * l + 1],
                                  QZ[rows, r, 0, half], ALU.add, ALU.subtract)
                ins.then_inc(s["q_lo"], 1)

            def attention(l):
                outputs = bank[6][:, 0:HEADS * (HD + 1)].rearrange("p (h d) -> p h d", h=HEADS)

                def shift(p, before_last):
                    i = TILES * l + p
                    dve.wait_ge(s["scores"], i + 1)
                    if i >= 2:
                        dve.wait_ge(s["pt_turned"], 2 * i - 2)
                    three_d = prob[p % 2].rearrange("p (h k) -> p h k", h=HEADS)
                    pairs = [(bank[2 * (p % 2) + r][:, :].rearrange("p (h k) -> p h k", h=HD),
                              three_d[:, HD * r:HD * r + HD, :], slice(HD * r, HD * r + HD)) for r in range(2)]
                    if l == 1:
                        dve.wait_ge(s["bias_ready"], p + 1)
                    seen = []
                    for ps, dst, heads in pairs:
                        if l == 3:
                            ins = ts(dst, ps, 50.0 / SCALE, -50.0 / SCALE, ALU.min, ALU.max)
                        elif l == 1:
                            step(stt(dst, ps, SCALE / 2, BIAS[:, p % 2, heads, :], ALU.mult, ALU.add))
                        else:
                            step(dve.tensor_reduce(top[:, p % 2, heads], ps, AX_X, ALU.max))
                        seen.append(steps[0])
                    if l == 1:
                        dve.wait_ge(s["dve_step"], seen[1])
                        dve.tensor_reduce(top[:, p % 2, :], three_d, AX_X, ALU.max).then_inc(s["maxima"], 1)
                    if before_last:
                        before_last()
                    if l == 1:
                        dve.wait_ge(s["maxima"], p + 1)
                        ins = tt(three_d[:, 0:HD, :], three_d[:, 0:HD, :], bc_last(top[:, p % 2, 0:HD], S),
                                 ALU.subtract)
                    elif l != 3:
                        for (ps, dst, heads), n in zip(pairs, seen):
                            dve.wait_ge(s["dve_step"], n)
                            ins = tt(dst, ps, bc_last(top[:, p % 2, heads], S), ALU.subtract)
                    ins.then_inc(s["shifted"], 1)

                def invert_sums(p):
                    dve.wait_ge(s["pv"], TILES * l + p + 1)
                    step(dve.reciprocal(rden[:, p % 2, :], outputs[:, :, HD]))

                def normalise(p):
                    i = TILES * l + p
                    settle()
                    if l == 3:
                        link(ts(rden[:, p % 2, :], rden[:, p % 2, :], QM[:, p:p + 1], None, ALU.mult))
                    if i >= 2:
                        dve.wait_ge(s["o_turned"], i - 1)
                    tt(ON[p % 2][:, :].rearrange("p (h d) -> p h d", h=HEADS), outputs[:, :, 0:HD],
                       bc_last(rden[:, p % 2, :], HD), ALU.mult).then_inc(s["o_norm"], 1)

                def add_out(p):
                    i = TILES * l + p
                    dve.wait_ge(s["y_done"], i + 1)
                    stt(X[:, p, :], bank[7][:, P:2 * P], TG[:, l:l + 1], X[:, p, :], ALU.mult, ALU.add
                        ).then_inc(s["x_attn"], 1)

                def first_stats(p):
                    dve.wait_ge(s["x_attn"], TILES * l + p + 1)
                    step(dve.bn_stats(bn[:, p, :], X[:, p, :]))

                def last_stats(p):
                    settle()
                    step(dve.bn_aggr(mv[:, p, :], bn[:, p, :]))

                for k in range(TILES + 4):
                    if l and k == 0:
                        normalise_tokens(2 * l, 1)
                    if l and k == 1:
                        turned(2 * l, 1)
                    if l and k == 2:
                        queries(l, 1)
                    if 3 <= k < TILES + 3:
                        invert_sums(k - 3)
                    if k >= 4:
                        add_out(k - 4)
                    if 3 <= k < TILES + 3:
                        normalise(k - 3)
                    if k < TILES:
                        shift(k, (lambda: first_stats(k - 4)) if k >= 4 else None)
                    elif k >= 4:
                        first_stats(k - 4)
                    if k == TILES:
                        normalise_tokens(2 * l + 1, 0)
                    if k == TILES + 1:
                        turned(2 * l + 1, 0)
                    if 3 <= k < TILES + 3:
                        i = TILES * l + k - 3
                        dve.wait_ge(s["ot_hi"], i + 1)
                        stt(OT[:, 1, :], bank[7][:, 0:P], cols[:, 3 * l + 2:3 * l + 3], OT[:, 0, :],
                            ALU.add, ALU.subtract).then_inc(s["ot_lo"], 1)
                    if k >= 4:
                        last_stats(k - 4)
                    if 1 <= k <= TILES:
                        i = TILES * l + k - 1
                        for g in range(2):
                            dve.wait_ge(s["pt_hi"], 2 * i + g + 1)
                            half = slice(HALF * g, HALF * g + HALF)
                            tt(PT[i % 2][1][:, half], bank[4 + g][:, :], PT[i % 2][0][:, half], ALU.subtract
                               ).then_inc(s["pt_lo"], 1)
                    if k == 3 and l < 3:
                        if l == 0:
                            dve.wait_ge(s["tanh_made"], 1)
                        link(stt(X[:, :, :], bc_mid(BO[:, l, :], TILES), TG[:, l:l + 1], X[:, :, :],
                                 ALU.mult, ALU.add))
                    if k == TILES - 1:
                        variance(2 * l + 1, 0, False)
                variance(2 * l + 1, 1, False)

            def router(l, part):
                e = EXPERTS[l]
                n = TILES * e
                v3 = lambda ap, g=TILES: ap.rearrange("p (t e) -> p t e", t=g)
                T = [r[:, 0:n] for r in rt]

                def first_max(src, sel, small, small2, tmp, groups, width):
                    sm, sm2 = small[:, 0:groups], small2[:, 0:groups]
                    link(dve.tensor_reduce(sm, v3(src, groups), AX_X, ALU.max))
                    link(tt(v3(sel, groups), v3(src, groups), bc_last(sm, width), ALU.is_equal))
                    link(tt(v3(tmp, groups), v3(sel, groups), bc_mid(REV[:, HEADS - width:HEADS], groups), ALU.mult))
                    link(dve.tensor_reduce(sm2, v3(tmp, groups), AX_X, ALU.max))
                    link(tt(v3(sel, groups), v3(tmp, groups), bc_last(sm2, width), ALU.is_equal))

                def largest(src, groups, width):
                    w = groups * width
                    first_max(src, T[3][:, 0:w], rs[0], rs[1], T[4][:, 0:w], groups, width)
                    link(stt(T[5][:, 0:w], T[3][:, 0:w], NEG, src, ALU.mult, ALU.add))

                def second(groups, width):
                    w = groups * width
                    first_max(T[5][:, 0:w], T[6][:, 0:w], rs[2], rs[1], T[4][:, 0:w], groups, width)
                    link(tt(T[3][:, 0:w], T[3][:, 0:w], T[6][:, 0:w], ALU.add))

                tg = TG[:, 4 + l:5 + l]
                ranked = (T[0], T[2], T[1], T[0])[l]
                c3 = comb[:, 0:TILES * COMB].rearrange("p (t e) -> p t e", t=TILES)

                if part == 0:
                    dve.wait_ge(s["logits"], l + 1)
                    dve.wait_ge(s["consts_made"], 1)
                    if l == 3:
                        link(tt(v3(T[0]), v3(bank[7][:, 0:n]), bc_mid(RB[:, 32:40], TILES), ALU.add))
                    else:
                        link(dve.tensor_copy(T[0], bank[7][:, 0:n]))
                    if l == 1:
                        dve.tensor_copy(T[1], T[0]).then_inc(s["exp_in"], 1)
                        link(tt(v3(T[2]), v3(T[0]), bc_mid(RB[:, 0:16], TILES), ALU.add))
                    else:
                        link(dve.tensor_reduce(rs[5][:, 0:TILES], v3(T[0]), AX_X, ALU.max))
                        tt(v3(T[1]), v3(T[0]), bc_last(rs[5][:, 0:TILES], e), ALU.subtract).then_inc(s["exp_in"], 1)
                if part == 1 and l != 1:
                    dve.wait_ge(s["exp_out"], l + 1)
                    link(dve.tensor_reduce(rs[3][:, 0:TILES], v3(T[1]), AX_X, ALU.add))
                    link(dve.reciprocal(rs[4][:, 0:TILES], rs[3][:, 0:TILES]))
                    link(tt(v3(T[0]), v3(T[1]), bc_last(rs[4][:, 0:TILES], e), ALU.mult))
                if part == 2 and l == 2:
                    link(tt(v3(T[1]), v3(T[0]), bc_mid(RB[:, 16:32], TILES), ALU.add))
                    g4 = v3(T[1], 4 * TILES)
                    more, less = (T[i][:, 0:8 * TILES].rearrange("p (g e) -> p g e", e=2) for i in (3, 4))
                    step(tt(more, g4[:, :, 0:2], g4[:, :, 2:4], ALU.max))
                    link(tt(less, g4[:, :, 0:2], g4[:, :, 2:4], ALU.min))
                    step(tt(rs[0][:, :], more[:, :, 0], more[:, :, 1], ALU.max))
                    step(tt(rs[1][:, :], more[:, :, 0], more[:, :, 1], ALU.min))
                    link(tt(rs[2][:, :], less[:, :, 0], less[:, :, 1], ALU.max))
                    link(tt(rs[1][:, :], rs[1][:, :], rs[2][:, :], ALU.max))
                    link(tt(rs[6][:, :], rs[0][:, :], rs[1][:, :], ALU.add))
                    largest(rs[6][:, :], TILES, 4)
                    second(TILES, 4)
                    link(ts(rs[7][:, :], T[3][:, 0:32], -NEG, NEG, ALU.mult, ALU.add))
                    link(tt(v3(T[1], 32), v3(T[1], 32), bc_last(rs[7][:, :], 4), ALU.add))
                if part == 3:
                    largest(ranked, TILES, e)
                if part == 4:
                    second(TILES, e)
                if part == 5 and l == 0:
                    link(stt(rs[3][:, 0:TILES], rs[0][:, 0:TILES], 1e-9, rs[2][:, 0:TILES], ALU.add, ALU.add))
                    link(dve.reciprocal(rs[4][:, 0:TILES], rs[3][:, 0:TILES]))
                    link(tt(T[0], T[0], T[3], ALU.mult))
                    link(tt(v3(T[0]), v3(T[0]), bc_last(rs[4][:, 0:TILES], e), ALU.mult))
                    ts(comb[:, 0:n], T[0], tg, None, ALU.mult).then_inc(s["comb_ready"], 1)
                if part == 5 and l == 1:
                    dve.wait_ge(s["exp_out"], l + 1)
                    link(ts(T[1], T[1], 1.0, None, ALU.add))
                    link(dve.reciprocal(T[0], T[1]))
                    link(tt(T[0], T[0], T[3], ALU.mult))
                    link(dve.tensor_reduce(rs[3][:, 0:TILES], v3(T[0]), AX_X, ALU.add))
                    link(ts(rs[3][:, 0:TILES], rs[3][:, 0:TILES], 1e-10, None, ALU.add))
                    link(dve.reciprocal(rs[4][:, 0:TILES], rs[3][:, 0:TILES]))
                    step(dve.tensor_copy(c3[:, :, 0], ones8[:, :]))
                    tt(c3[:, :, 1:COMB], v3(T[0]), bc_last(rs[4][:, 0:TILES], e), ALU.mult).then_inc(s["comb_ready"], 1)
                if part == 5 and l == 2:
                    step(dve.tensor_copy(c3[:, :, 0], ones8[:, :]))
                    tt(c3[:, :, 1:COMB], v3(T[0]), v3(T[3]), ALU.mult).then_inc(s["comb_ready"], 1)
                if part == 5 and l == 3:
                    link(tt(T[0], T[0], T[3], ALU.mult))
                    ts(mask16[:, :], T[0], 0.0, None, ALU.is_gt).then_inc(s["counts_in"], 1)
                if part == 7 and l == 3:
                    dve.wait_ge(s["counts"], 1)
                    link(ts(T[1], bank[7][:, 0:n], float(CAPACITY), None, ALU.is_lt))
                    link(tt(T[0], T[0], T[1], ALU.mult))
                    ts(comb[:, 0:n], T[0], tg, None, ALU.mult).then_inc(s["comb_ready"], 1)

            def spread(l):
                dve.wait_ge(s["comb_turned"], l)
                step(dve.tensor_copy(combT[:, 0:HALF], bank[6][0:COMB, :]))
                dve.tensor_copy(combT[:, HALF:2 * HALF], bank[7][0:COMB, :]).then_inc(s["combT_ready"], 1)

            def ffn(l):
                at = UNIT_AT[l]
                tg = TG[:, 4 + l:5 + l]

                def product(u):
                    c, t = unit(l, u)[0:2]
                    dve.wait_ge(s["silu_done"], at + u + 1)
                    dve.wait_ge(s["up_done"], at + u + 1)
                    if u >= 2:
                        dve.wait_ge(s["hh_done"], at + u - 1)
                        dve.wait_ge(s["hl_done"], at + u - 1)
                    if l == 0:
                        tt(h32[u % 2], bank[2 + u % 2][:, :], gated[u % 2], ALU.mult).then_inc(s["h32_done"], 1)
                        return
                    b3 = cols[:, 21 + 18 * (l - 1) + c:22 + 18 * (l - 1) + c]
                    ins = stt(h32[u % 2], bank[2 + u % 2][:, :], b3, gated[u % 2], ALU.add, ALU.mult)
                    if c:
                        link(ins)
                        j = c - 1
                        dve.wait_ge(s[f"comb_in{j % 4}"], 32 * (2 * (l - 1) + j // 4 + 1))
                        ins = tt(h32[u % 2], h32[u % 2], CB[:, j % 4, HALF * t:HALF * t + HALF], ALU.mult)
                    ins.then_inc(s["h32_done"], 1)

                def rest(u):
                    dve.wait_ge(s["hh_done"], at + u + 1)
                    if u >= 4:
                        dve.wait_ge(s["down_done"], at + u - 3)
                    if l == 3:
                        stt(hl[:, u % 4, :], bank[u % 4][:, :], 0.0, hh[:, u % 4, :], ALU.max, ALU.subtract
                            ).then_inc(s["hl_done"], 1)
                    else:
                        tt(hl[:, u % 4, :], h32[u % 2], hh[:, u % 4, :], ALU.subtract).then_inc(s["hl_done"], 1)

                def sums(u):
                    c, t, e, place = unit(l, u)
                    if place < PER_EXPERT[l] - 1:
                        return
                    if l in (1, 2):
                        dve.wait_ge(s["sum_done"], 2 * (l - 1) + t + 1)
                    dve.wait_ge(s["down_done"], at + u + 1)
                    acc = acc_bank(l, e, t)[:, :].rearrange("p (t d) -> p t d", t=4)
                    four = X[:, 4 * t:4 * t + 4, :]
                    if l in (1, 2) or (l == 0 and e == 0):
                        settle()
                        step_ = stt(four, acc, tg, four, ALU.mult, ALU.add)
                    else:
                        col = e - 1 if l == 0 else e
                        dve.wait_ge(s["comb_ready"], l + 1)
                        dve.wait_ge(s["sum_read"], SUM_AT[l] + 2 * e + t)
                        for q in range(4):
                            cc = EXPERTS[l] * (4 * t + q) + col
                            step_ = stt(X[:, 4 * t + q, :], acc[:, q, :], comb[:, cc:cc + 1],
                                        X[:, 4 * t + q, :], ALU.mult, ALU.add)
                    step_.then_inc(s["sum_read"], 1)

                for u in range(UNITS[l] + 3):
                    if u == 0 and l in (1, 2):
                        normalise_tokens(2 * l + 1, 1)
                        turned(2 * l + 1, 1)
                        for part in range(6):
                            router(l, part)
                    if u == 4 and l == 3:
                        turned(2 * l + 1, 1)
                    if u < UNITS[l] and l != 3:
                        product(u)
                    if u == 0 and l in (1, 2):
                        spread(l)
                    if u == 0 and l in (0, 3):
                        normalise_tokens(2 * l + 1, 1)
                    if 1 <= u <= UNITS[l] and l in (0, 3):
                        rest(u - 1)
                    if u == 3 and l == 0:
                        turned(2 * l + 1, 1)
                    if l in (0, 3) and u >= ROUTER_FIRST:
                        router(l, u - ROUTER_FIRST)
                    if l < 3 and KV_AT[l] < u <= KV_AT[l] + len(CONTEXT):
                        context(l + 1, u - KV_AT[l] - 1)
                    if l < 3:
                        if u >= 3:
                            sums(u - 3)
                        if u == LAST_FIRST[l] + 3:
                            variance(2 * l + 2, 0, True)
                        if u == LAST_FIRST[l] + 4:
                            normalise_tokens(2 * l + 2, 0)
                        if l == 0 and u == LAST_FIRST[l] + 5:
                            turned(2 * l + 2, 0)
                    elif u == ROUTER_FIRST + 8:
                        for v in range(u - 2):
                            sums(v)
                    elif u > ROUTER_FIRST + 8:
                        sums(u - 3)

            dve.wait_ge(s["x_in"], 16)
            variance(0, 0, True)
            variance(0, 1, True)
            split_weights(0, 6, 1)
            split_context()
            normalise_tokens(0, 0)
            turned(0, 0)
            normalise_tokens(0, 1)
            turned(0, 1)
            dve.wait_ge(s["first_in"], 48)
            for t in range(2):
                rotate(0, "k_proj", t + 1, bank[t], bank[6 + t], 1, 49, "k_rot", t)
            for i in range(len(CONTEXT)):
                context(0, i)
            for t in range(2):
                rotate(0, "q_proj", t + 1, bank[t], bank[2 + t], 0, 48, "q_rot", t)
            for t in range(2):
                queries(0, t)
            split_weights(6, 18, 2)
            prepare()
            for l in range(LAYERS):
                if l:
                    variance(2 * l, 1, True)
                    if l > 1:
                        turned(2 * l, 0)
                    queries(l, 0)
                attention(l)
                ffn(l)


def kernel(**inputs):
    import numpy as np
    import concourse.bacc as bacc
    from concourse.bass_utils import run_bass_kernel_spmd

    v = {k: np.asarray(x) for k, x in inputs.items()}
    zero = np.zeros(P, np.float32)
    swap = np.arange(P) ^ 1

    names = [("L0_xattn_Wq", "L0_xattn_Wk", "L0_xattn_Wv", "L0_xattn_Wo"),
             ("L1_xattn_Wq", "L1_xattn_Wk", "L1_xattn_Wv", "L1_xattn_Wo"),
             ("L2_xattn_W_q", "L2_xattn_W_k", "L2_xattn_W_v", "L2_xattn_W_o"),
             ("L3_xattn_W_q", "L3_xattn_W_k", "L3_xattn_W_v", "L3_xattn_W_o")]
    mats = [v[n].T for n in names[0]] + [v["L0_xattn_Wq"][swap].T, v["L0_xattn_Wk"][swap].T]
    mats += [v[n].T for layer in names[1:] for n in layer]
    attn_w = np.stack(mats, 1).reshape(P, AW_COLS)

    columns = [v["L0_xattn_bq"], v["L0_xattn_bk"], v["L0_xattn_bv"],
               v["L1_xattn_bq"], v["L1_xattn_bk"], v["L1_xattn_bv"],
               v["L2_xattn_b_q"], v["L2_xattn_b_k"], v["L2_xattn_b_v"],
               zero, zero, zero]
    layer1 = [v["L1_ffn_sb1"]] + list(v["L1_ffn_b1"].reshape(8, P)) + [v["L1_ffn_sb3"]] + list(v["L1_ffn_b3"].reshape(8, P))
    layer2 = [v["L2_ffn_bs1"]] + list(v["L2_ffn_be1"].reshape(8, P)) + [v["L2_ffn_bs3"]] + list(v["L2_ffn_be3"].reshape(8, P))
    columns = columns + layer1 + layer2 + [v["L0_xattn_bq"][swap], v["L0_xattn_bk"][swap]]

    freq = 1.0 / 10000.0 ** (np.arange(0, HD, 2, dtype=np.float32) / HD)
    angle = np.repeat(freq, 2)[:, None].astype(np.float32) * np.arange(S, dtype=np.float32)[None, :]
    sign = np.where(np.arange(HD) % 2 == 0, -1.0, 1.0)[:, None]
    rope = np.stack([np.tile(np.cos(angle), (HEADS, 1)), np.tile(np.sin(angle) * sign, (HEADS, 1))], 1)

    def slices(*ms):
        return np.stack(ms, 2).reshape(P, -1)

    def wide(m):
        return m.reshape(P, -1, P)

    def tall(m):
        return m.reshape(-1, P, P).transpose(1, 0, 2)

    def hidden(first, rest, flip):
        parts = ([first] if first is not None else []) + list(rest)
        return [p.T for p in parts] if flip else parts

    f = v
    ffn0 = slices(
        wide(np.concatenate(hidden(f["L0_ffn_shared_gate"], f["L0_ffn_routed_gate"], True), 1)),
        wide(np.concatenate(hidden(f["L0_ffn_shared_up"], f["L0_ffn_routed_up"], True), 1)),
        tall(np.concatenate(hidden(f["L0_ffn_shared_down"], f["L0_ffn_routed_down"], True), 0)))
    ffn1 = slices(
        wide(np.concatenate(hidden(f["L1_ffn_sw1"], f["L1_ffn_w1"], True), 1)),
        wide(np.concatenate(hidden(f["L1_ffn_sw3"], f["L1_ffn_w3"], True), 1)),
        tall(np.concatenate(hidden(f["L1_ffn_sw2"], f["L1_ffn_w2"], True), 0)))
    ffn2 = slices(
        wide(np.concatenate(hidden(f["L2_ffn_ws1"], f["L2_ffn_We1"], False), 1)),
        wide(np.concatenate(hidden(f["L2_ffn_ws3"], f["L2_ffn_We3"], False), 1)),
        tall(np.concatenate(hidden(f["L2_ffn_ws2"], f["L2_ffn_We2"], False), 0)))
    ffn3 = slices(
        wide(np.concatenate(hidden(None, f["L3_ffn_experts_inter"], False), 1)),
        tall(np.concatenate(hidden(None, f["L3_ffn_experts_out"], False), 0)))

    b2 = np.stack([np.concatenate([v["L1_ffn_sb2"][None], v["L1_ffn_b2"]]),
                   np.concatenate([v["L2_ffn_bs2"][None], v["L2_ffn_be2"]])], 1)
    fside = v["fside_Bx16xSxS2_0"].transpose(0, 2, 1, 3).reshape(TILES, P, HEADS * S)
    arrays = {
        "x": v["x"].reshape(B * S, D), "ctxT": v["ctx_1024"].reshape(B * S, D).T, "attn_w": attn_w,
        "ffn_w0": ffn0, "ffn_w1": ffn1, "ffn_w2": ffn2, "ffn_w3": ffn3,
        "router_w": np.concatenate([v["L0_ffn_router_w"].T, v["L1_ffn_gate_w"].T, v["L2_ffn_gate_w"].T,
                                    v["L3_ffn_W_router"].T], 1),
        "router_b": np.concatenate([v["L1_ffn_expert_bias"], v["L2_ffn_gate_b"], v["L3_ffn_b_router"]]),
        "cols": np.stack(columns, 1), "rope": rope.astype(np.float32),
        "bo": np.stack([v["L0_xattn_bo"], v["L1_xattn_bo"], v["L2_xattn_b_o"], zero]),
        "gates": np.concatenate([v["g_xattn"], v["g_ffn"]]),
        "sxs": np.concatenate([v["fside_SxS2_0"]] * 2),
        "pad": v["mask_BxS2_bf0"].reshape(TILES, 2, S).transpose(1, 0, 2),
        "qmask": v["mask_BxS_bf1"].reshape(TILES, P).T, "b2": b2, "fside": fside,
    }
    arrays = {k: np.ascontiguousarray(x) for k, x in arrays.items()}
    nc = bacc.Bacc("TRN2", target_bir_lowering=False, num_devices=1)
    aps = {k: nc.dram_tensor(f"in_{k}", x.shape, mybir.dt.from_np(x.dtype), kind="ExternalInput").ap()
           for k, x in arrays.items()}
    aps["out"] = nc.dram_tensor("out_x", (B * S, D), F32, kind="ExternalOutput").ap()
    build(nc, aps)
    r = run_bass_kernel_spmd(nc, [{f"in_{k}": x for k, x in arrays.items()}], core_ids=[0])
    return r.results[0]["out_x"].reshape(B, S, D)
```

```python
from contextlib import ExitStack

import concourse.bass as bass
from concourse import mybir

ALU = mybir.AluOpType
ACT = mybir.ActivationFunctionType
AX_X = mybir.AxisListType.X
F32 = mybir.dt.float32
F16 = mybir.dt.float16
U8 = mybir.dt.uint8

P = 128
B, S, D = 16, 64, 128
HEADS, HD = 16, 8
LAYERS = 4
TILES = B * S // P
HALF = 512
HP = HEADS // 2
SCALE = HD ** -0.5
EPS = 1e-5
NEG = -1e30
CAPACITY = 160

EXPERTS = [7, 16, 16, 8]
ROUTER_AT = [0, 7, 23, 39]
CHUNKS = [32, 9, 9, 32]
PER_EXPERT = [4, 9, 9, 4]
MATS = [3, 3, 3, 2]
UNITS = [2 * c for c in CHUNKS]
UNIT_AT = [sum(UNITS[:l]) for l in range(LAYERS + 1)]
FFN_COLS = [CHUNKS[l] * MATS[l] * P for l in range(LAYERS)]
GRAIN = 768
STAGES = 4
AW_COLS = 14 * P
AW_FIRST = 5 * P
COMB = 17
SUMS = [16, 2, 2, 16]
TURN_AT = [2, 1, 1, 3]
NEXT_AT = [58, 12, 12]
KV_AT = 24
SPREAD = [(0, 2), (2, 5), (5, 8)]
COMB_TURN_AT = 8
COUNT_AT = 12
ROUTER_PARTS = [0, 1, 3, 3.1, 4, 4.1, 5, 7]
ROUTER_FIRST = 5
SUM_AT = [sum(SUMS[:l]) for l in range(LAYERS + 1)]

GRAINS = []
for _l in range(LAYERS):
    for _c in range(0, FFN_COLS[_l], GRAIN):
        GRAINS.append((_l, _c, min(GRAIN, FFN_COLS[_l] - _c)))
GRAIN_AT = [next(n for n, g in enumerate(GRAINS) if g[0] == l) for l in range(LAYERS)]
SPLIT_AT = [[range(2 * p, 2 * p + 2) for p in range(TILES)],
            [range(GRAIN_AT[1] + p, min(GRAIN_AT[1] + p + 1, GRAIN_AT[2])) for p in range(TILES)],
            [range(GRAIN_AT[2] + 2 * p, min(GRAIN_AT[2] + 2 * p + 2, len(GRAINS))) for p in range(TILES)],
            [range(0)] * TILES]
assert [n for layer in SPLIT_AT for r in layer for n in r] == list(range(len(GRAINS)))


def unit(l, u):
    if l in (0, 3):
        k = PER_EXPERT[l]
        e, t, place = u // (2 * k), u // k % 2, u % k
        if l == 0 and e >= 6:
            e, t = 6 + t, e - 6
        return k * e + place, t, e, place
    if u < 2:
        return 0, u, 0, 0
    k = CHUNKS[l] - 1
    return 1 + (u - 2) % k, (u - 2) // k, 0, 1 + (u - 2) % k


def once(l, t=0):
    return (1, 2 + t, 4 + t, 6)[l]


def mat(l, m):
    return m if l == 0 else 2 + 3 * l + m


def bc_last(ap, n):
    return ap.unsqueeze(len(ap.shape)).broadcast_to(list(ap.shape) + [n])


def bc_mid(ap, n):
    return ap.unsqueeze(1).broadcast_to([ap.shape[0], n, ap.shape[1]])


def build(nc, a):
    ctx = ExitStack()
    with ctx:
        def sb(name, shape, dt=F32):
            return ctx.enter_context(nc.sbuf_tensor(name, shape, dt))

        def sem(name):
            return ctx.enter_context(nc.semaphore(name))

        bank = [ctx.enter_context(nc.psum_tensor(f"bank{i}", [P, 512], F32)) for i in range(8)]

        X = sb("X", [P, TILES, D])
        XN = sb("XN", [P, TILES // 2, D])
        xT = sb("xT", [P, 2, B * S], F16)
        QZ = sb("QZ", [P, 2, 2, B * S], F16)
        KT = sb("KT", [P, 2, B * S], F16)
        KM = sb("KM", [P, 2, HD, B * S], F16)
        VH = sb("VH", [P, B, HP, 2, HD + 1], F16)
        VL = sb("VL", [P, B, HP, 2, HD + 1], F16)
        CT = sb("CT", [P, 2, B, 2, S], F16)
        AW = sb("AW", [P, 2, 14, P], F16)
        WA = sb("WA", [P, 2, FFN_COLS[0]], F16)
        WB = sb("WB", [P, 2, FFN_COLS[1]], F16)
        stage = sb("stage", [P, STAGES, GRAIN])
        CB = sb("CB", [P, TILES, HALF])
        work = sb("work", [P, 4096])
        ident = sb("ident", [P, P])
        before = sb("before", [P, P], F16)
        ones16 = sb("ones16", [P, P], F16)
        ones8 = sb("ones8", [P, TILES])
        expo = sb("expo", [P, TILES])
        cols = sb("cols", [P, 50])
        rope = sb("rope", [P, 2, S])
        BO = sb("BO", [P, LAYERS, D])
        TG = sb("TG", [P, 8])
        RW = sb("RW", [P, 2, 47], F16)
        rw32 = sb("rw32", [P, 47])
        RB = sb("RB", [P, 40])
        SXS = sb("SXS", [P, S])
        base = sb("base", [P, TILES, S])
        pad8 = sb("pad8", [P, TILES, S], U8)
        qm8 = sb("qm8", [P, TILES], U8)
        QM = sb("QM", [P, TILES])
        B2 = sb("B2", [COMB, 2, D])
        REV = sb("REV", [P, HEADS])
        bn = sb("bn", [P, TILES, 6])
        mv = sb("mv", [P, TILES, 2])
        veps = sb("veps", [P, TILES])
        rstd = sb("rstd", [P, TILES])
        top = sb("top", [P, 2, HEADS])
        rden = sb("rden", [P, 2, HEADS])
        ON = [sb(f"ON{i}", [P, D]) for i in range(2)]
        OT = sb("OT", [P, 2, P])
        WO = sb("WO", [P, LAYERS, P])
        rt = [sb(f"rt{i}", [P, TILES * 16]) for i in range(8)]
        rs = [sb(f"rs{i}", [P, 32]) for i in range(8)]
        mask16 = sb("mask16", [P, TILES * 8], F16)
        spare = sb("spare", [P, 1])
        comb = sb("comb", [P, TILES * COMB])
        combT = sb("combT", [COMB, B * S])

        BIAS = CB[:, 0:4, :].rearrange("p (i a) (h k) -> p i (a h) k", a=2, k=S)
        prob = [work[:, 0:1024], work[:, 1024:2048]]
        PT = [[work[:, at:at + 512].bitcast(F16) for at in (lo, lo + 512)] for lo in (2048, 3072)]
        gated = [work[:, 0:512], work[:, 512:1024]]
        h32 = [work[:, 1024:1536], work[:, 1536:2048]]
        hh = work[:, 2048:3072].bitcast(F16).rearrange("p (s n) -> p s n", s=4)
        hl = work[:, 3072:4096].bitcast(F16).rearrange("p (s n) -> p s n", s=4)
        raw = WB[:, :, :].rearrange("p a n -> p (a n)").bitcast(F32)

        comb_dram = nc.dram_tensor("comb_scratch", [2, COMB, B * S], F32, kind="Internal").ap()

        names = """first_in consts_in rw_in aw0_in aw_in ctx_in x_in fside_in0 fside_in1 stage_in0 stage_in1 stage_in2 stage_in3 km_in km_zero
        comb_out comb_in0 comb_in1 comb_in2 out_done
        ident_made consts_made tanh_made table_used q_zero aw_hi aw_lo ctx_hi ctx_lo rw_hi rw_lo
        dve_step pool_step split_hi split_lo bias_ready
        var_ready rstd_ready xn_ready xn_turned xh_ready xl_ready
        k_proj k_rot k_hi k_lo v_proj v_hi v_lo q_proj q_rot q_hi q_lo
        scores maxima shifted shifted_last probs pt_turned pt_hi pt_lo pv o_norm o_turned ot_ready y_done x_attn
        logits copied exp_in exp_out counts_in counts comb_ready comb_turned combT_ready
        gate_done up_done silu_done h32_done hh_done hl_done down_done sum_done sum_read x_out""".split()
        s = {n: sem(n) for n in names}

        def aw(i, hl):
            return AW[:, hl, i, :]

        def weight(l, chunk, m, hl):
            at = (chunk * MATS[l] + m) * P
            return (WA if l in (0, 3) else WB)[:, hl, at:at + P]

        def grain_of(l, chunk):
            return GRAIN_AT[l] + ((chunk + 1) * MATS[l] * P - 1) // GRAIN + 1

        def turn_bank(n, t):
            if n == 0:
                return bank[4 + t]
            return bank[0 if n % 2 and t == 0 else 6 + t]

        ACCS = [2, 0, 0, 4]

        def acc_bank(l, u):
            return bank[4 + (u // 4 % ACCS[l] if ACCS[l] else unit(l, u)[1])]

        CONTEXT = [("k", 0), ("k", 1), ("v", 0), ("v", 1), ("v", 2), ("v", 3)]

        def context_bank(l, i):
            return bank[((0, 1, 2, 3, 4, 5), (6, 7) * 3, (4, 5, 7, 6, 4, 5), (4, 5, 7, 6, 4, 5))[l][i]]

        def context_frees(l, i):
            return None if l == 0 or i < 2 or (l > 1 and i < 4) else CONTEXT[i - 2 if l == 1 else i - 4]

        def context_at(l, u):
            if l == 0:
                return [u - KV_AT] if KV_AT <= u < KV_AT + len(CONTEXT) else []
            return range(2, len(CONTEXT)) if l < 3 and u == 1 else []

        LAST = TILES - 1

        def out_bank(p):
            return bank[5 if p == LAST else 6]

        def turned_out_bank(p):
            return bank[4 if p == LAST else 7]

        def finishing(k):
            return [k - 3] if 3 <= k <= TILES else [TILES - 2, LAST] if k == TILES + 1 else []

        def adding(k):
            return [k - 4] if 4 <= k <= TILES + 1 else [TILES - 2, LAST] if k == TILES + 2 else []

        def query_bank(l, t):
            return bank[t] if l == 0 else bank[7]

        block = ctx.enter_context(nc.Block())

        @block.sync
        def _(sp):
            sp.dma_start(X[:, :, :], a["x"].rearrange("(t p) d -> p t d", p=P)).then_inc(s["x_in"], 16)
            sp.dma_start(raw[:, 0:AW_FIRST], a["attn_w"][:, 0:AW_FIRST]).then_inc(s["aw0_in"], 16)
            sp.dma_start(raw[:, AW_COLS:AW_COLS + B * S], a["ctxT"]).then_inc(s["ctx_in"], 16)
            for dst, src in ((cols[:, :], a["cols"]), (rope[:, :, :], a["rope"]),
                             (TG[:, :], a["gates"].partition_broadcast(P))):
                sp.dma_start(dst, src).then_inc(s["first_in"], 16)
            sp.dma_start(raw[:, AW_FIRST:AW_COLS], a["attn_w"][:, AW_FIRST:AW_COLS]).then_inc(s["aw_in"], 16)
            sp.dma_start(rw32[:, :], a["router_w"]).then_inc(s["rw_in"], 16)
            for dst, src in (
                (BO[:, :, :], a["bo"].partition_broadcast(P)),
                (RB[:, :], a["router_b"].partition_broadcast(P)), (SXS[:, :], a["sxs"]),
                (pad8[0:S, :, :], a["pad"][0].partition_broadcast(S)),
                (pad8[S:P, :, :], a["pad"][1].partition_broadcast(S)),
                (qm8[:, :], a["qmask"]), (B2[:, :, :], a["b2"]), (WO[:, :, :], a["wo"]),
            ):
                sp.dma_start(dst, src).then_inc(s["consts_in"], 16)

            def load_grain(n):
                l, c, w = GRAINS[n]
                if n >= STAGES:
                    sp.wait_ge(s["split_lo"], n - STAGES + 1)
                sp.dma_start(stage[:, n % STAGES, 0:w], a[f"ffn_w{l}"][:, c:c + w]).then_inc(s[f"stage_in{n % STAGES}"], 16)

            def place_keys(l):
                sp.wait_ge(s["k_lo"], 2 * l + 2)
                if l == 0:
                    sp.wait_ge(s["km_zero"], 2)
                else:
                    sp.wait_ge(s["scores"], TILES * l)
                for j in range(HD):
                    for r in (0, S):
                        lo = r + HD * j
                        sp.dma_start(KM[lo:lo + HD, :, j, :], KT[lo:lo + HD, :, :]).then_inc(s["km_in"], 16)

            def load_fside(p):
                if p >= 2:
                    sp.wait_ge(s["shifted"], TILES + p - 1)
                sp.dma_start(BIAS[:, p % 2, :, :].rearrange("p h k -> p (h k)"),
                             a["fside"][p]).then_inc(s[f"fside_in{p % 2}"], 16)

            def spread_comb(l, t):
                half = slice(HALF * t, HALF * t + HALF)
                sp.wait_ge(s["combT_ready"], 2 * (l - 1) + t + 1)
                sp.dma_start(comb_dram[l - 1, :, half], combT[:, half]).then_inc(s["comb_out"], 16)
                sp.wait_ge(s["comb_out"], 16 * (2 * (l - 1) + t + 1))
                for g, (lo, hi) in enumerate(SPREAD):
                    if t:
                        sp.wait_ge(s["h32_done"], UNIT_AT[l] + 2 + hi)
                    for e in range(2):
                        rows = comb_dram[l - 1, 1:COMB, half].rearrange("(j e) n -> e j n", e=2)[e, lo:hi]
                        sp.dma_start(CB[S * e:S * e + S, lo:hi, :], rows.partition_broadcast(S)
                                     ).then_inc(s[f"comb_in{g}"], 16)

            for n in range(STAGES):
                load_grain(n)
            place_keys(0)
            for n in range(STAGES, GRAIN_AT[1]):
                load_grain(n)
            load_fside(0)
            load_fside(1)
            place_keys(1)
            for n in range(GRAIN_AT[1], GRAIN_AT[1] + STAGES):
                load_grain(n)
            for p in range(2, TILES):
                load_fside(p)
                if GRAIN_AT[1] + STAGES + p - 2 < GRAIN_AT[2] + STAGES:
                    load_grain(GRAIN_AT[1] + STAGES + p - 2)
            spread_comb(1, 0)
            place_keys(2)
            spread_comb(1, 1)
            for n in range(GRAIN_AT[2] + STAGES, len(GRAINS)):
                load_grain(n)
            spread_comb(2, 0)
            place_keys(3)
            spread_comb(2, 1)
            for t in range(2):
                sp.wait_ge(s["sum_read"], SUM_AT[4] - 1 + t)
                sp.dma_start(a["out"].rearrange("(t p) d -> p t d", p=P)[:, 4 * t:4 * t + 4, :],
                             X[:, 4 * t:4 * t + 4, :]).then_inc(s["out_done"], 16)
            sp.wait_ge(s["out_done"], 32)

        @block.gpsimd
        def _(pool):
            steps = [0]

            def step(ins):
                steps[0] += 1
                ins.then_inc(s["pool_step"], 1)

            def settle():
                pool.wait_ge(s["pool_step"], steps[0])

            def link(ins):
                step(ins)
                settle()

            link(pool.memset(ident[:, :], 0.0))
            link(pool.memset(before[:, :], 1.0))
            link(pool.memset(expo[:, :], -0.5))
            pool.affine_select(out=ident[:, :], in_=ident[:, :], compare_op=ALU.not_equal, fill=1.0, base=0,
                               pattern=[[-1, P]], channel_multiplier=1).then_inc(s["ident_made"], 1)
            pool.wait_ge(s["ident_made"], 1)

            def powers(n, t):
                pool.wait_ge(s["var_ready"], 2 * n + t + 1)
                pool.tensor_tensor(rstd[:, 4 * t:4 * t + 4], veps[:, 4 * t:4 * t + 4],
                                   expo[:, 4 * t:4 * t + 4], ALU.pow).then_inc(s["rstd_ready"], 1)
                pool.wait_ge(s["rstd_ready"], 2 * n + t + 1)

            powers(0, 0)
            powers(0, 1)
            pool.memset(QZ[:, :, :, :].rearrange("p r h n -> p (r h n)").bitcast(F32), 0.0).then_inc(s["q_zero"], 1)
            pool.wait_ge(s["q_zero"], 1)
            for hl_ in range(2):
                pool.memset(KM[:, hl_, :, :].rearrange("p j n -> p (j n)").bitcast(F32), 0.0
                            ).then_inc(s["km_zero"], 1)
                pool.wait_ge(s["km_zero"], hl_ + 1)
            for v in (VH, VL):
                link(pool.memset(v[:, :, :, :, :].rearrange("p b h e d -> p (b h e d)"), 0.0))
            for e in range(2):
                link(pool.memset(VH[S * e:S * e + S, :, :, e, HD], 1.0))
            link(pool.affine_select(out=before[:, :], in_=before[:, :], compare_op=ALU.is_gt, fill=0.0, base=0,
                                    pattern=[[1, P]], channel_multiplier=-1))
            link(pool.memset(ones16[:, :], 1.0))
            link(pool.memset(ones8[:, :], 1.0))
            for j in range(HEADS):
                link(pool.memset(REV[:, j:j + 1], float(HEADS - j)))
            pool.memset(REV[:, 0:1], float(HEADS)).then_inc(s["consts_made"], 1)
            pool.wait_ge(s["consts_made"], 1)

            def low_grain(n):
                l, c, w = GRAINS[n]
                dst = WA if l in (0, 3) else WB
                pool.wait_ge(s["split_hi"], n + 1)
                pool.tensor_tensor(dst[:, 1, c:c + w], stage[:, n % STAGES, 0:w], dst[:, 0, c:c + w],
                                   ALU.subtract).then_inc(s["split_lo"], 1)
                pool.wait_ge(s["split_lo"], n + 1)

            def low_halves(l):
                at = UNIT_AT[l]
                for u in range(UNITS[l]):
                    pool.wait_ge(s["hh_done"], at + u + 1)
                    if u >= 4:
                        pool.wait_ge(s["down_done"], at + u - 3)
                    pool.tensor_tensor(hl[:, u % 4, :], h32[u % 2], hh[:, u % 4, :], ALU.subtract
                                       ).then_inc(s["hl_done"], 1)
                    pool.wait_ge(s["hl_done"], at + u + 1)
                    if u == NEXT_AT[l]:
                        powers(2 * l + 2, 0)

            def shift(p):
                pool.wait_ge(s["maxima"], p + 1)
                dst = prob[p % 2][:, HALF:2 * HALF].rearrange("p (h k) -> p h k", h=HD)
                pool.tensor_tensor(dst, dst, bc_last(top[:, p % 2, HD:2 * HD], S), ALU.subtract
                                   ).then_inc(s["shifted_last"], 1)
                pool.wait_ge(s["shifted_last"], p + 1)

            def add_bias(p):
                pool.wait_ge(s[f"fside_in{p % 2}"], 16 * (p // 2 + 1))
                if p == 0:
                    pool.wait_ge(s["copied"], 1)
                if p >= 2:
                    pool.wait_ge(s["shifted"], TILES + p - 1)
                pool.tensor_tensor(BIAS[:, p % 2, :, :], BIAS[:, p % 2, :, :], bc_mid(base[:, p, :], HEADS),
                                   ALU.add).then_inc(s["bias_ready"], 1)
                pool.wait_ge(s["bias_ready"], p + 1)

            for l in range(LAYERS):
                if l == 1:
                    powers(2 * l, 0)
                if l:
                    powers(2 * l, 1)
                for p in range(TILES):
                    if l == 1 and p == 0:
                        add_bias(0)
                    if l == 1:
                        shift(p)
                    if l == 1 and p + 1 < TILES:
                        add_bias(p + 1)
                    if p == TILES - 1:
                        powers(2 * l + 1, 0)
                    for n in SPLIT_AT[l][p]:
                        low_grain(n)
                powers(2 * l + 1, 1)
                if l in (1, 2):
                    low_halves(l)

        @block.scalar
        def _(act):
            def split_weights(lo, hi, arrived):
                act.wait_ge(s[arrived], 16)
                act.activation(AW[:, 0, lo:hi, :].rearrange("p i n -> p (i n)"), raw[:, P * lo:P * hi], ACT.Copy
                               ).then_inc(s["aw_hi"], 1)

            def keys(l, t):
                dst = KT[:, 0, HALF * t:HALF * t + HALF]
                if t == 0 and l:
                    act.wait_ge(s["km_in"], 256 * l)
                if l == 0:
                    act.wait_ge(s["k_rot"], t + 1)
                    act.activation(dst, work[:, HALF * t:HALF * t + HALF], ACT.Copy).then_inc(s["k_hi"], 1)
                else:
                    act.wait_ge(s["k_proj"], 2 * l + t + 1)
                    act.activation(dst, context_bank(l, t)[:, :], ACT.Identity, bias=cols[:, 3 * l + 1:3 * l + 2]
                                   ).then_inc(s["k_hi"], 1)

            def values(l, j):
                if l == 0:
                    act.wait_ge(s["consts_made"], 1)
                else:
                    act.wait_ge(s["pv"], TILES * l)
                act.wait_ge(s["v_proj"], 4 * l + j + 1)
                for e in range(2):
                    rows = slice(S * e, S * e + S)
                    src = context_bank(l, 2 + j)[rows, :].rearrange("p (b h e d) -> p (b h) e d", b=4, h=HP, e=2)
                    dst = VH[rows, 4 * j:4 * j + 4, :, e, 0:HD].rearrange("p b h d -> p (b h) d")
                    ins = act.activation(dst, src[:, :, e, :], ACT.Copy)
                ins.then_inc(s["v_hi"], 1)

            def context(l, i):
                kind, part = CONTEXT[i]
                (keys if kind == "k" else values)(l, part)

            tables = [0]

            def load_table(kind):
                if tables[0]:
                    act.wait_ge(s["table_used"], tables[0])
                else:
                    act.wait_ge(s["consts_made"], 1)
                act.activation(spare[:, :], ones8[:, 0:1], kind).then_inc(s["table_used"], 1)
                tables[0] += 1

            def turned(n, t):
                act.wait_ge(s["xn_turned"], 2 * n + t + 1)
                act.activation(xT[:, 0, HALF * t:HALF * t + HALF], turn_bank(n, t)[:, :], ACT.Copy
                               ).then_inc(s["xh_ready"], 1)

            def queries(l, t):
                if l == 0:
                    act.wait_ge(s["q_zero"], 1)
                    act.wait_ge(s["q_rot"], t + 1)
                else:
                    act.wait_ge(s["q_proj"], 2 * l + t + 1)
                    if t == 0:
                        act.wait_ge(s["scores"], TILES * l)
                for r in range(2):
                    rows = slice(S * r, S * r + S)
                    dst = QZ[rows, r, 0, HALF * t:HALF * t + HALF]
                    if l == 0:
                        ins = act.activation(dst, work[rows, HALF * t:HALF * t + HALF], ACT.Copy)
                    else:
                        ins = act.activation(dst, query_bank(l, t)[rows, :], ACT.Identity, bias=cols[rows, 3 * l:3 * l + 1])
                ins.then_inc(s["q_hi"], 1)

            def high_grain(n):
                l, c, w = GRAINS[n]
                act.wait_ge(s[f"stage_in{n % STAGES}"], 16 * (n // STAGES + 1))
                if n == GRAIN_AT[1]:
                    act.wait_ge(s["aw_lo"], 2)
                    act.wait_ge(s["ctx_lo"], 2)
                if n == GRAIN_AT[2]:
                    act.wait_ge(s["down_done"], UNIT_AT[2])
                if n == GRAIN_AT[3]:
                    act.wait_ge(s["down_done"], UNIT_AT[1])
                act.activation((WA if l in (0, 3) else WB)[:, 0, c:c + w], stage[:, n % STAGES, 0:w], ACT.Copy
                               ).then_inc(s["split_hi"], 1)

            def attention(l):
                exp_scale = 2.0 if l == 1 else SCALE
                for k in range(TILES + 3):
                    if 1 <= k <= TILES:
                        i = TILES * l + k - 1
                        for g in range(2):
                            act.wait_ge(s["pt_turned"], 2 * i + g + 1)
                            if i >= 2:
                                act.wait_ge(s["pv"], i - 1)
                            act.activation(PT[i % 2][0][:, HALF * g:HALF * g + HALF], bank[4 + g][:, :], ACT.Copy
                                           ).then_inc(s["pt_hi"], 1)
                    if l and k == 1:
                        turned(2 * l, 1)
                    if l and k == 2:
                        queries(l, 1)
                    for p in finishing(k):
                        i = TILES * l + p
                        act.wait_ge(s["o_turned"], i + 1)
                        if i >= 2:
                            act.wait_ge(s["y_done"], i - 1)
                        act.activation(OT[:, p % 2, :], turned_out_bank(p)[:, 0:P], ACT.Identity,
                                       bias=cols[:, 3 * l + 2:3 * l + 3]).then_inc(s["ot_ready"], 1)
                    if k < TILES:
                        i = TILES * l + k
                        act.wait_ge(s["shifted"], i + 1)
                        if l == 1:
                            act.wait_ge(s["shifted_last"], k + 1)
                        act.activation(prob[k % 2], prob[k % 2], ACT.Exp, scale=exp_scale).then_inc(s["probs"], 1)
                    if k < TILES:
                        for n in SPLIT_AT[l][k]:
                            high_grain(n)
                    if k == TILES:
                        turned(2 * l + 1, 0)
                    if l in (1, 2) and k == TILES + 2:
                        exponent(l, 0)
                    if l == 0 and k == TILES + 1:
                        load_table(ACT.Silu)

            def exponent(l, t=0):
                n = EXPERTS[l] * TILES // (2 if l in (1, 2) else 1)
                act.wait_ge(s["exp_in"], once(l, t))
                act.activation(rt[1][:, 0:n], rt[1][:, 0:n], ACT.Exp, scale=-1.0 if l == 1 else 1.0
                               ).then_inc(s["exp_out"], 1)

            def spread(l, t):
                act.wait_ge(s["comb_turned"], 2 * (l - 1) + t + 1)
                if l == 2:
                    act.wait_ge(s["sum_done"], 1 + t)
                    act.wait_ge(s["comb_out"], 16 * (1 + t))
                act.activation(combT[:, HALF * t:HALF * t + HALF], bank[6][0:COMB, :], ACT.Copy
                               ).then_inc(s["combT_ready"], 1)

            def ffn(l):
                at = UNIT_AT[l]

                if l in (1, 2):
                    turned(2 * l + 1, 1)
                    context(l + 1, 0)
                    context(l + 1, 1)
                    spread(l, 0)
                    exponent(l, 1)
                for u in range(UNITS[l] + 1):
                    if l == 3 and u < UNITS[l]:
                        act.wait_ge(s["gate_done"], at + u + 1)
                        if u >= 4:
                            act.wait_ge(s["down_done"], at + u - 3)
                        act.activation(hh[:, u % 4, :], bank[u % 4][:, :], ACT.Relu).then_inc(s["hh_done"], 1)
                    if l < 3 and u < UNITS[l]:
                        c = unit(l, u)[0]
                        act.wait_ge(s["gate_done"], at + u + 1)
                        if u >= 2:
                            act.wait_ge(s["h32_done"], at + u - 1)
                        kind = {"bias": cols[:, 12 + 18 * (l - 1) + c:13 + 18 * (l - 1) + c]} if l else {}
                        act.activation(gated[u % 2], bank[u % 2][:, :], ACT.Silu, **kind).then_inc(s["silu_done"], 1)
                    if l < 3 and u >= 1:
                        v = u - 1
                        act.wait_ge(s["h32_done"], at + v + 1)
                        if v >= 4:
                            act.wait_ge(s["down_done"], at + v - 3)
                        act.activation(hh[:, v % 4, :], h32[v % 2], ACT.Copy).then_inc(s["hh_done"], 1)
                    for i in context_at(l, u):
                        context(l + 1, i)
                    if l in (0, 3) and u == TURN_AT[l]:
                        turned(2 * l + 1, 1)
                    if l in (0, 3) and u == ROUTER_FIRST:
                        exponent(l)
                    if l in (1, 2) and u == COMB_TURN_AT:
                        spread(l, 1)
                    if l < 3 and u == NEXT_AT[l] + 2:
                        turned(2 * l + 2, 0)
                    if l < 3 and u == NEXT_AT[l] + 4:
                        queries(l + 1, 0)

            split_weights(0, 5, "aw0_in")
            act.wait_ge(s["ctx_in"], 16)
            ctx32 = raw[:, AW_COLS:AW_COLS + B * S].rearrange("p (b k) -> p b k", b=B)
            for e in range(2):
                act.activation(CT[:, 0, :, e, :], ctx32, ACT.Copy).then_inc(s["ctx_hi"], 1)
            act.wait_ge(s["first_in"], 48)
            act.activation(TG[:, :], TG[:, :], ACT.Tanh).then_inc(s["tanh_made"], 1)
            turned(0, 0)
            context(0, 0)
            context(0, 1)
            turned(0, 1)
            queries(0, 0)
            queries(0, 1)
            for i in range(2, len(CONTEXT)):
                context(0, i)
            split_weights(5, 14, "aw_in")
            act.wait_ge(s["rw_in"], 16)
            act.activation(RW[:, 0, :], rw32[:, :], ACT.Copy).then_inc(s["rw_hi"], 1)
            for l in range(LAYERS):
                load_table(ACT.Exp)
                attention(l)
                ffn(l)

        @block.tensor
        def _(pe):
            def three(out, lhsT, rhs, start=True, stop=True):
                pe.matmul(out, lhsT(0), rhs(0), start=start, stop=False, skip_group_check=True)
                pe.matmul(out, lhsT(1), rhs(0), start=False, stop=False, skip_group_check=True)
                return pe.matmul(out, lhsT(0), rhs(1), start=False, stop=stop, skip_group_check=True)

            def project(out, w, src, t):
                return three(out, lambda h: aw(w, h), lambda h: src(h)[:, HALF * t:HALF * t + HALF] if src else
                             CT[:, h, 8 * t:8 * t + 8, 0, :])

            def keys(l, t):
                mm = project(context_bank(l, t)[:, :].rearrange("p (b k) -> p b k", b=8), mat(l, 1), None, t)
                if l == 0:
                    mm = project(bank[6 + t][:, :].rearrange("p (b k) -> p b k", b=8), mat(0, 4), None, t)
                mm.then_inc(s["k_proj"], 1)

            def values(l, j):
                for b in range(4):
                    mm = three(context_bank(l, 2 + j)[:, P * b:P * b + P],
                               lambda h: CT[:, h, 4 * j + b, :, :].rearrange("p e k -> p (e k)"),
                               lambda h: aw(mat(l, 2), h), start=(b == 0))
                mm.then_inc(s["v_proj"], 1)

            def context(l, i):
                kind, part = CONTEXT[i]
                if l == 0 and i == 0:
                    pe.wait_ge(s["aw_lo"], 1)
                    pe.wait_ge(s["ctx_lo"], 1)
                if l == 0 and i == 2:
                    pe.wait_ge(s["ctx_lo"], 2)
                if l == 0 and i >= 4:
                    pe.wait_ge(s["xl_ready"], i - 3)
                if l and i == 0:
                    pe.wait_ge(s["aw_lo"], 2)
                    pe.wait_ge(s["x_attn"], TILES * l)
                if i == (0 if l == 1 else 2) and l:
                    pe.wait_ge(s["exp_in"], once(l - 1, 1))
                    if l > 1:
                        pe.wait_ge(s["combT_ready"], 2 * (l - 2) + 1)
                if context_frees(l, i):
                    last, at = context_frees(l, i)
                    pe.wait_ge(s[f"{last}_lo"], (2 if last == "k" else 4) * l + at + 1)
                (keys if kind == "k" else values)(l, part)

            def turn_normed(n, t):
                if n == 0 and t == 0:
                    pe.wait_ge(s["ident_made"], 1)
                if n and n % 2 == 0 and t == 0:
                    pe.wait_ge(s["v_lo"], 2 * n + 4)
                pe.wait_ge(s["xn_ready"], 2 * n + t + 1)
                for q in range(4):
                    mm = pe.transpose(turn_bank(n, t)[:, P * q:P * q + P], XN[:, q, :], ident[:, :])
                mm.then_inc(s["xn_turned"], 1)

            def xn_split(n, t):
                pe.wait_ge(s["xh_ready"], 2 * n + t + 1)
                pe.wait_ge(s["xl_ready"], 2 * n + t + 1)

            def queries(l, t):
                xn_split(2 * l, t)
                if l == 0:
                    pe.wait_ge(s["k_rot"], t + 1)
                mm = project(query_bank(l, t)[:, :], mat(l, 0), lambda h: xT[:, h, :], t)
                if l == 0:
                    mm = project(bank[6 + t][:, :], mat(0, 3), lambda h: xT[:, h, :], t)
                mm.then_inc(s["q_proj"], 1)

            def take_scores(l, p):
                i = TILES * l + p
                if p == 0:
                    pe.wait_ge(s["km_in"], 256 * (l + 1))
                if l == 0 and p == 1:
                    pe.wait_ge(s["v_lo"], 2)
                if p % 4 == 0:
                    pe.wait_ge(s["q_hi"], 2 * l + p // 4 + 1)
                    pe.wait_ge(s["q_lo"], 2 * l + p // 4 + 1)
                if p >= 2:
                    pe.wait_ge(s["shifted"], i - 1)
                for ha, hb in ((0, 0), (1, 0), (0, 1)):
                    for r in range(2):
                        for b in range(2):
                            tok = slice(P * p + S * b, P * p + S * b + S)
                            mm = pe.matmul(bank[2 * (p % 2) + r][S * b:S * b + S, :].rearrange("p (j k) -> p j k", j=HD),
                                           QZ[:, r, ha, tok], KM[:, hb, :, tok],
                                           start=(ha == 0 and hb == 0), stop=(hb == 1))
                mm.then_inc(s["scores"], 1)

            def turn_probs(l, p):
                i = TILES * l + p
                pe.wait_ge(s["probs"], i + 1)
                for g in range(2):
                    if i >= 1:
                        pe.wait_ge(s["pt_lo"], 2 * i - 1 + g)
                    else:
                        pe.wait_ge(s["v_lo"], 3 + g)
                    for q in range(4):
                        at = (4 * g + q) * P
                        mm = pe.transpose(bank[4 + g][:, P * q:P * q + P], prob[p % 2][:, at:at + P], ident[:, :])
                    mm.then_inc(s["pt_turned"], 1)

            def weigh_values(l, p):
                i = TILES * l + p
                if p == 0:
                    pe.wait_ge(s["v_lo"], 4 * (l + 1))
                if i == 0:
                    pe.wait_ge(s["consts_made"], 1)
                if i >= 1 and p != LAST:
                    pe.wait_ge(s["o_norm"], i)
                if p == LAST:
                    pe.wait_ge(s["pt_lo"], 2 * i + 2)
                for g in range(2):
                    pe.wait_ge(s["pt_hi"], 2 * i + g + 1)
                    pe.wait_ge(s["pt_lo"], 2 * i + g + 1)
                    for q in range(4 * g, 4 * g + 4):
                        for ha, v in ((0, VH), (1, VH), (0, VL)):
                            for b in range(2):
                                mm = pe.matmul(out_bank(p)[S * b:S * b + S, 18 * q:18 * q + 18],
                                               PT[i % 2][ha][:, P * q + S * b:P * q + S * b + S],
                                               v[:, 2 * p + b, q, :, :].rearrange("p e d -> p (e d)"),
                                               start=(q == 0 and ha == 0 and v is VH), stop=(v is VL),
                                               skip_group_check=True)
                mm.then_inc(s["pv"], 1)

            def turn_out(l, p):
                i = TILES * l + p
                pe.wait_ge(s["o_norm"], i + 1)
                if i >= 1 and p != LAST:
                    pe.wait_ge(s["x_attn"], i)
                if p == 0:
                    pe.wait_ge(s["q_lo"], 2 * l + 2)
                pe.transpose(turned_out_bank(p)[:, 0:P], ON[p % 2][:, :], ident[:, :]).then_inc(s["o_turned"], 1)

            def project_out(l, p):
                i = TILES * l + p
                if i == 0:
                    pe.wait_ge(s["consts_in"], 16 * 8)
                pe.wait_ge(s["ot_ready"], i + 1)
                pe.matmul(turned_out_bank(p)[:, P:2 * P], OT[:, p % 2, :], WO[:, l, :], start=True, stop=True,
                          skip_group_check=True).then_inc(s["y_done"], 1)

            def attention(l):
                take_scores(l, 0)
                for k in range(TILES + 2):
                    if 1 <= k <= TILES:
                        turn_probs(l, k - 1)
                    for p in finishing(k):
                        turn_out(l, p)
                    if l and k == 1:
                        turn_normed(2 * l, 1)
                    if l and k == 2:
                        queries(l, 1)
                    if k + 1 < TILES:
                        take_scores(l, k + 1)
                    if 2 <= k <= TILES:
                        weigh_values(l, k - 2)
                    for p in finishing(k):
                        project_out(l, p)
                    if k == TILES:
                        weigh_values(l, LAST)
                        pe.wait_ge(s["shifted"], TILES * (l + 1))
                        turn_normed(2 * l + 1, 0)
                if l in (1, 2):
                    logits(l, 0)
                slice_in(l, 0)

            def slice_in(l, u):
                at = UNIT_AT[l]
                c, t = unit(l, u)[0:2]
                xn_split(2 * l + 1, t)
                pe.wait_ge(s["split_lo"], grain_of(l, c))
                rhs = lambda h: xT[:, h, HALF * t:HALF * t + HALF]
                if l == 3:
                    if u >= 4:
                        pe.wait_ge(s["hl_done"], at + u - 3)
                    three(bank[u % 4][:, :], lambda h: weight(l, c, 0, h), rhs).then_inc(s["gate_done"], 1)
                    return
                if u >= 2:
                    pe.wait_ge(s["silu_done"], at + u - 1)
                three(bank[u % 2][:, :], lambda h: weight(l, c, 0, h), rhs).then_inc(s["gate_done"], 1)
                if u >= 2:
                    pe.wait_ge(s["h32_done"], at + u - 1)
                three(bank[2 + u % 2][:, :], lambda h: weight(l, c, 1, h), rhs).then_inc(s["up_done"], 1)

            def logits(l, t=0):
                experts = EXPERTS[l]
                halves = l in (1, 2)
                xn_split(2 * l + 1, t if halves else 1)
                if l == 0:
                    pe.wait_ge(s["rw_lo"], 1)
                for q in range(TILES // 2 if halves else TILES):
                    tile = (4 * t + q) * P
                    mm = three(bank[1 if halves and t == 0 else 7][:, experts * q:experts * q + experts],
                               lambda h: xT[:, h, tile:tile + P],
                               lambda h: RW[:, h, ROUTER_AT[l]:ROUTER_AT[l] + experts], start=(q == 0))
                mm.then_inc(s["logits"], 1)

            def ffn(l):
                at = UNIT_AT[l]
                def second_half():
                    pe.wait_ge(s["x_attn"], TILES * (l + 1))
                    turn_normed(2 * l + 1, 1)

                def slice_out(u):
                    c, t, e, k = unit(l, u)
                    acc = acc_bank(l, u)
                    nth = u // 4 if l in (0, 3) else 0
                    if k == 0 and e == 0:
                        pe.wait_ge(s["x_attn"], TILES * (l + 1))
                        if l in (1, 2):
                            pe.wait_ge(s["v_lo"], 4 * (l + 2))
                    if k == 0 and nth and nth >= ACCS[l]:
                        pe.wait_ge(s["sum_read"], SUM_AT[l] + nth - ACCS[l] + 1)
                    if k == 0 and e == 1 and t == 1 and l == 3:
                        pe.wait_ge(s["comb_ready"], once(3))
                    pe.wait_ge(s["hl_done"], at + u + 1)
                    last = k == PER_EXPERT[l] - 1
                    for q in range(4):
                        mm = three(acc[:, P * q:P * q + P], lambda h: (hh, hl)[h][:, u % 4, P * q:P * q + P],
                                   lambda h: weight(l, c, MATS[l] - 1, h), start=(k == 0 and q == 0), stop=last)
                    mm.then_inc(s["down_done"], 1)
                    if last:
                        if l in (1, 2):
                            pe.wait_ge(s["combT_ready"], 2 * (l - 1) + t + 1)
                            for q in range(4):
                                tile = (4 * t + q) * P
                                mm = pe.matmul(acc[:, P * q:P * q + P], combT[:, tile:tile + P], B2[:, l - 1, :],
                                               start=False, stop=True, skip_group_check=True)
                            mm.then_inc(s["sum_done"], 1)

                def turn_comb(t):
                    pe.wait_ge(s["comb_ready"], once(l, t))
                    if t == 0:
                        pe.wait_ge(s["o_norm"], TILES * (l + 1))
                    else:
                        pe.wait_ge(s["combT_ready"], 2 * (l - 1) + 1)
                        if l < 3:
                            pe.wait_ge(s["v_lo"], 4 * (l + 2))
                    for q in range(4):
                        at_ = COMB * (4 * t + q)
                        mm = pe.transpose(bank[6][0:COMB, P * q:P * q + P], comb[:, at_:at_ + COMB], ident[:, :])
                    mm.then_inc(s["comb_turned"], 1)

                def count():
                    pe.wait_ge(s["counts_in"], 1)
                    pe.wait_ge(s["consts_made"], 1)
                    pe.matmul(bank[7][:, 0:64], before[:, :], mask16[:, :], start=True, stop=False,
                              skip_group_check=True)
                    for q in range(TILES - 1):
                        mm = pe.matmul(bank[7][:, 8 * q + 8:64].rearrange("p (t e) -> p t e", e=8), ones16[:, :],
                                       bc_mid(mask16[:, 8 * q:8 * q + 8], TILES - 1 - q),
                                       start=False, stop=(q == TILES - 2), skip_group_check=True)
                    mm.then_inc(s["counts"], 1)

                for u in range(UNITS[l] + 2):
                    if l in (1, 2) and u == 1:
                        context(l + 1, 0)
                        second_half()
                        context(l + 1, 1)
                        logits(l, 1)
                        pe.wait_ge(s["exp_in"], once(l, 0))
                    if 1 <= u < UNITS[l]:
                        slice_in(l, u)
                    if l in (1, 2) and u == 1:
                        turn_comb(0)
                    if l in (1, 2) and u == COMB_TURN_AT:
                        turn_comb(1)
                    if l in (0, 3) and u == TURN_AT[l]:
                        second_half()
                    if l in (0, 3) and u == 4:
                        logits(l)
                    if l == 3 and u == COUNT_AT:
                        count()
                    if u >= 2:
                        slice_out(u - 2)
                    for i in context_at(l, u):
                        context(l + 1, i)
                    if l < 3 and u == NEXT_AT[l] + 2:
                        turn_normed(2 * l + 2, 0)
                    if l < 3 and u == NEXT_AT[l] + 4:
                        queries(l + 1, 0)

            for t in range(2):
                context(0, t)
                turn_normed(0, t)
            for t in range(2):
                queries(0, t)
            for i in range(2, len(CONTEXT)):
                context(0, i)
            for l in range(LAYERS):
                attention(l)
                ffn(l)

        @block.vector
        def _(dve):
            steps = [0]

            def step(ins):
                steps[0] += 1
                ins.then_inc(s["dve_step"], 1)

            def settle():
                dve.wait_ge(s["dve_step"], steps[0])

            def link(ins):
                step(ins)
                settle()

            tt, ts, stt = dve.tensor_tensor, dve.tensor_scalar, dve.scalar_tensor_tensor

            def split_weights(lo, hi, n):
                dve.wait_ge(s["aw_hi"], n)
                tt(AW[:, 1, lo:hi, :].rearrange("p i n -> p (i n)"), raw[:, P * lo:P * hi],
                   AW[:, 0, lo:hi, :].rearrange("p i n -> p (i n)"), ALU.subtract).then_inc(s["aw_lo"], 1)

            def split_context():
                dve.wait_ge(s["ctx_hi"], 2)
                ctx32 = raw[:, AW_COLS:AW_COLS + B * S].rearrange("p (b k) -> p b k", b=B)
                for e in range(2):
                    tt(CT[:, 1, :, e, :], ctx32, CT[:, 0, :, e, :], ALU.subtract).then_inc(s["ctx_lo"], 1)

            def prepare():
                dve.wait_ge(s["rw_hi"], 1)
                tt(RW[:, 1, :], rw32[:, :], RW[:, 0, :], ALU.subtract).then_inc(s["rw_lo"], 1)
                dve.wait_ge(s["consts_in"], 16 * 8)
                step(dve.tensor_copy(QM[:, :], qm8[:, :]))
                link(ts(base[:, :, :], pad8[:, :, :], NEG, None, ALU.mult))
                stt(base[:, :, :], bc_mid(SXS[:, :], TILES), 0.5, base[:, :, :], ALU.mult, ALU.add
                    ).then_inc(s["copied"], 1)

            def rotate(l, sem_in, count, even, swap, b0, b1, done, t):
                dve.wait_ge(s[sem_in], count)
                ra = work[:, HALF * t:HALF * t + HALF].rearrange("p (b k) -> p b k", b=8)
                rb = work[:, 1024 + HALF * t:1024 + HALF * t + HALF].rearrange("p (b k) -> p b k", b=8)
                step(stt(ra, even[:, :].rearrange("p (b k) -> p b k", b=8), cols[:, b0:b0 + 1],
                         bc_mid(rope[:, 0, :], 8), ALU.add, ALU.mult))
                link(stt(rb, swap[:, :].rearrange("p (b k) -> p b k", b=8), cols[:, b1:b1 + 1],
                         bc_mid(rope[:, 1, :], 8), ALU.add, ALU.mult))
                tt(ra, ra, rb, ALU.add).then_inc(s[done], 1)

            def keys(l, t):
                dve.wait_ge(s["k_hi"], 2 * l + t + 1)
                half = slice(HALF * t, HALF * t + HALF)
                if l == 0:
                    tt(KT[:, 1, half], work[:, half], KT[:, 0, half], ALU.subtract).then_inc(s["k_lo"], 1)
                else:
                    stt(KT[:, 1, half], context_bank(l, t)[:, :], cols[:, 3 * l + 1:3 * l + 2], KT[:, 0, half],
                        ALU.add, ALU.subtract).then_inc(s["k_lo"], 1)

            def values(l, j):
                dve.wait_ge(s["v_hi"], 4 * l + j + 1)
                for e in range(2):
                    rows = slice(S * e, S * e + S)
                    src = context_bank(l, 2 + j)[rows, :].rearrange("p (b h e d) -> p (b h) e d", b=4, h=HP, e=2)
                    hi, lo = (v[rows, 4 * j:4 * j + 4, :, e, 0:HD].rearrange("p b h d -> p (b h) d")
                              for v in (VH, VL))
                    ins = tt(lo, src[:, :, e, :], hi, ALU.subtract)
                ins.then_inc(s["v_lo"], 1)

            def context(l, i):
                kind, part = CONTEXT[i]
                (keys if kind == "k" else values)(l, part)

            def variance(n, t, with_stats):
                if with_stats:
                    if n:
                        dve.wait_ge(s["sum_read"], SUM_AT[n // 2] + (0 if t else -2 if n == 2 else -1))
                    for q in range(4 * t, 4 * t + 4):
                        step(dve.bn_stats(bn[:, q, :], X[:, q, :]))
                    settle()
                    for q in range(4 * t, 4 * t + 4):
                        step(dve.bn_aggr(mv[:, q, :], bn[:, q, :]))
                settle()
                if n:
                    dve.wait_ge(s["rstd_ready"], 2 * (n - 1) + t + 1)
                ts(veps[:, 4 * t:4 * t + 4], mv[:, 4 * t:4 * t + 4, 1], EPS, None, ALU.add
                   ).then_inc(s["var_ready"], 1)

            def normalise_tokens(n, t):
                dve.wait_ge(s["rstd_ready"], 2 * n + t + 1)
                if n or t:
                    dve.wait_ge(s["xn_turned"], 2 * n + t)
                for q in range(4):
                    tile = 4 * t + q
                    ins = ts(XN[:, q, :], X[:, tile, :], mv[:, tile, 0:1], rstd[:, tile:tile + 1],
                             ALU.subtract, ALU.mult)
                ins.then_inc(s["xn_ready"], 1)

            def turned(n, t):
                dve.wait_ge(s["xh_ready"], 2 * n + t + 1)
                half = slice(HALF * t, HALF * t + HALF)
                tt(xT[:, 1, half], turn_bank(n, t)[:, :], xT[:, 0, half], ALU.subtract).then_inc(s["xl_ready"], 1)

            def queries(l, t):
                dve.wait_ge(s["q_hi"], 2 * l + t + 1)
                for r in range(2):
                    rows = slice(S * r, S * r + S)
                    half = slice(HALF * t, HALF * t + HALF)
                    if l == 0:
                        ins = tt(QZ[rows, r, 1, half], work[rows, half], QZ[rows, r, 0, half], ALU.subtract)
                    else:
                        ins = stt(QZ[rows, r, 1, half], query_bank(l, t)[rows, :], cols[rows, 3 * l:3 * l + 1],
                                  QZ[rows, r, 0, half], ALU.add, ALU.subtract)
                ins.then_inc(s["q_lo"], 1)

            def attention(l):
                def outputs(p):
                    return out_bank(p)[:, 0:HEADS * (HD + 1)].rearrange("p (h d) -> p h d", h=HEADS)

                def shift(p, before_last):
                    i = TILES * l + p
                    dve.wait_ge(s["scores"], i + 1)
                    if i >= 2:
                        dve.wait_ge(s["pt_turned"], 2 * i - 2)
                    three_d = prob[p % 2].rearrange("p (h k) -> p h k", h=HEADS)
                    pairs = [(bank[2 * (p % 2) + r][:, :].rearrange("p (h k) -> p h k", h=HD),
                              three_d[:, HD * r:HD * r + HD, :], slice(HD * r, HD * r + HD)) for r in range(2)]
                    if l == 1:
                        dve.wait_ge(s["bias_ready"], p + 1)
                    seen = []
                    for ps, dst, heads in pairs:
                        if l == 3:
                            ins = ts(dst, ps, 50.0 / SCALE, -50.0 / SCALE, ALU.min, ALU.max)
                        elif l == 1:
                            step(stt(dst, ps, SCALE / 2, BIAS[:, p % 2, heads, :], ALU.mult, ALU.add))
                        else:
                            step(dve.tensor_reduce(top[:, p % 2, heads], ps, AX_X, ALU.max))
                        seen.append(steps[0])
                    if l == 1:
                        dve.wait_ge(s["dve_step"], seen[1])
                        dve.tensor_reduce(top[:, p % 2, :], three_d, AX_X, ALU.max).then_inc(s["maxima"], 1)
                    if before_last:
                        before_last()
                    if l == 1:
                        dve.wait_ge(s["maxima"], p + 1)
                        ins = tt(three_d[:, 0:HD, :], three_d[:, 0:HD, :], bc_last(top[:, p % 2, 0:HD], S),
                                 ALU.subtract)
                    elif l != 3:
                        for (ps, dst, heads), n in zip(pairs, seen):
                            dve.wait_ge(s["dve_step"], n)
                            ins = tt(dst, ps, bc_last(top[:, p % 2, heads], S), ALU.subtract)
                    ins.then_inc(s["shifted"], 1)

                def invert_sums(p):
                    dve.wait_ge(s["pv"], TILES * l + p + 1)
                    step(dve.reciprocal(rden[:, p % 2, :], outputs(p)[:, :, HD]))

                def normalise(p):
                    i = TILES * l + p
                    settle()
                    if l == 3:
                        link(ts(rden[:, p % 2, :], rden[:, p % 2, :], QM[:, p:p + 1], None, ALU.mult))
                    if i >= 2:
                        dve.wait_ge(s["o_turned"], i - 1)
                    tt(ON[p % 2][:, :].rearrange("p (h d) -> p h d", h=HEADS), outputs(p)[:, :, 0:HD],
                       bc_last(rden[:, p % 2, :], HD), ALU.mult).then_inc(s["o_norm"], 1)

                def add_out(p):
                    i = TILES * l + p
                    dve.wait_ge(s["y_done"], i + 1)
                    stt(X[:, p, :], turned_out_bank(p)[:, P:2 * P], TG[:, l:l + 1], X[:, p, :], ALU.mult, ALU.add
                        ).then_inc(s["x_attn"], 1)

                def first_stats(p):
                    dve.wait_ge(s["x_attn"], TILES * l + p + 1)
                    step(dve.bn_stats(bn[:, p, :], X[:, p, :]))

                def last_stats(p):
                    settle()
                    step(dve.bn_aggr(mv[:, p, :], bn[:, p, :]))

                for k in range(TILES + 3):
                    for p in finishing(k)[0:1]:
                        invert_sums(p)
                    for p in adding(k):
                        add_out(p)
                    for p in finishing(k)[0:1]:
                        normalise(p)
                    for p in finishing(k)[1:]:
                        invert_sums(p)
                        normalise(p)
                    if k < TILES:
                        shift(k, (lambda: first_stats(k - 4)) if k >= 4 else None)
                    else:
                        for p in adding(k):
                            first_stats(p)
                    if k == TILES:
                        normalise_tokens(2 * l + 1, 0)
                    if k == TILES + 1:
                        turned(2 * l + 1, 0)
                    if l and k == 0:
                        normalise_tokens(2 * l, 1)
                    for p in adding(k):
                        last_stats(p)
                    if 1 <= k <= TILES:
                        i = TILES * l + k - 1
                        for g in range(2):
                            dve.wait_ge(s["pt_hi"], 2 * i + g + 1)
                            half = slice(HALF * g, HALF * g + HALF)
                            tt(PT[i % 2][1][:, half], bank[4 + g][:, :], PT[i % 2][0][:, half], ALU.subtract
                               ).then_inc(s["pt_lo"], 1)
                    if l and k == 1:
                        turned(2 * l, 1)
                    if l and k == 2:
                        queries(l, 1)
                    if k == 3 and l < 3:
                        if l == 0:
                            dve.wait_ge(s["tanh_made"], 1)
                        link(stt(X[:, :, :], bc_mid(BO[:, l, :], TILES), TG[:, l:l + 1], X[:, :, :],
                                 ALU.mult, ALU.add))
                    if k == TILES - 1:
                        variance(2 * l + 1, 0, False)
                variance(2 * l + 1, 1, False)
                if l in (1, 2):
                    router(l, 0)

            def router(l, part, t=0):
                halves = l in (1, 2)
                G = TILES // 2 if halves else TILES
                e = EXPERTS[l]
                n = G * e
                v3 = lambda ap, g=G: ap.rearrange("p (t e) -> p t e", t=g)
                T = [r[:, 0:n] for r in rt]

                def first_max(src, sel, small, small2, tmp, groups, width, opens, closes):
                    sm, sm2 = small[:, 0:groups], small2[:, 0:groups]
                    if opens:
                        link(dve.tensor_reduce(sm, v3(src, groups), AX_X, ALU.max))
                        link(tt(v3(sel, groups), v3(src, groups), bc_last(sm, width), ALU.is_equal))
                        link(tt(v3(tmp, groups), v3(sel, groups), bc_mid(REV[:, HEADS - width:HEADS], groups),
                                ALU.mult))
                    if closes:
                        link(dve.tensor_reduce(sm2, v3(tmp, groups), AX_X, ALU.max))
                        link(tt(v3(sel, groups), v3(tmp, groups), bc_last(sm2, width), ALU.is_equal))

                def largest(src, groups, width, opens=True, closes=True):
                    w = groups * width
                    first_max(src, T[3][:, 0:w], rs[0], rs[1], T[4][:, 0:w], groups, width, opens, closes)
                    if closes:
                        link(stt(T[5][:, 0:w], T[3][:, 0:w], NEG, src, ALU.mult, ALU.add))

                def second(groups, width, opens=True, closes=True):
                    w = groups * width
                    first_max(T[5][:, 0:w], T[6][:, 0:w], rs[2], rs[1], T[4][:, 0:w], groups, width, opens, closes)
                    if closes:
                        link(tt(T[3][:, 0:w], T[3][:, 0:w], T[6][:, 0:w], ALU.add))

                tg = TG[:, 4 + l:5 + l]
                ranked = (T[0], T[2], T[1], T[0])[l]
                c3 = comb[:, COMB * G * t:COMB * G * (t + 1)].rearrange("p (t e) -> p t e", t=G)

                logits = bank[1 if l in (1, 2) and t == 0 else 7][:, 0:n]
                if part == 0:
                    dve.wait_ge(s["logits"], once(l, t))
                    if t:
                        dve.wait_ge(s["comb_ready"], once(l, 0))
                    dve.wait_ge(s["consts_made"], 1)
                    if l == 3:
                        link(tt(v3(T[0]), v3(logits), bc_mid(RB[:, 32:40], G), ALU.add))
                    else:
                        link(dve.tensor_copy(T[0], logits))
                    if l == 1:
                        dve.tensor_copy(T[1], T[0]).then_inc(s["exp_in"], 1)
                        link(tt(v3(T[2]), v3(T[0]), bc_mid(RB[:, 0:16], G), ALU.add))
                    else:
                        link(dve.tensor_reduce(rs[5][:, 0:G], v3(T[0]), AX_X, ALU.max))
                        tt(v3(T[1]), v3(T[0]), bc_last(rs[5][:, 0:G], e), ALU.subtract).then_inc(s["exp_in"], 1)
                if part == 1 and l != 1:
                    dve.wait_ge(s["exp_out"], once(l, t))
                    link(dve.tensor_reduce(rs[3][:, 0:G], v3(T[1]), AX_X, ALU.add))
                    link(dve.reciprocal(rs[4][:, 0:G], rs[3][:, 0:G]))
                    link(tt(v3(T[0]), v3(T[1]), bc_last(rs[4][:, 0:G], e), ALU.mult))
                if part == 2 and l == 2:
                    link(tt(v3(T[1]), v3(T[0]), bc_mid(RB[:, 16:32], G), ALU.add))
                    g4 = v3(T[1], 4 * G)
                    more, less = (T[i][:, 0:8 * G].rearrange("p (g e) -> p g e", e=2) for i in (3, 4))
                    step(tt(more, g4[:, :, 0:2], g4[:, :, 2:4], ALU.max))
                    link(tt(less, g4[:, :, 0:2], g4[:, :, 2:4], ALU.min))
                    step(tt(rs[0][:, 0:4 * G], more[:, :, 0], more[:, :, 1], ALU.max))
                    step(tt(rs[1][:, 0:4 * G], more[:, :, 0], more[:, :, 1], ALU.min))
                    link(tt(rs[2][:, 0:4 * G], less[:, :, 0], less[:, :, 1], ALU.max))
                    link(tt(rs[1][:, 0:4 * G], rs[1][:, 0:4 * G], rs[2][:, 0:4 * G], ALU.max))
                    link(tt(rs[6][:, 0:4 * G], rs[0][:, 0:4 * G], rs[1][:, 0:4 * G], ALU.add))
                    largest(rs[6][:, 0:4 * G], G, 4)
                    second(G, 4)
                    link(ts(rs[7][:, 0:4 * G], T[3][:, 0:4 * G], -NEG, NEG, ALU.mult, ALU.add))
                    link(tt(v3(T[1], 4 * G), v3(T[1], 4 * G), bc_last(rs[7][:, 0:4 * G], 4), ALU.add))
                if part in (3, 3.1):
                    largest(ranked, G, e, part == 3, part == 3.1 or halves)
                if part in (4, 4.1):
                    second(G, e, part == 4, part == 4.1 or halves)
                if part == 5 and l == 0:
                    link(stt(rs[3][:, 0:G], rs[0][:, 0:G], 1e-9, rs[2][:, 0:G], ALU.add, ALU.add))
                    link(dve.reciprocal(rs[4][:, 0:G], rs[3][:, 0:G]))
                    link(tt(T[0], T[0], T[3], ALU.mult))
                    link(tt(v3(T[0]), v3(T[0]), bc_last(rs[4][:, 0:G], e), ALU.mult))
                    ts(comb[:, 0:n], T[0], tg, None, ALU.mult).then_inc(s["comb_ready"], 1)
                if part == 5 and l == 1:
                    dve.wait_ge(s["exp_out"], once(l, t))
                    link(ts(T[1], T[1], 1.0, None, ALU.add))
                    link(dve.reciprocal(T[0], T[1]))
                    link(tt(T[0], T[0], T[3], ALU.mult))
                    link(dve.tensor_reduce(rs[3][:, 0:G], v3(T[0]), AX_X, ALU.add))
                    link(ts(rs[3][:, 0:G], rs[3][:, 0:G], 1e-10, None, ALU.add))
                    link(dve.reciprocal(rs[4][:, 0:G], rs[3][:, 0:G]))
                    step(dve.tensor_copy(c3[:, :, 0], ones8[:, 0:G]))
                    tt(c3[:, :, 1:COMB], v3(T[0]), bc_last(rs[4][:, 0:G], e), ALU.mult).then_inc(s["comb_ready"], 1)
                if part == 5 and l == 2:
                    step(dve.tensor_copy(c3[:, :, 0], ones8[:, 0:G]))
                    tt(c3[:, :, 1:COMB], v3(T[0]), v3(T[3]), ALU.mult).then_inc(s["comb_ready"], 1)
                if part == 5 and l == 3:
                    link(tt(T[0], T[0], T[3], ALU.mult))
                    ts(mask16[:, :], T[0], 0.0, None, ALU.is_gt).then_inc(s["counts_in"], 1)
                if part == 7 and l == 3:
                    dve.wait_ge(s["counts"], 1)
                    link(ts(T[1], bank[7][:, 0:n], float(CAPACITY), None, ALU.is_lt))
                    link(tt(T[0], T[0], T[1], ALU.mult))
                    ts(comb[:, 0:n], T[0], tg, None, ALU.mult).then_inc(s["comb_ready"], 1)

            def ffn(l):
                at = UNIT_AT[l]
                tg = TG[:, 4 + l:5 + l]

                def product(u):
                    c, t = unit(l, u)[0:2]
                    dve.wait_ge(s["silu_done"], at + u + 1)
                    dve.wait_ge(s["up_done"], at + u + 1)
                    if u >= 2:
                        dve.wait_ge(s["hh_done"], at + u - 1)
                        dve.wait_ge(s["hl_done"], at + u - 1)
                    if l == 0:
                        tt(h32[u % 2], bank[2 + u % 2][:, :], gated[u % 2], ALU.mult).then_inc(s["h32_done"], 1)
                        return
                    b3 = cols[:, 21 + 18 * (l - 1) + c:22 + 18 * (l - 1) + c]
                    ins = stt(h32[u % 2], bank[2 + u % 2][:, :], b3, gated[u % 2], ALU.add, ALU.mult)
                    if c:
                        link(ins)
                        j = c - 1
                        group = next(g for g, (lo, hi) in enumerate(SPREAD) if lo <= j < hi)
                        dve.wait_ge(s[f"comb_in{group}"], 32 * (2 * (l - 1) + t + 1))
                        ins = tt(h32[u % 2], h32[u % 2], CB[:, j, :], ALU.mult)
                    ins.then_inc(s["h32_done"], 1)

                def rest(u):
                    dve.wait_ge(s["hh_done"], at + u + 1)
                    if u >= 4:
                        dve.wait_ge(s["down_done"], at + u - 3)
                    if l == 3:
                        stt(hl[:, u % 4, :], bank[u % 4][:, :], 0.0, hh[:, u % 4, :], ALU.max, ALU.subtract
                            ).then_inc(s["hl_done"], 1)
                    else:
                        tt(hl[:, u % 4, :], h32[u % 2], hh[:, u % 4, :], ALU.subtract).then_inc(s["hl_done"], 1)

                def sums(u):
                    c, t, e, place = unit(l, u)
                    if place < PER_EXPERT[l] - 1:
                        return
                    if l in (1, 2):
                        dve.wait_ge(s["sum_done"], 2 * (l - 1) + t + 1)
                    dve.wait_ge(s["down_done"], at + u + 1)
                    acc = acc_bank(l, u)[:, :].rearrange("p (t d) -> p t d", t=4)
                    four = X[:, 4 * t:4 * t + 4, :]
                    if l in (1, 2) or (l == 0 and e == 0):
                        settle()
                        step_ = stt(four, acc, tg, four, ALU.mult, ALU.add)
                    else:
                        col = e - 1 if l == 0 else e
                        dve.wait_ge(s["comb_ready"], once(l))
                        dve.wait_ge(s["sum_read"], SUM_AT[l] + u // 4)
                        for q in range(4):
                            cc = EXPERTS[l] * (4 * t + q) + col
                            step_ = stt(X[:, 4 * t + q, :], acc[:, q, :], comb[:, cc:cc + 1],
                                        X[:, 4 * t + q, :], ALU.mult, ALU.add)
                    step_.then_inc(s["sum_read"], 1)

                for u in range(UNITS[l] + 3):
                    if u == 0 and l in (1, 2):
                        normalise_tokens(2 * l + 1, 1)
                        router(l, 1)
                        router(l, 2)
                        router(l, 3)
                        turned(2 * l + 1, 1)
                        router(l, 4)
                        router(l, 5)
                        router(l, 0, 1)
                        context(l + 1, 0)
                        context(l + 1, 1)
                    if u == 4 and l == 3:
                        turned(2 * l + 1, 1)
                    if u < UNITS[l] and l != 3:
                        product(u)
                    if u == 0 and l in (0, 3):
                        normalise_tokens(2 * l + 1, 1)
                    if 1 <= u <= UNITS[l] and l in (0, 3):
                        rest(u - 1)
                    if u == 3 and l == 0:
                        turned(2 * l + 1, 1)
                    if l in (0, 3) and 0 <= u - ROUTER_FIRST < len(ROUTER_PARTS):
                        router(l, ROUTER_PARTS[u - ROUTER_FIRST])
                    if l in (1, 2) and 2 <= u <= 6:
                        router(l, u - 1, 1)
                    for i in context_at(l, u - 1 if l == 0 else u):
                        context(l + 1, i)
                    if l < 3:
                        if u >= 3:
                            sums(u - 3)
                        if u == NEXT_AT[l]:
                            variance(2 * l + 2, 0, True)
                        if u == NEXT_AT[l] + 1:
                            normalise_tokens(2 * l + 2, 0)
                        if u == NEXT_AT[l] + 3:
                            turned(2 * l + 2, 0)
                        if u == NEXT_AT[l] + 5:
                            queries(l + 1, 0)
                    elif u == ROUTER_FIRST + 8:
                        for v in range(u - 2):
                            sums(v)
                    elif u > ROUTER_FIRST + 8:
                        sums(u - 3)

            dve.wait_ge(s["x_in"], 16)
            variance(0, 0, True)
            variance(0, 1, True)
            split_weights(0, 5, 1)
            split_context()
            normalise_tokens(0, 0)
            dve.wait_ge(s["first_in"], 48)
            rotate(0, "k_proj", 1, bank[0], bank[6], 1, 49, "k_rot", 0)
            normalise_tokens(0, 1)
            rotate(0, "k_proj", 2, bank[1], bank[7], 1, 49, "k_rot", 1)
            context(0, 0)
            context(0, 1)
            turned(0, 0)
            turned(0, 1)
            for t in range(2):
                rotate(0, "q_proj", t + 1, bank[t], bank[6 + t], 0, 48, "q_rot", t)
            for t in range(2):
                queries(0, t)
            for i in range(2, len(CONTEXT)):
                context(0, i)
            split_weights(5, 14, 2)
            prepare()
            for l in range(LAYERS):
                if l:
                    variance(2 * l, 1, True)
                attention(l)
                ffn(l)


def kernel(**inputs):
    import numpy as np
    import concourse.bacc as bacc
    from concourse.bass_utils import run_bass_kernel_spmd

    v = {k: np.asarray(x) for k, x in inputs.items()}
    zero = np.zeros(P, np.float32)
    swap = np.arange(P) ^ 1

    names = [("L0_xattn_Wq", "L0_xattn_Wk", "L0_xattn_Wv", "L0_xattn_Wo"),
             ("L1_xattn_Wq", "L1_xattn_Wk", "L1_xattn_Wv", "L1_xattn_Wo"),
             ("L2_xattn_W_q", "L2_xattn_W_k", "L2_xattn_W_v", "L2_xattn_W_o"),
             ("L3_xattn_W_q", "L3_xattn_W_k", "L3_xattn_W_v", "L3_xattn_W_o")]
    mats = [v[n].T for n in names[0][:3]] + [v["L0_xattn_Wq"][swap].T, v["L0_xattn_Wk"][swap].T]
    mats += [v[n].T for layer in names[1:] for n in layer[:3]]
    attn_w = np.stack(mats, 1).reshape(P, AW_COLS)

    columns = [v["L0_xattn_bq"], v["L0_xattn_bk"], v["L0_xattn_bv"],
               v["L1_xattn_bq"], v["L1_xattn_bk"], v["L1_xattn_bv"],
               v["L2_xattn_b_q"], v["L2_xattn_b_k"], v["L2_xattn_b_v"],
               zero, zero, zero]
    layer1 = [v["L1_ffn_sb1"]] + list(v["L1_ffn_b1"].reshape(8, P)) + [v["L1_ffn_sb3"]] + list(v["L1_ffn_b3"].reshape(8, P))
    layer2 = [v["L2_ffn_bs1"]] + list(v["L2_ffn_be1"].reshape(8, P)) + [v["L2_ffn_bs3"]] + list(v["L2_ffn_be3"].reshape(8, P))
    columns = columns + layer1 + layer2 + [v["L0_xattn_bq"][swap], v["L0_xattn_bk"][swap]]

    freq = 1.0 / 10000.0 ** (np.arange(0, HD, 2, dtype=np.float32) / HD)
    angle = np.repeat(freq, 2)[:, None].astype(np.float32) * np.arange(S, dtype=np.float32)[None, :]
    sign = np.where(np.arange(HD) % 2 == 0, -1.0, 1.0)[:, None]
    rope = np.stack([np.tile(np.cos(angle), (HEADS, 1)), np.tile(np.sin(angle) * sign, (HEADS, 1))], 1)

    def slices(*ms):
        return np.stack(ms, 2).reshape(P, -1)

    def wide(m):
        return m.reshape(P, -1, P)

    def tall(m):
        return m.reshape(-1, P, P).transpose(1, 0, 2)

    def hidden(first, rest, flip):
        parts = ([first] if first is not None else []) + list(rest)
        return [p.T for p in parts] if flip else parts

    f = v
    ffn0 = slices(
        wide(np.concatenate(hidden(f["L0_ffn_shared_gate"], f["L0_ffn_routed_gate"], True), 1)),
        wide(np.concatenate(hidden(f["L0_ffn_shared_up"], f["L0_ffn_routed_up"], True), 1)),
        tall(np.concatenate(hidden(f["L0_ffn_shared_down"], f["L0_ffn_routed_down"], True), 0)))
    ffn1 = slices(
        wide(np.concatenate(hidden(f["L1_ffn_sw1"], f["L1_ffn_w1"], True), 1)),
        wide(np.concatenate(hidden(f["L1_ffn_sw3"], f["L1_ffn_w3"], True), 1)),
        tall(np.concatenate(hidden(f["L1_ffn_sw2"], f["L1_ffn_w2"], True), 0)))
    ffn2 = slices(
        wide(np.concatenate(hidden(f["L2_ffn_ws1"], f["L2_ffn_We1"], False), 1)),
        wide(np.concatenate(hidden(f["L2_ffn_ws3"], f["L2_ffn_We3"], False), 1)),
        tall(np.concatenate(hidden(f["L2_ffn_ws2"], f["L2_ffn_We2"], False), 0)))
    ffn3 = slices(
        wide(np.concatenate(hidden(None, f["L3_ffn_experts_inter"], False), 1)),
        tall(np.concatenate(hidden(None, f["L3_ffn_experts_out"], False), 0)))

    b2 = np.stack([np.concatenate([v["L1_ffn_sb2"][None], v["L1_ffn_b2"]]),
                   np.concatenate([v["L2_ffn_bs2"][None], v["L2_ffn_be2"]])], 1)
    fside = v["fside_Bx16xSxS2_0"].transpose(0, 2, 1, 3).reshape(TILES, P, HEADS * S)
    arrays = {
        "x": v["x"].reshape(B * S, D), "ctxT": v["ctx_1024"].reshape(B * S, D).T, "attn_w": attn_w,
        "wo": np.stack([v[layer[3]].T for layer in names], 1),
        "ffn_w0": ffn0, "ffn_w1": ffn1, "ffn_w2": ffn2, "ffn_w3": ffn3,
        "router_w": np.concatenate([v["L0_ffn_router_w"].T, v["L1_ffn_gate_w"].T, v["L2_ffn_gate_w"].T,
                                    v["L3_ffn_W_router"].T], 1),
        "router_b": np.concatenate([v["L1_ffn_expert_bias"], v["L2_ffn_gate_b"], v["L3_ffn_b_router"]]),
        "cols": np.stack(columns, 1), "rope": rope.astype(np.float32),
        "bo": np.stack([v["L0_xattn_bo"], v["L1_xattn_bo"], v["L2_xattn_b_o"], zero]),
        "gates": np.concatenate([v["g_xattn"], v["g_ffn"]]),
        "sxs": np.concatenate([v["fside_SxS2_0"]] * 2),
        "pad": v["mask_BxS2_bf0"].reshape(TILES, 2, S).transpose(1, 0, 2),
        "qmask": v["mask_BxS_bf1"].reshape(TILES, P).T, "b2": b2, "fside": fside,
    }
    arrays = {k: np.ascontiguousarray(x) for k, x in arrays.items()}
    nc = bacc.Bacc("TRN2", target_bir_lowering=False, num_devices=1)
    aps = {k: nc.dram_tensor(f"in_{k}", x.shape, mybir.dt.from_np(x.dtype), kind="ExternalInput").ap()
           for k, x in arrays.items()}
    aps["out"] = nc.dram_tensor("out_x", (B * S, D), F32, kind="ExternalOutput").ap()
    build(nc, aps)
    r = run_bass_kernel_spmd(nc, [{f"in_{k}": x for k, x in arrays.items()}], core_ids=[0])
    return r.results[0]["out_x"].reshape(B, S, D)
```
